# Optimizing a Trainium2 kernel written in Bass

```python
import numpy as np
import jax
import jax.numpy as jnp

def _softmax(x, axis=-1):
    return jax.nn.softmax(x, axis=axis)

def _gelu(x):
    return jax.nn.gelu(x, approximate=True)

def _silu(x):
    return jax.nn.silu(x)

def _sigmoid(x):
    return jax.nn.sigmoid(x)

def _layernorm(x, axis=-1, eps=1e-05):
    m = jnp.mean(x, axis=axis, keepdims=True)
    v = jnp.var(x, axis=axis, keepdims=True)
    return (x - m) / jnp.sqrt(v + eps)

def _scatter_add(tgt, idx, src, axis=0):
    return tgt.at[idx].add(src)

def _segment_sum(src, seg, n):
    return jax.ops.segment_sum(src, seg, n)
kernel_name = 'mk_flamingo_gated_d4_seqx_r8_b0d937'

def setup_inputs(seed: int=0):
    np.random.seed(seed)
    _w = jnp.asarray

    def _rec_inputs():
        import jax
        import jax.numpy as jnp
        _rk = jax.random.key(seed)
        x = 4.136e-05 + 0.9999 * jax.random.normal(jax.random.fold_in(_rk, 1), (4, 256, 256), jnp.float32)
        _lenS = 256 - jax.random.randint(jax.random.fold_in(_rk, 7), (4,), 0, max(1, 256 // 4) + 1, jnp.int32)
        _lenS2 = 256 - jax.random.randint(jax.random.fold_in(_rk, 8), (4,), 0, max(1, 256 // 4) + 1, jnp.int32)
        _ctx_1024P = jax.random.normal(jax.random.fold_in(_rk, 11), (4, 16, 128), jnp.float32)
        _ctx_1024c = jax.random.dirichlet(jax.random.fold_in(_rk, 511), 0.3 * jnp.ones((16,), jnp.float32), (4, 256))
        _ctx_1024t = jnp.einsum('bsk,bkd->bsd', _ctx_1024c, _ctx_1024P)
        _ctx_1024t = _ctx_1024t * jax.lax.rsqrt(jnp.mean(jnp.square(_ctx_1024t)) + 1e-12) * 0.953939
        ctx_1024 = -0.000292821 + 1.00034 * (_ctx_1024t + 0.3 * jax.random.normal(jax.random.fold_in(_rk, 611), (4, 256, 128), jnp.float32))
        _g = jax.random.normal(jax.random.fold_in(_rk, 9001), (2, 4), jnp.float32)
        _g = jnp.sign(_g) * jnp.maximum(jnp.abs(_g), 1.0) + (_g == 0) * 1.0
        g_xattn = _g[0]
        g_ffn = _g[1]
        return (x, ctx_1024, g_xattn, g_ffn)
    x, ctx_1024, g_xattn, g_ffn = _rec_inputs()

    def _L0_xattn_setup():
        import jax, jax.numpy as jnp
        import numpy as np
        import math
        B, L, DM = (2, 256, 128)
        DS, DC, EXP = (16, 4, 2)
        DI = EXP * DM
        DR = math.ceil(DM / 16)
        DT_MIN, DT_MAX, DT_FLOOR = (0.001, 0.1, 0.0001)

        def _ssm_forward(hidden_states, z, in_proj_w, conv_w, conv_b, x_proj_w, dt_proj_w, dt_proj_b, A_log, D):
            b = hidden_states.shape[0]
            x = jnp.einsum('ed,bld->bel', in_proj_w, hidden_states)
            xp = jnp.pad(x, ((0, 0), (0, 0), (DC - 1, 0)))
            xc = jax.lax.conv_general_dilated(xp, conv_w[:, None, :], window_strides=(1,), padding='VALID', dimension_numbers=('NCH', 'OIH', 'NCH'), feature_group_count=DI)
            u = jax.nn.silu(xc + conv_b[None, :, None])
            x_dbl = jnp.einsum('ke,bel->bkl', x_proj_w, u)
            dt_lo = x_dbl[:, :DR]
            Bm = x_dbl[:, DR:DR + DS]
            Cm = x_dbl[:, DR + DS:]
            delta = jax.nn.softplus(jnp.einsum('er,brl->bel', dt_proj_w, dt_lo) + dt_proj_b[None, :, None])
            A = -jnp.exp(A_log)

            def step(state, xs):
                d_t, B_t, C_t, u_t = xs
                dA = jnp.exp(d_t[..., None] * A)
                state = state * dA + (d_t * u_t)[..., None] * B_t[:, None, :]
                y_t = jnp.einsum('ben,bn->be', state, C_t)
                return (state, y_t)
            xs = (jnp.moveaxis(delta, -1, 0), jnp.moveaxis(Bm, -1, 0), jnp.moveaxis(Cm, -1, 0), jnp.moveaxis(u, -1, 0))
            state0 = jnp.zeros((b, DI, DS), delta.dtype)
            _, ys = jax.lax.scan(step, state0, xs)
            y = jnp.moveaxis(ys, 0, -1)
            y = y + D[None, :, None] * u
            y = y * jax.nn.silu(z)
            return jnp.swapaxes(y, 1, 2)
        key = jax.random.key(seed)
        ks = jax.random.split(key, 8)
        hidden_states = jax.random.normal(ks[0], (B, L, DM), jnp.float32)
        z = jax.random.normal(ks[1], (B, DI, L), jnp.float32)
        in_proj_w = jax.random.normal(ks[2], (DI, DM), jnp.float32) * DM ** (-0.5)
        conv_w = jax.random.normal(ks[3], (DI, DC), jnp.float32) * DC ** (-0.5)
        conv_b = jnp.zeros((DI,), jnp.float32)
        x_proj_w = jax.random.normal(ks[4], (DR + 2 * DS, DI), jnp.float32) * DI ** (-0.5)
        dt_std = DR ** (-0.5)
        dt_proj_w = jax.random.uniform(ks[5], (DI, DR), jnp.float32, -dt_std, dt_std)
        dt = jnp.exp(jax.random.uniform(ks[6], (DI,), jnp.float32) * (math.log(DT_MAX) - math.log(DT_MIN)) + math.log(DT_MIN))
        dt = jnp.clip(dt, DT_FLOOR)
        dt_proj_b = dt + jnp.log(-jnp.expm1(-dt))
        A_log = jnp.log(jnp.broadcast_to(jnp.arange(1, DS + 1, dtype=jnp.float32), (DI, DS)))
        D = jnp.ones((DI,), jnp.float32)
        return dict(hidden_states=hidden_states, z=z, in_proj_w=in_proj_w, conv_w=conv_w, conv_b=conv_b, x_proj_w=x_proj_w, dt_proj_w=dt_proj_w, dt_proj_b=dt_proj_b, A_log=A_log, D=D)
    _L0_xattn_all = _L0_xattn_setup()
    _L0_xattn_in = {k: v for k, v in _L0_xattn_all.items() if k in ('in_proj_w', 'conv_w', 'conv_b', 'x_proj_w', 'dt_proj_w', 'dt_proj_b', 'A_log', 'D')}
    del _L0_xattn_all

    def _L0_ffn_setup():
        import jax, jax.numpy as jnp
        import numpy as np
        EPS = 1e-05

        def _quant_weight(w):
            scale = jnp.mean(jnp.abs(w)) + EPS
            wq = jnp.clip(jnp.round(w / scale), -1.0, 1.0)
            return (wq, scale)

        def _quant_act(x):
            s = jnp.max(jnp.abs(x), axis=-1, keepdims=True) / 127.0 + EPS
            xq = jnp.clip(jnp.round(x / s), -128.0, 127.0)
            return (xq, s)

        def _qlinear(x, w):
            wq, ws = _quant_weight(w)
            xq, xs = _quant_act(x)
            y = jnp.einsum('bsi,oi->bso', xq, wq)
            return y * xs * ws
        key = jax.random.key(seed)
        k1, k2, k3, k4 = jax.random.split(key, 4)
        H, I = (256, 1024)
        x = jax.random.normal(k1, (4, 512, H), dtype=jnp.float32)
        w_gate = jax.random.normal(k2, (I, H), dtype=jnp.float32) * (1.0 / np.sqrt(H))
        w_up = jax.random.normal(k3, (I, H), dtype=jnp.float32) * (1.0 / np.sqrt(H))
        w_down = jax.random.normal(k4, (H, I), dtype=jnp.float32) * (1.0 / np.sqrt(I))
        return {'x': x, 'w_gate': w_gate, 'w_up': w_up, 'w_down': w_down}
    _L0_ffn_all = _L0_ffn_setup()
    _L0_ffn_in = {k: v for k, v in _L0_ffn_all.items() if k in ('w_gate', 'w_up', 'w_down')}
    del _L0_ffn_all

    def _L1_xattn_setup():
        import jax, jax.numpy as jnp
        import numpy as np
        EPS = 1e-05

        def rmsnorm(x, g, eps=EPS):
            var = jnp.mean(jnp.square(x), axis=-1, keepdims=True)
            return x * jax.lax.rsqrt(var + eps) * g
        key = jax.random.key(seed)
        ks = jax.random.split(key, 8)
        B, Sq, Skv = (2, 512, 64)
        dim, cdim, H, D = (256, 128, 16, 128)
        inner = H * D
        s = lambda f: 1.0 / np.sqrt(f)
        return {'hidden_states': jax.random.normal(ks[0], (B, Sq, dim), jnp.float32), 'encoder_hidden_states': jax.random.normal(ks[1], (B, Skv, cdim), jnp.float32), 'Wq': jax.random.normal(ks[2], (dim, inner), jnp.float32) * s(dim), 'Wk': jax.random.normal(ks[3], (cdim, inner), jnp.float32) * s(cdim), 'Wv': jax.random.normal(ks[4], (cdim, inner), jnp.float32) * s(cdim), 'Wo': jax.random.normal(ks[5], (inner, dim), jnp.float32) * s(inner), 'gq': jnp.ones((D,), jnp.float32), 'gk': jnp.ones((D,), jnp.float32)}
    _L1_xattn_all = _L1_xattn_setup()
    _L1_xattn_in = {k: v for k, v in _L1_xattn_all.items() if k in ('Wq', 'Wk', 'Wv', 'Wo', 'gq', 'gk')}
    del _L1_xattn_all

    def _L1_ffn_setup():
        import jax, jax.numpy as jnp
        import numpy as np
        B, S, H = (4, 128, 256)
        E, K, I, SI = (16, 4, 176, 704)

        def _silu_mul(gu, inter):
            return jax.nn.silu(gu[:, :inter]) * gu[:, inter:]
        key = jax.random.key(seed)
        ks = jax.random.split(key, 7)
        s = 0.02
        return {'hidden_states': jax.random.normal(ks[0], (B, S, H), jnp.float32), 'gate_w': jax.random.normal(ks[1], (E, H), jnp.float32) * s, 'expert_gate_up': jax.random.normal(ks[2], (E, 2 * I, H), jnp.float32) * s, 'expert_down': jax.random.normal(ks[3], (E, H, I), jnp.float32) * s, 'shared_gate_up': jax.random.normal(ks[4], (2 * SI, H), jnp.float32) * s, 'shared_down': jax.random.normal(ks[5], (H, SI), jnp.float32) * s, 'shared_gate_vec': jax.random.normal(ks[6], (1, H), jnp.float32) * s}
    _L1_ffn_all = _L1_ffn_setup()
    _L1_ffn_in = {k: v for k, v in _L1_ffn_all.items() if k in ('gate_w', 'expert_gate_up', 'expert_down', 'shared_gate_up', 'shared_down', 'shared_gate_vec')}
    del _L1_ffn_all

    def _L2_xattn_setup():
        import jax, jax.numpy as jnp
        import numpy as np
        key = jax.random.key(seed)
        ks = jax.random.split(key, 6)
        B, L, N, C, D = (8, 64, 256, 128, 128)
        return {'teacher_logits': jax.random.normal(ks[0], (B, L, N), dtype=jnp.float32), 'teacher_features': jax.random.normal(ks[1], (B, N, C), dtype=jnp.float32), 'Wq': jax.random.normal(ks[2], (D, C), dtype=jnp.float32) * (1.0 / np.sqrt(C)), 'bq': jnp.zeros((D,), dtype=jnp.float32), 'Wk': jax.random.normal(ks[3], (D, C), dtype=jnp.float32) * (1.0 / np.sqrt(C)), 'bk': jnp.zeros((D,), dtype=jnp.float32)}
    _L2_xattn_all = _L2_xattn_setup()
    _L2_xattn_in = {k: v for k, v in _L2_xattn_all.items() if k in ('Wq', 'bq', 'Wk', 'bk')}
    del _L2_xattn_all

    def _L2_ffn_setup():
        import jax, jax.numpy as jnp
        import numpy as np
        B, S, D, H = (4, 256, 256, 1024)

        def fwht(x):
            orig_shape = x.shape
            n = orig_shape[-1]
            x = x.reshape(-1, n)
            h = 1
            while h < n:
                xb = x.reshape(-1, n // (2 * h), 2, h)
                a = xb[:, :, 0, :]
                b = xb[:, :, 1, :]
                x = jnp.stack([a + b, a - b], axis=2).reshape(-1, n)
                h *= 2
            scale = jnp.asarray(1.0 / np.sqrt(n), dtype=x.dtype)
            return (x * scale).reshape(orig_shape)
        key = jax.random.key(seed)
        kx, k1, k2, k3 = jax.random.split(key, 4)
        x = jax.random.normal(kx, (B, S, D), dtype=jnp.float32)
        W1 = jax.random.normal(k1, (H, D), dtype=jnp.float32) * (1.0 / np.sqrt(D))
        W2 = jax.random.normal(k2, (D, H), dtype=jnp.float32) * (1.0 / np.sqrt(H))
        W3 = jax.random.normal(k3, (H, D), dtype=jnp.float32) * (1.0 / np.sqrt(D))
        return {'x': x, 'W1': W1, 'W2': W2, 'W3': W3}
    _L2_ffn_all = _L2_ffn_setup()
    _L2_ffn_in = {k: v for k, v in _L2_ffn_all.items() if k in ('W1', 'W2', 'W3')}
    del _L2_ffn_all

    def _L3_xattn_setup():
        import jax, jax.numpy as jnp
        import numpy as np
        key = jax.random.key(seed)
        ks = jax.random.split(key, 6)
        B, L, N, C, D = (8, 64, 256, 128, 128)
        return {'teacher_logits': jax.random.normal(ks[0], (B, L, N), dtype=jnp.float32), 'teacher_features': jax.random.normal(ks[1], (B, N, C), dtype=jnp.float32), 'Wq': jax.random.normal(ks[2], (D, C), dtype=jnp.float32) * (1.0 / np.sqrt(C)), 'bq': jnp.zeros((D,), dtype=jnp.float32), 'Wk': jax.random.normal(ks[3], (D, C), dtype=jnp.float32) * (1.0 / np.sqrt(C)), 'bk': jnp.zeros((D,), dtype=jnp.float32)}
    _L3_xattn_all = _L3_xattn_setup()
    _L3_xattn_in = {k: v for k, v in _L3_xattn_all.items() if k in ('Wq', 'bq', 'Wk', 'bk')}
    del _L3_xattn_all

    def _L3_ffn_setup():
        import jax, jax.numpy as jnp
        import numpy as np
        TOP_K = 2
        key = jax.random.key(seed)
        ks = jax.random.split(key, 6)
        B, S, H, F, E = (1, 256, 256, 176, 8)
        Fs = 2 * F
        std = jnp.float32(0.02)
        return {'hidden_states': jax.random.normal(ks[0], (B, S, H), jnp.float32), 'gate_weight': jax.random.normal(ks[1], (E, H), jnp.float32) * std, 'gate_up_weights': jax.random.normal(ks[2], (E, 2 * F, H), jnp.float32) * std, 'down_weights': jax.random.normal(ks[3], (E, H, F), jnp.float32) * std, 'shared_gate_up': jax.random.normal(ks[4], (2 * Fs, H), jnp.float32) * std, 'shared_down': jax.random.normal(ks[5], (H, Fs), jnp.float32) * std}
    _L3_ffn_all = _L3_ffn_setup()
    _L3_ffn_in = {k: v for k, v in _L3_ffn_all.items() if k in ('gate_weight', 'gate_up_weights', 'down_weights', 'shared_gate_up', 'shared_down')}
    del _L3_ffn_all
    return {'x': x, 'ctx_1024': ctx_1024, 'g_xattn': g_xattn, 'g_ffn': g_ffn, 'L0_xattn_in_proj_w': _L0_xattn_in['in_proj_w'], 'L0_xattn_conv_w': _L0_xattn_in['conv_w'], 'L0_xattn_conv_b': _L0_xattn_in['conv_b'], 'L0_xattn_x_proj_w': _L0_xattn_in['x_proj_w'], 'L0_xattn_dt_proj_w': _L0_xattn_in['dt_proj_w'], 'L0_xattn_dt_proj_b': _L0_xattn_in['dt_proj_b'], 'L0_xattn_A_log': _L0_xattn_in['A_log'], 'L0_xattn_D': _L0_xattn_in['D'], 'L0_ffn_w_gate': _L0_ffn_in['w_gate'], 'L0_ffn_w_up': _L0_ffn_in['w_up'], 'L0_ffn_w_down': _L0_ffn_in['w_down'], 'L1_xattn_Wq': _L1_xattn_in['Wq'], 'L1_xattn_Wk': _L1_xattn_in['Wk'], 'L1_xattn_Wv': _L1_xattn_in['Wv'], 'L1_xattn_Wo': _L1_xattn_in['Wo'], 'L1_xattn_gq': _L1_xattn_in['gq'], 'L1_xattn_gk': _L1_xattn_in['gk'], 'L1_ffn_gate_w': _L1_ffn_in['gate_w'], 'L1_ffn_expert_gate_up': _L1_ffn_in['expert_gate_up'], 'L1_ffn_expert_down': _L1_ffn_in['expert_down'], 'L1_ffn_shared_gate_up': _L1_ffn_in['shared_gate_up'], 'L1_ffn_shared_down': _L1_ffn_in['shared_down'], 'L1_ffn_shared_gate_vec': _L1_ffn_in['shared_gate_vec'], 'L2_xattn_Wq': _L2_xattn_in['Wq'], 'L2_xattn_bq': _L2_xattn_in['bq'], 'L2_xattn_Wk': _L2_xattn_in['Wk'], 'L2_xattn_bk': _L2_xattn_in['bk'], 'L2_ffn_W1': _L2_ffn_in['W1'], 'L2_ffn_W2': _L2_ffn_in['W2'], 'L2_ffn_W3': _L2_ffn_in['W3'], 'L3_xattn_Wq': _L3_xattn_in['Wq'], 'L3_xattn_bq': _L3_xattn_in['bq'], 'L3_xattn_Wk': _L3_xattn_in['Wk'], 'L3_xattn_bk': _L3_xattn_in['bk'], 'L3_ffn_gate_weight': _L3_ffn_in['gate_weight'], 'L3_ffn_gate_up_weights': _L3_ffn_in['gate_up_weights'], 'L3_ffn_down_weights': _L3_ffn_in['down_weights'], 'L3_ffn_shared_gate_up': _L3_ffn_in['shared_gate_up'], 'L3_ffn_shared_down': _L3_ffn_in['shared_down']}

def reference(x, ctx_1024, g_xattn, g_ffn, L0_xattn_in_proj_w, L0_xattn_conv_w, L0_xattn_conv_b, L0_xattn_x_proj_w, L0_xattn_dt_proj_w, L0_xattn_dt_proj_b, L0_xattn_A_log, L0_xattn_D, L0_ffn_w_gate, L0_ffn_w_up, L0_ffn_w_down, L1_xattn_Wq, L1_xattn_Wk, L1_xattn_Wv, L1_xattn_Wo, L1_xattn_gq, L1_xattn_gk, L1_ffn_gate_w, L1_ffn_expert_gate_up, L1_ffn_expert_down, L1_ffn_shared_gate_up, L1_ffn_shared_down, L1_ffn_shared_gate_vec, L2_xattn_Wq, L2_xattn_bq, L2_xattn_Wk, L2_xattn_bk, L2_ffn_W1, L2_ffn_W2, L2_ffn_W3, L3_xattn_Wq, L3_xattn_bq, L3_xattn_Wk, L3_xattn_bk, L3_ffn_gate_weight, L3_ffn_gate_up_weights, L3_ffn_down_weights, L3_ffn_shared_gate_up, L3_ffn_shared_down):
    import jax
    import jax.numpy as jnp

    def _L0_xattn_ref(hidden_states, z, in_proj_w, conv_w, conv_b, x_proj_w, dt_proj_w, dt_proj_b, A_log, D):
        import jax, jax.numpy as jnp
        import numpy as np
        import math
        B, L, DM = (2, 256, 128)
        DS, DC, EXP = (16, 4, 2)
        DI = EXP * DM
        DR = math.ceil(DM / 16)
        DT_MIN, DT_MAX, DT_FLOOR = (0.001, 0.1, 0.0001)

        def _ssm_forward(hidden_states, z, in_proj_w, conv_w, conv_b, x_proj_w, dt_proj_w, dt_proj_b, A_log, D):
            b = hidden_states.shape[0]
            x = jnp.einsum('ed,bld->bel', in_proj_w, hidden_states)
            xp = jnp.pad(x, ((0, 0), (0, 0), (DC - 1, 0)))
            xc = jax.lax.conv_general_dilated(xp, conv_w[:, None, :], window_strides=(1,), padding='VALID', dimension_numbers=('NCH', 'OIH', 'NCH'), feature_group_count=DI)
            u = jax.nn.silu(xc + conv_b[None, :, None])
            x_dbl = jnp.einsum('ke,bel->bkl', x_proj_w, u)
            dt_lo = x_dbl[:, :DR]
            Bm = x_dbl[:, DR:DR + DS]
            Cm = x_dbl[:, DR + DS:]
            delta = jax.nn.softplus(jnp.einsum('er,brl->bel', dt_proj_w, dt_lo) + dt_proj_b[None, :, None])
            A = -jnp.exp(A_log)

            def step(state, xs):
                d_t, B_t, C_t, u_t = xs
                dA = jnp.exp(d_t[..., None] * A)
                state = state * dA + (d_t * u_t)[..., None] * B_t[:, None, :]
                y_t = jnp.einsum('ben,bn->be', state, C_t)
                return (state, y_t)
            xs = (jnp.moveaxis(delta, -1, 0), jnp.moveaxis(Bm, -1, 0), jnp.moveaxis(Cm, -1, 0), jnp.moveaxis(u, -1, 0))
            state0 = jnp.zeros((b, DI, DS), delta.dtype)
            _, ys = jax.lax.scan(step, state0, xs)
            y = jnp.moveaxis(ys, 0, -1)
            y = y + D[None, :, None] * u
            y = y * jax.nn.silu(z)
            return jnp.swapaxes(y, 1, 2)
        return _ssm_forward(hidden_states, z, in_proj_w, conv_w, conv_b, x_proj_w, dt_proj_w, dt_proj_b, A_log, D)

    def _L0_ffn_ref(x, w_gate, w_up, w_down):
        import jax, jax.numpy as jnp
        import numpy as np
        EPS = 1e-05

        def _quant_weight(w):
            scale = jnp.mean(jnp.abs(w)) + EPS
            wq = jnp.clip(jnp.round(w / scale), -1.0, 1.0)
            return (wq, scale)

        def _quant_act(x):
            s = jnp.max(jnp.abs(x), axis=-1, keepdims=True) / 127.0 + EPS
            xq = jnp.clip(jnp.round(x / s), -128.0, 127.0)
            return (xq, s)

        def _qlinear(x, w):
            wq, ws = _quant_weight(w)
            xq, xs = _quant_act(x)
            y = jnp.einsum('bsi,oi->bso', xq, wq)
            return y * xs * ws
        gate = jax.nn.silu(_qlinear(x, w_gate))
        up = _qlinear(x, w_up)
        return _qlinear(gate * up, w_down)

    def _L1_xattn_ref(hidden_states, encoder_hidden_states, Wq, Wk, Wv, Wo, gq, gk):
        import jax, jax.numpy as jnp
        import numpy as np
        EPS = 1e-05

        def rmsnorm(x, g, eps=EPS):
            var = jnp.mean(jnp.square(x), axis=-1, keepdims=True)
            return x * jax.lax.rsqrt(var + eps) * g
        B, Sq, _ = hidden_states.shape
        Skv = encoder_hidden_states.shape[1]
        D = gq.shape[0]
        H = Wq.shape[1] // D
        scale = 1.0 / np.sqrt(D)
        q = (hidden_states @ Wq).reshape(B, Sq, H, D)
        k = (encoder_hidden_states @ Wk).reshape(B, Skv, H, D)
        v = (encoder_hidden_states @ Wv).reshape(B, Skv, H, D)
        q = rmsnorm(q, gq)
        k = rmsnorm(k, gk)
        scores = jnp.einsum('bqhd,bkhd->bhqk', q, k) * scale
        attn = jax.nn.softmax(scores, axis=-1)
        out = jnp.einsum('bhqk,bkhd->bqhd', attn, v)
        out = out.reshape(B, Sq, H * D)
        return out @ Wo

    def _L1_ffn_ref(hidden_states, gate_w, expert_gate_up, expert_down, shared_gate_up, shared_down, shared_gate_vec):
        import jax, jax.numpy as jnp
        import numpy as np
        B, S, H = (4, 128, 256)
        E, K, I, SI = (16, 4, 176, 704)

        def _silu_mul(gu, inter):
            return jax.nn.silu(gu[:, :inter]) * gu[:, inter:]
        orig_shape = hidden_states.shape
        x = hidden_states.reshape(-1, H)
        router_logits = x @ gate_w.T
        routing_probs = jax.nn.softmax(router_logits.astype(jnp.float32), axis=-1)
        topk_w, topk_idx = jax.lax.top_k(routing_probs, K)
        topk_w = topk_w / topk_w.sum(axis=-1, keepdims=True)
        topk_w = topk_w.astype(x.dtype)
        combine = (jax.nn.one_hot(topk_idx, E, dtype=x.dtype) * topk_w[..., None]).sum(1)
        shared = _silu_mul(x @ shared_gate_up.T, SI) @ shared_down.T
        shared = shared * jax.nn.sigmoid(x @ shared_gate_vec.T)

        def step(acc, ew):
            w_gu, w_d, cw = ew
            h = _silu_mul(x @ w_gu.T, I)
            return (acc + h @ w_d.T * cw[:, None], None)
        acc0 = jnp.zeros_like(x)
        sparse, _ = jax.lax.scan(step, acc0, (expert_gate_up, expert_down, combine.T))
        return (shared + sparse).reshape(orig_shape)

    def _L2_xattn_ref(teacher_logits, teacher_features, Wq, bq, Wk, bk):
        import jax, jax.numpy as jnp
        import numpy as np
        query = jnp.einsum('bnc,dc->bnd', teacher_features, Wq) + bq
        key = jnp.einsum('bnc,dc->bnd', teacher_features, Wk) + bk
        energy = jnp.einsum('bnd,bmd->bnm', query, key)
        attention = jax.nn.softmax(energy, axis=-1)
        x_m = jnp.einsum('bln,bmn->blm', teacher_logits, attention)
        return x_m

    def _L2_ffn_ref(x, W1, W2, W3):
        import jax, jax.numpy as jnp
        import numpy as np
        B, S, D, H = (4, 256, 256, 1024)

        def fwht(x):
            orig_shape = x.shape
            n = orig_shape[-1]
            x = x.reshape(-1, n)
            h = 1
            while h < n:
                xb = x.reshape(-1, n // (2 * h), 2, h)
                a = xb[:, :, 0, :]
                b = xb[:, :, 1, :]
                x = jnp.stack([a + b, a - b], axis=2).reshape(-1, n)
                h *= 2
            scale = jnp.asarray(1.0 / np.sqrt(n), dtype=x.dtype)
            return (x * scale).reshape(orig_shape)
        up_gate = jnp.einsum('bsd,hd->bsh', x, W1)
        up_lin = jnp.einsum('bsd,hd->bsh', x, W3)
        hidden = jax.nn.silu(up_gate) * up_lin
        hidden = fwht(hidden)
        out = jnp.einsum('bsh,dh->bsd', hidden, W2)
        return out

    def _L3_xattn_ref(teacher_logits, teacher_features, Wq, bq, Wk, bk):
        import jax, jax.numpy as jnp
        import numpy as np
        query = jnp.einsum('bnc,dc->bnd', teacher_features, Wq) + bq
        key = jnp.einsum('bnc,dc->bnd', teacher_features, Wk) + bk
        energy = jnp.einsum('bnd,bmd->bnm', query, key)
        attention = jax.nn.softmax(energy, axis=-1)
        x_m = jnp.einsum('bln,bmn->blm', teacher_logits, attention)
        return x_m

    def _L3_ffn_ref(hidden_states, gate_weight, gate_up_weights, down_weights, shared_gate_up, shared_down):
        import jax, jax.numpy as jnp
        import numpy as np
        TOP_K = 2
        B, S, H = hidden_states.shape
        E, twoF, _ = gate_up_weights.shape
        F = twoF // 2
        T = B * S
        x = hidden_states.reshape(T, H)
        logits = x @ gate_weight.T
        scores = jax.nn.softmax(logits, axis=-1)
        topk_w, topk_idx = jax.lax.top_k(scores, TOP_K)
        combine = jnp.zeros((T, E), x.dtype).at[jnp.arange(T)[:, None], topk_idx].add(topk_w)
        gu = jnp.einsum('th,efh->tef', x, gate_up_weights)
        act = jax.nn.silu(gu[..., :F]) * gu[..., F:]
        y = jnp.einsum('tef,te,ehf->th', act, combine, down_weights)
        Fs = shared_gate_up.shape[0] // 2
        sgu = x @ shared_gate_up.T
        sact = jax.nn.silu(sgu[:, :Fs]) * sgu[:, Fs:]
        y = y + sact @ shared_down.T
        return y.reshape(B, S, H)
    x = x + jnp.tanh(g_xattn[0]) * _L0_xattn_ref(ctx_1024, _layernorm(x, axis=-1), L0_xattn_in_proj_w, L0_xattn_conv_w, L0_xattn_conv_b, L0_xattn_x_proj_w, L0_xattn_dt_proj_w, L0_xattn_dt_proj_b, L0_xattn_A_log, L0_xattn_D)
    x = x + jnp.tanh(g_ffn[0]) * _L0_ffn_ref(_layernorm(x, axis=-1), L0_ffn_w_gate, L0_ffn_w_up, L0_ffn_w_down)
    x = x + jnp.tanh(g_xattn[1]) * _L1_xattn_ref(_layernorm(x, axis=-1), ctx_1024, L1_xattn_Wq, L1_xattn_Wk, L1_xattn_Wv, L1_xattn_Wo, L1_xattn_gq, L1_xattn_gk)
    x = x + jnp.tanh(g_ffn[1]) * _L1_ffn_ref(_layernorm(x, axis=-1), L1_ffn_gate_w, L1_ffn_expert_gate_up, L1_ffn_expert_down, L1_ffn_shared_gate_up, L1_ffn_shared_down, L1_ffn_shared_gate_vec)
    x = x + jnp.tanh(g_xattn[2]) * _L2_xattn_ref(_layernorm(x, axis=-1), ctx_1024, L2_xattn_Wq, L2_xattn_bq, L2_xattn_Wk, L2_xattn_bk)
    x = x + jnp.tanh(g_ffn[2]) * _L2_ffn_ref(_layernorm(x, axis=-1), L2_ffn_W1, L2_ffn_W2, L2_ffn_W3)
    x = x + jnp.tanh(g_xattn[3]) * _L3_xattn_ref(_layernorm(x, axis=-1), ctx_1024, L3_xattn_Wq, L3_xattn_bq, L3_xattn_Wk, L3_xattn_bk)
    x = x + jnp.tanh(g_ffn[3]) * _L3_ffn_ref(_layernorm(x, axis=-1), L3_ffn_gate_weight, L3_ffn_gate_up_weights, L3_ffn_down_weights, L3_ffn_shared_gate_up, L3_ffn_shared_down)
    return x

_drawn_inputs = setup_inputs


def setup_inputs(seed=0):
    import zlib

    import numpy as np

    out = dict(_drawn_inputs(seed))
    spreads = {'L0_xattn_conv_b': (0.0, 0.1),
     'L0_xattn_D': (1.0, 0.2),
     'L1_xattn_gq': (1.0, 0.2),
     'L1_xattn_gk': (1.0, 0.2),
     'L2_xattn_bq': (0.0, 0.1),
     'L2_xattn_bk': (0.0, 0.8),
     'L3_xattn_bq': (0.0, 0.1),
     'L3_xattn_bk': (0.0, 0.8)}
    factors = {'g_ffn': 8.0,
     'L0_xattn_dt_proj_w': 7.34,
     'L0_xattn_dt_proj_b': 3.418,
     'L0_xattn_A_log': 2.957,
     'L1_ffn_gate_w': 8.0,
     'L1_ffn_expert_gate_up': 8.0,
     'L1_ffn_expert_down': 8.0,
     'L1_ffn_shared_gate_up': 4.877,
     'L1_ffn_shared_down': 4.802,
     'L1_ffn_shared_gate_vec': 8.0,
     'L3_ffn_gate_weight': 8.0,
     'L3_ffn_gate_up_weights': 8.0,
     'L3_ffn_down_weights': 8.0,
     'L3_ffn_shared_gate_up': 5.825,
     'L3_ffn_shared_down': 5.782}
    for name, (base, spread) in spreads.items():
        noise = np.random.default_rng([zlib.crc32(name.encode()), seed]).standard_normal(out[name].shape)
        drawn = base * np.exp(spread * noise) if base else spread * noise
        out[name] = jnp.asarray(drawn.astype(out[name].dtype))
    for name, factor in factors.items():
        out[name] = (out[name] * factor).astype(out[name].dtype)
    return out
```

```python
def flamingo_kernel(nc, dram, out):
    import concourse.bass as bass
    from concourse import mybir
    from contextlib import ExitStack

    f32, bf16 = mybir.dt.float32, mybir.dt.bfloat16
    ALU, ACT = mybir.AluOpType, mybir.ActivationFunctionType
    AX = mybir.AxisListType.X

    P = 128
    DM, TOK, HALF = 256, 1024, 512
    NT, TH = TOK // P, HALF // P
    KC = DM // P
    NS = 16
    HEADS = 16
    I0, I2 = 1024, 1024
    E1, F1, TOP1 = 16, 176, 4
    E3, F3, TOP3 = 8, 176, 2
    I1, I3 = 20 * F1, 10 * F3
    NJ = {1: -(-I1 // P), 2: I2 // P, 3: -(-I3 // P)}
    WIDTH = {1: I1, 2: I2, 3: I3}
    MAGIC = 1.5 * 2.0 ** 23
    EPS = 1e-5
    SCALE = float(P) ** -0.5

    at = {"fixed": -(-nc.sbuf_base // 64) * 64}
    limit = nc.sbuf_usable_end

    def place(region, name, shape, dt=f32):
        size = 2 if dt == bf16 else 4
        for n in shape[1:]:
            size *= n
        size = -(-size // 64) * 64
        t = nc.alloc_sbuf_tensor_at(name, shape, dt, offset=at[region])
        at[region] += size
        assert at[region] <= limit, (name, at[region], limit)
        return t

    x = place("fixed", "x_res", [P, NT, DM])
    xn = [place("fixed", f"x_norm{h}", [P, TH, DM]) for h in range(2)]
    xnT = place("fixed", "x_norm_T", [P, KC, HALF])
    ctxT = place("fixed", "ctx_T", [P, TOK])
    ctk = place("fixed", "ctx_tok", [P, NT, P])
    small = place("fixed", "small_params", [P, 64])
    ident = place("fixed", "ident_f", [P, P])
    identb = place("fixed", "ident_b", [P, P], bf16)
    had = place("fixed", "hadamard", [P, P])
    ones = place("fixed", "ones", [P, P])
    sel_bc = place("fixed", "sel_bc", [96, 2 * NS, P], bf16)
    sel1 = place("fixed", "sel1", [96, NJ[1], P], bf16)
    sel3 = place("fixed", "sel3", [96, NJ[3], P], bf16)
    tg = place("fixed", "tanh_gates", [P, 8])
    negA = place("fixed", "neg_A", [P, 2, NS])
    wabs = place("fixed", "w_abs", [P, 3])
    wscale = place("fixed", "w_scale", [P, 3])
    winv = place("fixed", "w_inv", [P, 3])
    epsc = place("fixed", "eps_col", [P, 1])
    mhalf = place("fixed", "minus_half", [P, TH])
    gqk = place("fixed", "g_qk", [P, 1])
    bst = place("fixed", "bn_st", [P, TH, 6])
    mv = place("fixed", "bn_mv", [P, TH, 2])
    ve = place("fixed", "var_eps", [P, TH])
    rstd = place("fixed", "rstd", [P, TH])
    mask_small = place("fixed", "scratch_small", [P, 64])

    at["A1"] = at["A2"] = at["fixed"]
    wq = place("A1", "a1_wq", [P, KC, HEADS * P])
    wk = place("A1", "a1_wk", [P, HEADS * P])
    wvo = place("A1", "a1_wvo", [P, HEADS, DM])
    w1t = place("A2", "f2_w1", [P, KC, I2])
    w3t = place("A2", "f2_w3", [P, KC, I2])
    w2t = place("A2", "f2_w2", [P, I2 // P, DM])
    attT = place("A2", "att_T", [P, 2, 2, HALF])
    attT2 = place("A2", "att_T2", [P, 2, 2, HALF])
    at["B"] = max(at["A1"], at["A2"])
    at["B0"] = at["B1"] = at["B3"] = at["B"]
    f1g = place("B1", "f1_gate", [P, KC, I1])
    f1u = place("B1", "f1_up", [P, KC, I1])
    f1d = place("B1", "f1_down", [P, NJ[1], DM])
    f1r = place("B1", "f1_router", [P, KC, E1 + 1])
    f3g = place("B3", "f3_gate", [P, KC, I3])
    f3u = place("B3", "f3_up", [P, KC, I3])
    f3d = place("B3", "f3_down", [P, NJ[3], DM])
    f3r = place("B3", "f3_router", [P, KC, E3])
    w0raw = place("B0", "w0_raw", [P, 3, KC * I0])
    at["Bp"] = at["Bm"] = at["Bf"] = at["B0"]
    wvT = place("Bp", "a1_wvT", [P, HEADS, P])
    wo = place("Bp", "a1_wo", [P, HEADS, DM])
    wtmp = place("Bp", "w_tmp", [P, 2, KC * I0])
    xpad = place("Bm", "m_xpad", [P, 2, 2, DM + 3])
    u = place("Bm", "m_u", [P, 2, HALF])
    dlt = place("Bm", "m_delta", [P, 2, HALF])
    du = place("Bm", "m_du", [P, 2, HALF])
    zs = place("Bm", "m_z", [P, TH, DM])
    dA = [place("Bm", f"m_dA{i}", [P, 2, HALF]) for i in range(2)]
    dBu = [place("Bm", f"m_dBu{i}", [P, 2, HALF]) for i in range(2)]
    Bs = [place("Bm", f"m_Bs{i}", [P, HALF]) for i in range(2)]
    hst = place("Bm", "m_h", [P, 2, HALF])
    hC = [place("Bm", f"m_hC{i}", [P, 2, HALF]) for i in range(2)]
    bcs = place("Bm", "m_bc_split", [96, HALF], bf16)
    dts = place("Bm", "m_dt", [8, HALF])
    m_in = place("Bm", "m_in_w", [P, DM])
    m_bc = place("Bm", "m_bc_w", [P, 2, 96])
    m_dt = place("Bm", "m_dt_w", [P, 2, 8])
    m_dtw = place("Bm", "m_dtw", [8, DM])
    xq = place("Bf", "q_x", [P, TH, DM], bf16)
    xqa = place("Bf", "q_xa", [P, TH, DM])
    xqT = place("Bf", "q_xT", [P, KC, HALF], bf16)
    sg0 = [place("Bf", f"q_sg{i}", [P, I0]) for i in range(2)]
    h0 = place("Bf", "q_h", [P, I0])
    h0a = place("Bf", "q_ha", [P, I0])
    hq = place("Bf", "q_hq", [P, I0], bf16)
    hqT = place("Bf", "q_hqT", [P, I0 // P, P], bf16)
    qs = place("Bf", "q_scales", [P, 8 * TH])
    qt = place("Bf", "q_tile_scales", [P, 4])
    at["W"] = max(at["B1"], at["B3"], at["Bp"], at["Bm"], at["Bf"])
    at["W0"] = at["W1"] = at["W2"] = at["W3"] = at["W"]
    w0q = [place("W0", f"w0_quant{i}", [P, KC * I0], bf16) for i in range(3)]
    qT = place("W1", "a_qT", [P, HALF])
    kT = place("W1", "a_kT", [P, HALF])
    qsq = place("W1", "a_qsq", [P, HALF])
    ksq = place("W1", "a_ksq", [P, HALF])
    rk = place("W1", "a_rk", [P, HALF])
    rkl = place("W1", "a_rk_ln", [P, HALF])
    khat = place("W1", "a_khat", [P, HALF])
    Pm = place("W1", "a_P", [P, TH, DM])
    PT = place("W1", "a_PT", [P, 2, HALF])
    ACs = place("W1", "a_AC", [P, HALF])
    rq = place("W1", "a_rq", [P, TH])
    rql = place("W1", "a_rq_ln", [P, TH])
    nb = place("W1", "a_negmax", [P, TH])
    mx = place("W1", "a_max", [P, TH])
    rs = place("W1", "a_rowsum", [P, TH])
    ri = place("W1", "a_rowinv", [P, TH])
    sg = [place("W2", f"f_silu{i}", [P, HALF]) for i in range(2)]
    gu = [place("W2", f"f_gu{i}", [P, HALF]) for i in range(2)]
    hT = [place("W2", f"f_h{i}", [P, HALF]) for i in range(2)]
    cmb = place("W2", "r_combine", [P, TH, 96], bf16)
    cmbT = place("W2", "r_combine_T", [96, HALF], bf16)
    rl = place("W2", "r_logits", [P, TH, 24])
    rp = place("W2", "r_probs", [P, TH, 24])
    rr = place("W2", "r_replaced", [P, TH, 24])
    rt = place("W2", "r_top", [P, TH, 8])
    rw = place("W2", "r_weights", [P, TH, 24])
    rr2 = place("W2", "r_rest", [P, TH, 24])
    rc = place("W2", "r_columns", [P, 4, TH])
    aw = {l: [place("W3", f"m{l}_w{n}", [P, P]) for n in "qk"] for l in (2, 3)}
    aq = place("W3", "am_q", [P, TOK])
    ak = place("W3", "am_k", [P, TOK])
    aP = [place("W3", f"am_P{i}", [P, DM]) for i in range(2)]
    am = place("W3", "am_cols", [P, 8])
    wmix = [place("W3", f"w2_mix{i}", [P, I2 // P, DM]) for i in range(1)]

    c_gate, c_cw, c_cb, c_dtb, c_al, c_D, c_gq, c_gk, c_b = 0, 8, 16, 18, 20, 52, 54, 55, 56

    stack = ExitStack()
    ps = stack.enter_context(nc.psum_tensor("psum", [P, 8, 512], f32))
    psb = ps[:, :, :].bitcast(bf16)
    sems = {}

    def S(name):
        if name not in sems:
            sems[name] = stack.enter_context(nc.semaphore(name))
        return sems[name]

    LOADS = [
        ("x", x, 0), ("small", small, 0), ("w0raw", w0raw, 0), ("identb", identb, 0), ("ident", ident, 0),
        ("wvT", wvT, 0), ("wo", wo, 0), ("ctxT", ctxT, 0), ("ctk", ctk, 0),
        ("sel_bc", sel_bc, 0), ("wq", wq, 0), ("wk", wk, 0), ("sel1", sel1, 0), ("sel3", sel3, 0), ("had", had, 0),
        ("m_in", m_in, 1), ("m_bc", m_bc, 1), ("m_dt", m_dt, 1), ("m_dtw", m_dtw, 1),
        ("f1g", f1g, 5), ("f1u", f1u, 5), ("f1d", f1d, 5), ("f1r", f1r, 5),
        ("w1t", w1t, 7), ("w3t", w3t, 7), ("w2t", w2t, 7),
        ("f3g", f3g, 9), ("f3u", f3u, 9), ("f3d", f3d, 9), ("f3r", f3r, 9),
        ("m2q", aw[2][0], 9), ("m2k", aw[2][1], 9), ("m3q", aw[3][0], 9), ("m3k", aw[3][1], 9),
    ]

    ORDER = ["prep"] + [(b, h) for b in ("M", "F0", "A1", "F1") for h in range(2)] + ["maps"] + \
            [(b, h) for b in ("A2", "F2", "A3", "F3") for h in range(2)]
    POOL_STEPS = [k for k, s in enumerate(ORDER) if s != "prep" and s[0] in ("M", "A1")]

    def begin(eng, k):
        if k:
            eng.wait_ge(S("pe_step"), k)
            eng.wait_ge(S("act_step"), k)
            eng.wait_ge(S("dve_step"), k)
            done = sum(1 for s in POOL_STEPS if s < k)
            if done:
                eng.wait_ge(S("pool_step"), done)

    def loaded(eng, *names):
        for n in names:
            eng.wait_ge(S("ld_" + n), 16)

    def chain(eng, sem):
        n = [0]

        def link(ins):
            n[0] += 1
            ins.then_inc(S(sem), 1)
            eng.wait_ge(S(sem), n[0])
        return link

    def bc(ap, shape):
        return ap.to_broadcast(shape)

    gate_col = {"M": 0, "F0": 4, "A1": 1, "F1": 5, "A2": 2, "F2": 6, "A3": 3, "F3": 7}
    ln_index = {}
    n_ln = 2
    for s in ORDER[1:]:
        if s != "maps":
            ln_index[s] = len(ln_index) + 1
    xt_index = {s: i + 1 for i, s in enumerate(s for s in ORDER if s not in ("prep", "maps") and s[0] not in ("M", "F0"))}

    block = stack.enter_context(nc.Block())

    @block.sync
    def _(sp):
        reached = 0
        for name, dst, step in LOADS:
            if step > reached:
                begin(sp, step)
                reached = step
            full = tuple(slice(None) for _ in dst.shape)
            sp.dma_start(dst[full], dram[name]).then_inc(S("ld_" + name), 16)
        for h in range(2):
            sp.wait_ge(S("x_final"), h + 1)
            sp.dma_start(out[:, h * TH:(h + 1) * TH, :], x[:, h * TH:(h + 1) * TH, :]).then_inc(S("stored"), 16)
        sp.wait_ge(S("stored"), 32)

    @block.tensor
    def _(pe):
        mm = nc.tensor.matmul

        def transpose_norm(h, s, banks=(2, 3)):
            pe.wait_ge(S("ln_done"), ln_index[s])
            for c in range(KC):
                for t in range(TH):
                    last = nc.tensor.transpose(ps[:, banks[c], t * P:(t + 1) * P], xn[h][:, t, c * P:(c + 1) * P], ident[:, :])
            last.then_inc(S("xT_psum"), 1)
            pe.wait_ge(S("xT_ready"), xt_index[s])

        def prep(k):
            pe.wait_ge(S("ones_set"), 1)
            pe.wait_ge(S("wabs_part"), 1)
            mm(ps[:, 0, 0:3], ones[:, :], wabs[:, :], start=True, stop=True).then_inc(S("wabs_sum"), 1)
            loaded(pe, "wvT", "wo")
            for g in range(HEADS // 2):
                if g >= 4:
                    pe.wait_ge(S("wvo_copied"), g - 3)
                for i in range(2):
                    last = mm(ps[:, 2 + g % 4, i * DM:(i + 1) * DM], wvT[:, 2 * g + i, :], wo[:, 2 * g + i, :],
                              start=True, stop=True)
                last.then_inc(S("wvo_psum"), 1)
            last2 = last
            pe.wait_ge(S("wvo_copied"), HEADS // 2)
            mm(ps[:, 1, 0:3], ones[:, :], wabs[:, :], start=True, stop=True).then_inc(S("pe_step"), 1)

        def ssm(k, h):
            toks = slice(h * HALF, (h + 1) * HALF)
            loaded(pe, "ctxT", "m_in", "sel_bc")
            for e in range(2):
                last = mm(ps[:, e, :], m_in[:, e * P:(e + 1) * P], ctxT[:, toks], start=True, stop=True)
            last.then_inc(S("m_x"), 1)
            loaded(pe, "m_bc", "m_dt", "m_dtw")
            pe.wait_ge(S("m_u"), h + 1)
            for e in range(2):
                mm(ps[0:96, 2, :], m_bc[:, e, :], u[:, e, :], start=e == 0, stop=e == 1)
            for e in range(2):
                last = mm(ps[0:8, 3, :], m_dt[:, e, :], u[:, e, :], start=e == 0, stop=e == 1)
            last.then_inc(S("m_dbl"), 1)
            pe.wait_ge(S("m_dts"), h + 1)
            for e in range(2):
                last = mm(ps[:, e, :], m_dtw[:, e * P:(e + 1) * P], dts[:, :], start=True, stop=True)
            last.then_inc(S("m_dpre"), 1)
            pe.wait_ge(S("m_bcs"), h + 1)
            pe.wait_ge(S("m_xs"), h + 1)
            for n in range(NS + 1):
                g = h * NS + n
                if n < NS:
                    if n >= 2:
                        pe.wait_ge(S("m_Bcopy"), g - 1)
                        pe.wait_ge(S("m_hC"), g - 1)
                    mm(ps[:, 2 + n % 2, :], sel_bc[:, n, :], bcs[:, :], start=True, stop=True)
                    mm(ps[:, 4 + n % 2, :], sel_bc[:, NS + n, :], bcs[:, :], start=True, stop=True).then_inc(S("m_BC"), 1)
                if n:
                    pe.wait_ge(S("m_hC"), g)
                    for e in range(2):
                        last = mm(ps[:, e, :], ident[:, :], hC[(n - 1) % 2][:, e, :], start=n == 1, stop=n == NS)
                    last.then_inc(S("m_y"), 1)
            pe.wait_ge(S("m_yz"), h + 1)
            for t in range(TH):
                b, lb = t // 2, t % 2
                for e in range(2):
                    last = nc.tensor.transpose(ps[:, 6 + t // 2, (t % 2) * DM + e * P:(t % 2) * DM + (e + 1) * P],
                                               u[:, e, b * DM + lb * P:b * DM + (lb + 1) * P], ident[:, :])
            last.then_inc(S("pe_step"), 1)

        def ffn0(k, h):
            loaded(pe, "identb")
            pe.wait_ge(S("q_xq"), h + 1)
            for c in range(KC):
                for t in range(TH):
                    last = nc.tensor.transpose(psb[:, 2, c * HALF + t * P:c * HALF + (t + 1) * P],
                                               xq[:, t, c * P:(c + 1) * P], identb[:, :])
            last.then_inc(S("q_xTp"), 1)
            pe.wait_ge(S("q_xT"), h + 1)
            def down(t):
                g = h * TH + t
                pe.wait_ge(S("q_hq"), g + 1)
                if g:
                    pe.wait_ge(S("q_hT"), g)
                for j in range(I0 // P):
                    last = nc.tensor.transpose(psb[:, 7, j * P:(j + 1) * P], hq[:, j * P:(j + 1) * P], identb[:, :])
                last.then_inc(S("q_hTp"), 1)
                pe.wait_ge(S("q_hT"), g + 1)
                if t >= 2:
                    pe.wait_ge(S("q_out"), g - 1)
                for j in range(I0 // P):
                    last = mm(ps[:, t % 2, 0:DM], hqT[:, j, :], w0q[2][:, j * DM:(j + 1) * DM], start=j == 0, stop=j == I0 // P - 1)
                last.then_inc(S("q_down"), 1)
                return last
            for t in range(TH):
                g = h * TH + t
                for w, b0, free in ((0, 3, "q_sg"), (1, 5, "q_h")):
                    if t:
                        pe.wait_ge(S(free), g)
                    for n in range(2):
                        for c in range(KC):
                            last = mm(ps[:, b0 + n, :], xqT[:, c, t * P:(t + 1) * P],
                                      w0q[w][:, c * I0 + n * 512:c * I0 + (n + 1) * 512], start=c == 0, stop=c == KC - 1)
                    last.then_inc(S("q_gate" if w == 0 else "q_up"), 1)
                if t:
                    down(t - 1)
            down(TH - 1)
            pe.wait_ge(S("q_down"), (h + 1) * TH)
            nc.tensor.transpose(psb[:, 2, 0:P], identb[:, :], identb[:, :]).then_inc(S("pe_step"), 1)

        def attn1(k, h):
            toks = slice(h * HALF, (h + 1) * HALF)
            loaded(pe, "wq", "wk", "ctk")
            transpose_norm(h, ("A1", h), (6, 7))
            for i in range(HEADS + 1):
                g = h * HEADS + i
                if i < HEADS:
                    if i:
                        pe.wait_ge(S("a_rk"), g)
                    mm(ps[:, 7, :], wk[:, i * P:(i + 1) * P], ctxT[:, toks], start=True, stop=True).then_inc(S("a_k"), 1)
                    if i:
                        pe.wait_ge(S("a_rq"), g)
                    for c in range(KC):
                        last = mm(ps[:, 6, :], wq[:, c, i * P:(i + 1) * P], xnT[:, c, :], start=c == 0, stop=c == KC - 1)
                    last.then_inc(S("a_q"), 1)
                if i:
                    pe.wait_ge(S("a_pn"), g)
                    if i > 1:
                        pe.wait_ge(S("a_acs"), g - 1)
                    for t in range(TH):
                        b, qb = t // 2, t % 2
                        for kv in range(2):
                            last = nc.tensor.transpose(ps[:, 4 + b, kv * DM + qb * P:kv * DM + (qb + 1) * P],
                                                       Pm[:, t, kv * P:(kv + 1) * P], ident[:, :])
                    last.then_inc(S("a_pt"), 1)
                if i < HEADS:
                    pe.wait_ge(S("a_ksq"), g + 1)
                    mm(ps[:, 7, :], ones[:, :], ksq[:, :], start=True, stop=True).then_inc(S("a_kn"), 1)
                    pe.wait_ge(S("a_qsq"), g + 1)
                    for t in range(TH):
                        last = mm(ps[:, 6, t:t + 1], qsq[:, t * P:(t + 1) * P], ones[:, 0:1], start=True, stop=True)
                    last.then_inc(S("a_qn"), 1)
                if i:
                    pe.wait_ge(S("a_pts"), g)
                    for b in range(2):
                        for kv in range(2):
                            last = mm(ps[:, 4, b * DM:(b + 1) * DM], ctk[:, h * TH + 2 * b + kv, :],
                                      PT[:, b, kv * DM:(kv + 1) * DM], start=kv == 0, stop=kv == 1)
                    last.then_inc(S("a_ac"), 1)
                if i < HEADS:
                    pe.wait_ge(S("a_khat"), g + 1)
                    if i:
                        pe.wait_ge(S("a_exp"), g)
                    for t in range(TH):
                        last = mm(ps[:, 2 + t // 2, (t % 2) * DM:(t % 2 + 1) * DM], qT[:, t * P:(t + 1) * P],
                                  khat[:, (t // 2) * DM:(t // 2 + 1) * DM], start=True, stop=True)
                    last.then_inc(S("a_s"), 1)
                if i:
                    pe.wait_ge(S("a_acs"), g)
                    for t in range(TH):
                        last = mm(ps[:, t // 2, (t % 2) * DM:(t % 2 + 1) * DM], ACs[:, t * P:(t + 1) * P], wvo[:, i - 1, :],
                                  start=i == 1 and t % 2 == 0, stop=i == HEADS, skip_group_check=True)
                    if i < HEADS:
                        last.then_inc(S("a_out"), 1)
            last.then_inc(S("pe_step"), 1)

        def ffn(k, l, h):
            wg, wu, wd, wr, sel, ne = {1: (f1g, f1u, f1d, f1r, sel1, E1 + 1), 2: (w1t, w3t, w2t, None, None, 0),
                                       3: (f3g, f3u, f3d, f3r, sel3, E3)}[l]
            J = NJ[l]
            f = f"f{l}_"
            product = f + ("m" if l == 2 else "h")
            loaded(pe, *{1: ("f1g", "f1u", "f1d", "f1r", "sel1"), 2: ("w1t", "w3t"), 3: ("f3g", "f3u", "f3d", "f3r", "sel3")}[l])
            transpose_norm(h, (f"F{l}", h))
            if wr is not None:
                for t in range(TH):
                    for c in range(KC):
                        last = mm(ps[:, 7, t * 32:t * 32 + ne], xnT[:, c, t * P:(t + 1) * P], wr[:, c, :],
                                  start=c == 0, stop=c == KC - 1)
                last.then_inc(S(f + "logits"), 1)
            for j in range(J + 2):
                g = h * J + j
                if j < J:
                    m = min(P, WIDTH[l] - j * P)
                    if j >= 2:
                        pe.wait_ge(S(f + "sg"), g - 1)
                        pe.wait_ge(S(f + "m"), g - 1)
                    for b, w in ((0, wg), (1, wu)):
                        for c in range(KC):
                            last = mm(ps[0:m, 2 + 2 * (j % 2) + b, :], w[:, c, j * P:j * P + m], xnT[:, c, :],
                                      start=c == 0, stop=c == KC - 1)
                    last.then_inc(S(f + "gu"), 1)
                if wr is not None and j == 1:
                    pe.wait_ge(S(f + "cmb"), h + 1)
                    for t in range(TH):
                        last = nc.tensor.transpose(psb[0:96, 6, t * P:(t + 1) * P], cmb[:, t, :], identb[:, :])
                    last.then_inc(S(f + "cmbTp"), 1)
                    pe.wait_ge(S(f + "cmbT"), h + 1)
                if wr is not None and 1 <= j <= J:
                    i = j - 1
                    m = min(P, WIDTH[l] - i * P)
                    if i >= 2:
                        pe.wait_ge(S(f + "h"), h * J + i - 1)
                    mm(ps[0:m, 6 + i % 2, :], sel[:, i, 0:m], cmbT[:, :], start=True, stop=True).then_inc(S(f + "cw"), 1)
                if j >= 2:
                    i = j - 2
                    m = min(P, WIDTH[l] - i * P)
                    pe.wait_ge(S(product), h * J + i + 1)
                    for t in range(TH):
                        last = mm(ps[:, t // 2, (t % 2) * DM:(t % 2 + 1) * DM], hT[i % 2][0:m, t * P:(t + 1) * P], wd[0:m, i, :],
                                  start=i == 0 and t % 2 == 0, stop=i == J - 1, skip_group_check=True)
                    if i < J - 1:
                        last.then_inc(S(f + "down"), 1)
            last.then_inc(S("pe_step"), 1)

        def maps(k):
            loaded(pe, "m2q", "m2k", "m3q", "m3k", "w2t", "had")
            for j in range(I2 // P):
                if j % 2 == 0 and j >= 2:
                    pe.wait_ge(S("w2_mid"), j // 2)
                last = mm(ps[:, 7, (j % 2) * DM:(j % 2 + 1) * DM], had[:, :], w2t[:, j, :], start=True, stop=True)
                if j % 2:
                    last.then_inc(S("w2_had"), 1)
            n = 0
            for l in (2, 3):
                for w, bank in ((0, 0), (1, 2)):
                    if l == 3 and w == 0:
                        pe.wait_ge(S("am_copied"), 2)
                    for c in range(2):
                        last = mm(ps[:, bank + c, :], aw[l][w][:, :], ctxT[:, c * HALF:(c + 1) * HALF], start=True, stop=True)
                    last.then_inc(S("am_qk"), 1)
                pe.wait_ge(S("am_copied"), 2 * (l - 1))
                for t in range(NT):
                    b = t // 2
                    if n >= 2:
                        pe.wait_ge(S("am_exp"), n - 1)
                    mm(ps[:, 4 + n % 2, 0:DM], aq[:, t * P:(t + 1) * P], ak[:, b * DM:(b + 1) * DM],
                       start=True, stop=True).then_inc(S("am_s"), 1)
                    pe.wait_ge(S("am_pn"), n + 1)
                    if n:
                        pe.wait_ge(S("am_out"), n)
                    for kv in range(2):
                        last = nc.tensor.transpose(ps[:, 6, kv * P:(kv + 1) * P], aP[n % 2][:, kv * P:(kv + 1) * P], ident[:, :])
                    if n < 2 * NT - 1:
                        last.then_inc(S("am_t"), 1)
                    n += 1
            last.then_inc(S("pe_step"), 1)

        def attn_map(k, l, h):
            transpose_norm(h, (f"A{l}", h))
            am_ = attT if l == 2 else attT2
            for t in range(TH):
                for c in range(KC):
                    last = mm(ps[:, t // 2, (t % 2) * DM:(t % 2 + 1) * DM], xnT[:, c, t * P:(t + 1) * P],
                              am_[:, c, h, (t // 2) * DM:(t // 2 + 1) * DM], start=c == 0, stop=c == KC - 1)
            last.then_inc(S("pe_step"), 1)

        loaded(pe, "ident")
        for k, s in enumerate(ORDER):
            begin(pe, k)
            if s == "prep":
                prep(k)
            elif s == "maps":
                maps(k)
            else:
                b, h = s
                {"M": ssm, "F0": ffn0, "A1": attn1, "F1": lambda k, h: ffn(k, 1, h), "F2": lambda k, h: ffn(k, 2, h),
                 "F3": lambda k, h: ffn(k, 3, h), "A2": lambda k, h: attn_map(k, 2, h),
                 "A3": lambda k, h: attn_map(k, 3, h)}[b](k, h)

    @block.scalar
    def _(act):
        A = nc.scalar.activation
        link = chain(act, "act_chain")

        def copy(out_, in_):
            return A(out_, in_, ACT.Copy)

        def norm_T(s, banks=(2, 3)):
            act.wait_ge(S("xT_psum"), xt_index[s])
            for c in range(KC):
                last = copy(xnT[:, c, :], ps[:, banks[c], :])
            return last

        def prep(k):
            loaded(act, "small")
            A(tg[:, :], small[:, c_gate:c_gate + 8], ACT.Tanh).then_inc(S("tg_ready"), 1)
            link(A(negA[:, :, :], small[:, c_al:c_al + 32].rearrange("p (e n) -> p e n", e=2), ACT.Exp))
            link(A(negA[:, :, :], negA[:, :, :], ACT.Copy, scale=-1.0))
            for g in range(HEADS // 2):
                act.wait_ge(S("wvo_psum"), g + 1)
                copy(wvo[:, 2 * g:2 * g + 2, :].rearrange("p a d -> p (a d)"), ps[:, 2 + g % 4, :]).then_inc(S("wvo_copied"), 1)
            copy(mask_small[:, 0:8], tg[:, :]).then_inc(S("act_step"), 1)

        def ssm(k, h):
            act.wait_ge(S("ln_done"), ln_index[("M", h)])
            A(zs[:, :, :], xn[h][:, :, :], ACT.Silu)
            act.wait_ge(S("m_conv"), h + 1)
            for e in range(2):
                last = A(u[:, e, :], dlt[:, e, :], ACT.Silu, bias=small[:, c_cb + e:c_cb + e + 1])
            last.then_inc(S("m_u"), 1)
            act.wait_ge(S("m_xs"), h + 1)
            link(A(dA[0][:, :, :], dlt[:, :, :], ACT.Abs))
            A(dA[1][:, :, :], dA[0][:, :, :], ACT.Exp, scale=-1.0).then_inc(S("m_ex"), 1)
            act.wait_ge(S("m_w"), h + 1)
            link(A(hC[0][:, :, :], dBu[0][:, :, :], ACT.Ln))
            A(hC[1][:, :, :], hC[0][:, :, :], ACT.Exp, scale=-1.0).then_inc(S("m_lnw"), 1)
            act.wait_ge(S("m_du"), h + 1)
            for n in range(NS):
                g = h * NS + n
                if n >= 2:
                    act.wait_ge(S("m_h"), g - 1)
                for e in range(2):
                    last = A(dA[n % 2][:, e, :].rearrange("p (b l) -> p b l", b=2)[:, :, 1:DM],
                             dlt[:, e, :].rearrange("p (b l) -> p b l", b=2)[:, :, 1:DM],
                             ACT.Exp, scale=negA[:, e, n:n + 1])
                last.then_inc(S("m_dA"), 1)
                act.wait_ge(S("m_BC"), g + 1)
                if n >= 2:
                    act.wait_ge(S("m_dBu"), g - 1)
                copy(Bs[n % 2][:, :], ps[:, 2 + n % 2, :]).then_inc(S("m_Bcopy"), 1)
            copy(mask_small[:, 0:8], tg[:, :]).then_inc(S("act_step"), 1)

        def ffn0(k, h):
            act.wait_ge(S("q_xTp"), h + 1)
            copy(xqT[:, :, :].rearrange("p c t -> p (c t)"), psb[:, 2, :]).then_inc(S("q_xT"), 1)
            for t in range(TH + 1):
                g = h * TH + t
                if t < TH:
                    act.wait_ge(S("q_gate"), g + 1)
                    act.wait_ge(S("q_s"), h + 1)
                    if g >= 2:
                        act.wait_ge(S("q_h"), g - 1)
                    A(sg0[g % 2][:, :], ps[:, 3:5, :].rearrange("p a n -> p (a n)"), ACT.Silu,
                      scale=qs[:, t:t + 1]).then_inc(S("q_sg"), 1)
                if t:
                    act.wait_ge(S("q_hTp"), g)
                    if g > 1:
                        act.wait_ge(S("q_down"), g - 1)
                    copy(hqT[:, :, :].rearrange("p j t -> p (j t)"), psb[:, 7, :]).then_inc(S("q_hT"), 1)
            copy(mask_small[:, 0:8], tg[:, :]).then_inc(S("act_step"), 1)

        def attn1(k, h):
            norm_T(("A1", h), (6, 7)).then_inc(S("xT_ready"), 1)
            for i in range(HEADS + 1):
                g = h * HEADS + i
                if i < HEADS:
                    act.wait_ge(S("a_q"), g + 1)
                    if i:
                        act.wait_ge(S("a_s"), g)
                        act.wait_ge(S("a_qsq"), g)
                    copy(qT[:, :], ps[:, 6, :]).then_inc(S("a_qs"), 1)
                    act.wait_ge(S("a_kn"), g + 1)
                    if i:
                        act.wait_ge(S("a_khat"), g)
                    link(A(rkl[:, :], ps[:, 7, :], ACT.Ln, bias=epsc[:, :], scale=1.0 / P))
                    A(rk[:, :], rkl[:, :], ACT.Exp, scale=-0.5).then_inc(S("a_rk"), 1)
                    act.wait_ge(S("a_qn"), g + 1)
                    if i:
                        act.wait_ge(S("a_nb"), g)
                    link(A(rql[:, :], ps[:, 6, 0:TH], ACT.Ln, bias=epsc[:, :], scale=1.0 / P))
                    link_n = A(rq[:, :], rql[:, :], ACT.Exp, scale=-0.5)
                    link_n.then_inc(S("a_rq"), 1)
                if i:
                    act.wait_ge(S("a_ac"), g)
                    if i > 1:
                        act.wait_ge(S("a_out"), (HEADS - 1) * h + i - 1)
                    copy(ACs[:, :], ps[:, 4, :]).then_inc(S("a_acs"), 1)
                if i < HEADS:
                    act.wait_ge(S("a_nb"), g + 1)
                    if i:
                        act.wait_ge(S("a_pt"), g)
                        act.wait_ge(S("a_pn"), g)
                    for t in range(TH):
                        last = A(Pm[:, t, :], ps[:, 2 + t // 2, (t % 2) * DM:(t % 2 + 1) * DM], ACT.Exp,
                                 bias=nb[:, t:t + 1], scale=rq[:, t:t + 1], accum_out=rs[:, t:t + 1])
                    last.then_inc(S("a_exp"), 1)
            copy(mask_small[:, 0:8], tg[:, :]).then_inc(S("act_step"), 1)

        def ffn(k, l, h):
            f = f"f{l}_"
            J = NJ[l]
            norm_T((f"F{l}", h)).then_inc(S("xT_ready"), 1)
            if l != 2:
                e = E1 if l == 1 else E3
                act.wait_ge(S(f + "shift"), h + 1)
                A(rp[:, :, 0:e], rw[:, :, 0:e], ACT.Exp)
                if l == 1:
                    A(rc[:, 3, :], rl[:, :, e], ACT.Exp, scale=-1.0)
                copy(mask_small[:, 0:8], tg[:, :]).then_inc(S(f + "ex"), 1)
            for j in range(J):
                g = h * J + j
                m = min(P, WIDTH[l] - j * P)
                act.wait_ge(S(f + "gu"), g + 1)
                if j >= 2:
                    act.wait_ge(S(f + "m"), g - 1)
                A(sg[j % 2][0:m, :], ps[0:m, 2 + 2 * (j % 2), :], ACT.Silu).then_inc(S(f + "sg"), 1)
            copy(mask_small[:, 0:8], tg[:, :]).then_inc(S("act_step"), 1)

        def maps(k):
            for n in range(4):
                act.wait_ge(S("am_qk"), n + 1)
                l, w = 2 + n // 2, n % 2
                if n >= 2:
                    act.wait_ge(S("am_s"), NT)
                A((aq, ak)[w][:, :], ps[:, 2 * w:2 * w + 2, :].rearrange("p a n -> p (a n)"), ACT.Identity,
                  bias=small[:, c_b + 2 * (l - 2) + w:c_b + 2 * (l - 2) + w + 1]).then_inc(S("am_copied"), 1)
                if w == 0:
                    continue
                for i in range(NT):
                    m = (l - 2) * NT + i
                    act.wait_ge(S("am_nb"), m + 1)
                    if m >= 2:
                        act.wait_ge(S("am_t"), m - 1)
                    A(aP[m % 2][:, :], ps[:, 4 + m % 2, 0:DM], ACT.Exp, bias=am[:, 1:2], accum_out=am[:, 2:3]).then_inc(S("am_exp"), 1)
            copy(mask_small[:, 0:8], tg[:, :]).then_inc(S("act_step"), 1)

        def attn_map(k, l, h):
            norm_T((f"A{l}", h)).then_inc(S("xT_ready"), 1)
            copy(mask_small[:, 0:8], tg[:, :]).then_inc(S("act_step"), 1)

        for k, s in enumerate(ORDER):
            begin(act, k)
            if s == "prep":
                prep(k)
            elif s == "maps":
                maps(k)
            else:
                b, h = s
                {"M": ssm, "F0": ffn0, "A1": attn1, "F1": lambda k, h: ffn(k, 1, h), "F2": lambda k, h: ffn(k, 2, h),
                 "F3": lambda k, h: ffn(k, 3, h), "A2": lambda k, h: attn_map(k, 2, h),
                 "A3": lambda k, h: attn_map(k, 3, h)}[b](k, h)

    @block.vector
    def _(dve):
        V = nc.vector
        link = chain(dve, "dve_chain")
        n_tail = [0]

        def tail(h):
            n_tail[0] += 1
            for t in range(TH):
                last = V.bn_stats(bst[:, t, :], x[:, h * TH + t, :])
            link(last)
            for t in range(TH):
                last = V.bn_aggr(mv[:, t, :], bst[:, t, :])
            link(last)
            V.tensor_scalar(ve[:, :], mv[:, :, 1], EPS, None, ALU.add).then_inc(S("ln_var"), 1)
            dve.wait_ge(S("ln_rstd"), n_tail[0])
            for t in range(TH):
                last = V.tensor_scalar(xn[h][:, t, :], x[:, h * TH + t, :], mv[:, t, 0:1], rstd[:, t:t + 1],
                                       ALU.subtract, ALU.mult)
            last.then_inc(S("ln_done"), 1)

        def residual(s, h, k, bank=0):
            dve.wait_ge(S("pe_step"), k + 1)
            xv = x[:, h * TH:(h + 1) * TH, :].rearrange("p t d -> p (t d)")
            c = gate_col[s]
            link(V.scalar_tensor_tensor(xv, ps[:, bank:bank + 2, :].rearrange("p a n -> p (a n)"), tg[:, c:c + 1], xv, ALU.mult, ALU.add))

        def done(s, h, k):
            V.tensor_copy(mask_small[:, 8:9], epsc[:, :]).then_inc(S("dve_step"), 1)
            dve.wait_ge(S("act_step"), k + 1)
            if s != "F3":
                tail(h)

        def prep(k):
            V.memset(ones[:, :], 1.0).then_inc(S("ones_set"), 1)
            V.memset(epsc[:, :], EPS)
            V.memset(mhalf[:, :], -0.5).then_inc(S("mhalf_set"), 1)
            loaded(dve, "w0raw")
            for i in range(3):
                last = V.tensor_reduce(wabs[:, i:i + 1], w0raw[:, i, :], AX, ALU.add, apply_absolute_value=True)
            last.then_inc(S("wabs_part"), 1)
            loaded(dve, "x")
            tail(0)
            tail(1)
            dve.wait_ge(S("wabs_sum"), 1)
            link(V.tensor_scalar(wscale[:, :], ps[:, 0, 0:3], 1.0 / (DM * I0), EPS, ALU.mult, ALU.add))
            link(V.reciprocal(winv[:, :], wscale[:, :]))
            for i in range(3):
                link(V.tensor_scalar(wtmp[:, 0, :], w0raw[:, i, :], winv[:, i:i + 1], MAGIC, ALU.mult, ALU.add))
                link(V.tensor_scalar(wtmp[:, 1, :], wtmp[:, 0, :], MAGIC, 1.0, ALU.subtract, ALU.min))
                link(V.tensor_scalar(w0q[i][:, :], wtmp[:, 1, :], -1.0, None, ALU.max))
            loaded(dve, "small")
            link(V.tensor_scalar(gqk[:, :], small[:, c_gq:c_gq + 1], small[:, c_gk:c_gk + 1], SCALE, ALU.mult, ALU.mult))
            V.tensor_copy(mask_small[:, 8:9], epsc[:, :]).then_inc(S("dve_step"), 1)

        def ssm(k, h):
            if h == 0:
                V.memset(xpad[:, :, :, 0:3], 0.0)
            for i in range(2):
                pass
            dve.wait_ge(S("m_x"), h + 1)
            for e in range(2):
                last = V.tensor_copy(xpad[:, e, :, 3:DM + 3], ps[:, e, :].rearrange("p (b l) -> p b l", b=2))
            link(last)
            for e in range(2):
                for c in range(4):
                    w = small[:, c_cw + 4 * e + c:c_cw + 4 * e + c + 1]
                    src = xpad[:, e, :, c:c + DM]
                    dst = (dA[0], dlt)[c % 2][:, e, :].rearrange("p (b l) -> p b l", b=2)
                    prev = (dA[0], dlt)[(c + 1) % 2][:, e, :].rearrange("p (b l) -> p b l", b=2)
                    if c == 0:
                        link(V.tensor_scalar(dst, src, w, None, ALU.mult))
                    elif c < 3 or e == 0:
                        link(V.scalar_tensor_tensor(dst, src, w, prev, ALU.mult, ALU.add))
                    else:
                        V.scalar_tensor_tensor(dst, src, w, prev, ALU.mult, ALU.add).then_inc(S("m_conv"), 1)
            dve.wait_ge(S("m_dbl"), h + 1)
            V.tensor_copy(dts[:, :], ps[0:8, 3, :]).then_inc(S("m_dts"), 1)
            r1, r2 = dBu[1][0:96, 0, :], dBu[1][0:96, 1, :]
            p1, p2 = Bs[0][0:96, 0:256].bitcast(bf16), Bs[0][0:96, 256:512].bitcast(bf16)
            link(V.tensor_copy(p1, ps[0:96, 2, :]))
            link(V.tensor_tensor(r1, ps[0:96, 2, :], p1, ALU.subtract))
            link(V.tensor_copy(p2, r1))
            link(V.tensor_tensor(r2, r1, p2, ALU.subtract))
            V.tensor_copy(bcs[0:32, :], p1[0:32, :])
            V.tensor_copy(bcs[32:64, :], p2[32:64, :])
            V.tensor_copy(bcs[64:96, :], r2[64:96, :]).then_inc(S("m_bcs"), 1)
            dve.wait_ge(S("m_dpre"), h + 1)
            for e in range(2):
                last = V.tensor_scalar(dlt[:, e, :], ps[:, e, :], small[:, c_dtb + e:c_dtb + e + 1], None, ALU.add)
            last.then_inc(S("m_xs"), 1)
            dve.wait_ge(S("m_ex"), h + 1)
            V.tensor_scalar(dBu[0][:, :, :], dA[1][:, :, :], 1.0, None, ALU.add).then_inc(S("m_w"), 1)
            dve.wait_ge(S("m_w"), h + 1)
            link(V.scalar_tensor_tensor(du[:, :, :], dBu[0][:, :, :], 1.0, dA[1][:, :, :], ALU.subtract, ALU.subtract))
            dve.wait_ge(S("m_lnw"), h + 1)
            link(V.tensor_tensor(du[:, :, :], du[:, :, :], hC[1][:, :, :], ALU.mult))
            link(V.scalar_tensor_tensor(dlt[:, :, :], dlt[:, :, :], 0.0, hC[0][:, :, :], ALU.max, ALU.add))
            link(V.tensor_tensor(dlt[:, :, :], dlt[:, :, :], du[:, :, :], ALU.subtract))
            for i in range(2):
                V.memset(dA[i][:, :, :].rearrange("p e (b l) -> p (e b) l", b=2)[:, :, 0:1], 0.0)
            V.tensor_tensor(du[:, :, :], dlt[:, :, :], u[:, :, :], ALU.mult).then_inc(S("m_du"), 1)
            for n in range(NS):
                g = h * NS + n
                dve.wait_ge(S("m_dA"), g + 1)
                dve.wait_ge(S("m_dBu"), g + 1)
                if n:
                    dve.wait_ge(S("m_hC"), g)
                flat = "p e t -> p (e t)"
                V.tensor_tensor_scan(hst[:, :, :].rearrange(flat), dA[n % 2][:, :, :].rearrange(flat),
                                     dBu[n % 2][:, :, :].rearrange(flat), 0.0, ALU.mult, ALU.add).then_inc(S("m_h"), 1)
                dve.wait_ge(S("m_h"), g + 1)
                if n >= 2:
                    dve.wait_ge(S("m_y"), g - 1)
                V.tensor_tensor(hC[n % 2][:, :, :], hst[:, :, :], bc(ps[:, 4 + n % 2, :].unsqueeze(1), [P, 2, HALF]),
                                ALU.mult).then_inc(S("m_hC"), 1)
            dve.wait_ge(S("m_y"), (h + 1) * NS)
            for e in range(2):
                last = V.scalar_tensor_tensor(dlt[:, e, :], u[:, e, :], small[:, c_D + e:c_D + e + 1], ps[:, e, :], ALU.mult, ALU.add)
            link(last)
            for e in range(2):
                last = V.tensor_tensor(u[:, e, :].rearrange("p (b l) -> p b l", b=2), dlt[:, e, :].rearrange("p (b l) -> p b l", b=2),
                                       zs[:, :, :].rearrange("p (b e) l -> p e b l", e=2)[:, e], ALU.mult)
            last.then_inc(S("m_yz"), 1)
            residual("M", h, k, 6)
            done("M", h, k)

        def ffn0(k, h):
            x_h = xn[h]
            am_, s_, r_, su = qs[:, 4:8], qs[:, 8:12], qs[:, 12:16], qs[:, 16:20]
            dve.wait_ge(S("ln_done"), ln_index[("F0", h)])
            link(V.tensor_reduce(am_, x_h[:, :, :], AX, ALU.max, apply_absolute_value=True))
            link(V.tensor_scalar(s_, am_, 1.0 / 127.0, EPS, ALU.mult, ALU.add))
            link(V.reciprocal(r_, s_))
            V.tensor_scalar(qs[:, 0:4], s_, wscale[:, 0:1], None, ALU.mult).then_inc(S("q_s"), 1)
            V.tensor_scalar(su, s_, wscale[:, 1:2], None, ALU.mult)
            for t in range(TH):
                last = V.tensor_scalar(xqa[:, t, :], x_h[:, t, :], qs[:, 12 + t:13 + t], MAGIC, ALU.mult, ALU.add)
            link(last)
            link(V.tensor_scalar(xqa[:, :, :], xqa[:, :, :], MAGIC, 127.0, ALU.subtract, ALU.min))
            V.tensor_scalar(xq[:, :, :], xqa[:, :, :], -128.0, None, ALU.max).then_inc(S("q_xq"), 1)
            def out(t):
                g = h * TH + t
                dve.wait_ge(S("q_down"), g + 1)
                xv = x[:, g, :]
                V.scalar_tensor_tensor(xv, ps[:, t % 2, 0:DM], qs[:, 20 + t:21 + t], xv, ALU.mult, ALU.add).then_inc(S("q_out"), 1)
            for t in range(TH):
                g = h * TH + t
                dve.wait_ge(S("q_up"), g + 1)
                dve.wait_ge(S("q_sg"), g + 1)
                V.scalar_tensor_tensor(h0[:, :], ps[:, 5:7, :].rearrange("p a n -> p (a n)"), qs[:, 16 + t:17 + t],
                                       sg0[g % 2][:, :], ALU.mult, ALU.mult).then_inc(S("q_h"), 1)
                dve.wait_ge(S("q_h"), g + 1)
                link(V.tensor_reduce(qt[:, 0:1], h0[:, :], AX, ALU.max, apply_absolute_value=True))
                link(V.tensor_scalar(qt[:, 1:2], qt[:, 0:1], 1.0 / 127.0, EPS, ALU.mult, ALU.add))
                link(V.reciprocal(qt[:, 2:3], qt[:, 1:2]))
                V.tensor_scalar(qs[:, 20 + t:21 + t], qt[:, 1:2], wscale[:, 2:3], tg[:, gate_col["F0"]:gate_col["F0"] + 1], ALU.mult, ALU.mult)
                link(V.tensor_scalar(h0a[:, :], h0[:, :], qt[:, 2:3], MAGIC, ALU.mult, ALU.add))
                link(V.tensor_scalar(h0a[:, :], h0a[:, :], MAGIC, 127.0, ALU.subtract, ALU.min))
                if g:
                    dve.wait_ge(S("q_hTp"), g)
                V.tensor_scalar(hq[:, :], h0a[:, :], -128.0, None, ALU.max).then_inc(S("q_hq"), 1)
                if t:
                    out(t - 1)
            out(TH - 1)
            dve.wait_ge(S("q_out"), (h + 1) * TH)
            dve.wait_ge(S("pe_step"), k + 1)
            done("F0", h, k)

        def attn1(k, h):
            for i in range(HEADS + 1):
                g = h * HEADS + i
                if i < HEADS:
                    dve.wait_ge(S("a_k"), g + 1)
                    if i:
                        dve.wait_ge(S("a_ksq"), g)
                        dve.wait_ge(S("a_khat"), g)
                    V.tensor_copy(kT[:, :], ps[:, 7, :]).then_inc(S("a_ks"), 1)
                if i:
                    dve.wait_ge(S("a_pt"), g)
                    if i > 1:
                        dve.wait_ge(S("a_ac"), g - 1)
                    V.tensor_copy(PT[:, :, :], ps[:, 4:6, :]).then_inc(S("a_pts"), 1)
                if i < HEADS:
                    dve.wait_ge(S("a_rk"), g + 1)
                    if i:
                        dve.wait_ge(S("a_s"), g)
                    dve.wait_ge(S("a_ks"), g + 1)
                    V.scalar_tensor_tensor(khat[:, :], kT[:, :], gqk[:, :], rk[:, :], ALU.mult, ALU.mult).then_inc(S("a_khat"), 1)
                    dve.wait_ge(S("a_s"), g + 1)
                    link(V.tensor_reduce(mx[:, :], ps[:, 2:4, :].rearrange("p a (b n) -> p (a b) n", b=2), AX, ALU.max))
                    dve.wait_ge(S("a_rq"), g + 1)
                    V.scalar_tensor_tensor(nb[:, :], mx[:, :], -1.0, rq[:, :], ALU.mult, ALU.mult).then_inc(S("a_nb"), 1)
                    dve.wait_ge(S("a_exp"), g + 1)
                    link(V.reciprocal(ri[:, :], rs[:, :]))
                    V.tensor_tensor(Pm[:, :, :], Pm[:, :, :], bc(ri[:, :].unsqueeze(2), [P, TH, DM]), ALU.mult).then_inc(S("a_pn"), 1)
            residual("A1", h, k)
            done("A1", h, k)

        def router(l, h):
            f = f"f{l}_"
            e, top = (E1, TOP1) if l == 1 else (E3, TOP3)
            n = e + 1
            dve.wait_ge(S(f + "logits"), h + 1)
            nl = e + 1 if l == 1 else e
            link(V.tensor_copy(rl[:, :, 0:nl], ps[:, 7, 0:TH * 32].rearrange("p (t n) -> p t n", t=TH)[:, :, 0:nl]))
            V.memset(rp[:, :, e:24], -1.0)
            link(V.tensor_reduce(rc[:, 0, :], rl[:, :, 0:e], AX, ALU.max))
            V.tensor_tensor(rw[:, :, 0:e], rl[:, :, 0:e], bc(rc[:, 0, :].unsqueeze(2), [P, TH, e]), ALU.subtract).then_inc(S(f + "shift"), 1)
            dve.wait_ge(S(f + "ex"), h + 1)
            link(V.tensor_reduce(rc[:, 1, :], rp[:, :, 0:e], AX, ALU.add))
            link(V.reciprocal(rc[:, 1, :], rc[:, 1, :]))
            link(V.tensor_tensor(rp[:, :, 0:e], rp[:, :, 0:e], bc(rc[:, 1, :].unsqueeze(2), [P, TH, e]), ALU.mult))
            for t in range(TH):
                last = V.max(rt[:, t, :], rp[:, t, 0:e])
            link(last)
            link(V.memset(rt[:, :, top:8], -1.0))
            for t in range(TH):
                last = V.match_replace(rr[:, t, :], rt[:, t, :], rp[:, t, :], 0.0)
            link(last)
            link(V.tensor_tensor(rw[:, :, 0:e], rp[:, :, 0:e], rr[:, :, 0:e], ALU.subtract))
            if l == 1:
                link(V.tensor_reduce(rc[:, 2, :], rw[:, :, 0:e], AX, ALU.add))
                link(V.reciprocal(rc[:, 2, :], rc[:, 2, :]))
                link(V.tensor_tensor(rw[:, :, 0:e], rw[:, :, 0:e], bc(rc[:, 2, :].unsqueeze(2), [P, TH, e]), ALU.mult))
                link(V.tensor_scalar(rc[:, 3, :], rc[:, 3, :], 1.0, None, ALU.add))
                link(V.reciprocal(rw[:, :, e], rc[:, 3, :]))
            else:
                link(V.memset(rw[:, :, e:n], 1.0))
            link(V.memset(cmb[:, :, :], 0.0))
            link(V.tensor_copy(cmb[:, :, 0:n], rw[:, :, 0:n]))
            link(V.tensor_tensor(rr2[:, :, 0:n], rw[:, :, 0:n], cmb[:, :, 0:n], ALU.subtract))
            link(V.tensor_copy(cmb[:, :, 32:32 + n], rr2[:, :, 0:n]))
            V.tensor_tensor(cmb[:, :, 64:64 + n], rr2[:, :, 0:n], cmb[:, :, 32:32 + n], ALU.subtract).then_inc(S(f + "cmb"), 1)

        def ffn(k, l, h):
            f = f"f{l}_"
            J = NJ[l]
            routed = l != 2
            if routed:
                router(l, h)
            for j in range(J):
                g = h * J + j
                m = min(P, WIDTH[l] - j * P)
                dve.wait_ge(S(f + "sg"), g + 1)
                if not routed and j >= 2:
                    dve.wait_ge(S(f + "down"), (J - 1) * h + j - 1)
                if not routed:
                    V.tensor_tensor(hT[j % 2][0:m, :], sg[j % 2][0:m, :], ps[0:m, 3 + 2 * (j % 2), :], ALU.mult).then_inc(S(f + "m"), 1)
                    continue
                V.tensor_tensor(gu[j % 2][0:m, :], sg[j % 2][0:m, :], ps[0:m, 3 + 2 * (j % 2), :], ALU.mult).then_inc(S(f + "m"), 1)
                if j == 0:
                    dve.wait_ge(S(f + "cmbTp"), h + 1)
                    V.tensor_copy(cmbT[:, :], psb[0:96, 6, 0:HALF]).then_inc(S(f + "cmbT"), 1)
                dve.wait_ge(S(f + "m"), g + 1)
                dve.wait_ge(S(f + "cw"), g + 1)
                if j >= 2:
                    dve.wait_ge(S(f + "down"), (J - 1) * h + j - 1)
                V.tensor_tensor(hT[j % 2][0:m, :], gu[j % 2][0:m, :], ps[0:m, 6 + j % 2, :], ALU.mult).then_inc(S(f + "h"), 1)
            residual(f"F{l}", h, k)
            if l == 3:
                V.tensor_copy(mask_small[:, 10:11], epsc[:, :]).then_inc(S("x_final"), 1)
            done(f"F{l}", h, k)

        def maps(k):
            flat = "p j d -> p (j d)"
            for j in range(0, I2 // P, 2):
                dve.wait_ge(S("w2_had"), j // 2 + 1)
                V.tensor_scalar(wmix[0][:, j:j + 2, :].rearrange(flat), ps[:, 7, :], float(I2) ** -0.5, None, ALU.mult).then_inc(S("w2_mid"), 1)
            dve.wait_ge(S("w2_mid"), I2 // P // 2)
            src, dst = wmix[0], w2t
            for st in (1, 2, 4):
                a = src[:, :, :].rearrange("p (g two s) d -> p g two (s d)", two=2, s=st)
                o = dst[:, :, :].rearrange("p (g two s) d -> p g two (s d)", two=2, s=st)
                V.tensor_tensor(o[:, :, 0, :], a[:, :, 0, :], a[:, :, 1, :], ALU.add)
                link(V.tensor_tensor(o[:, :, 1, :], a[:, :, 0, :], a[:, :, 1, :], ALU.subtract))
                src, dst = dst, src
            for m in range(2 * NT):
                l, t = m // NT, m % NT
                dve.wait_ge(S("am_s"), m + 1)
                if m:
                    dve.wait_ge(S("am_exp"), m)
                link(V.tensor_reduce(am[:, 0:1], ps[:, 4 + m % 2, 0:DM], AX, ALU.max))
                V.tensor_scalar(am[:, 1:2], am[:, 0:1], -1.0, None, ALU.mult).then_inc(S("am_nb"), 1)
                dve.wait_ge(S("am_exp"), m + 1)
                link(V.reciprocal(am[:, 3:4], am[:, 2:3]))
                V.tensor_scalar(aP[m % 2][:, :], aP[m % 2][:, :], am[:, 3:4], None, ALU.mult).then_inc(S("am_pn"), 1)
                if m < 2 * NT - 1:
                    dve.wait_ge(S("am_t"), m + 1)
                else:
                    dve.wait_ge(S("pe_step"), k + 1)
                dst = attT if l == 0 else attT2
                V.tensor_copy(dst[:, :, t // 4, (t % 4) * P:(t % 4 + 1) * P],
                              ps[:, 6, 0:2 * P].rearrange("p (c m) -> p c m", c=2)).then_inc(S("am_out"), 1)
            V.tensor_copy(mask_small[:, 8:9], wmix[0][:, 0, 0:1]).then_inc(S("dve_step"), 1)

        def attn_map(k, l, h):
            residual(f"A{l}", h, k)
            done(f"A{l}", h, k)

        for k, s in enumerate(ORDER):
            begin(dve, k)
            if s == "prep":
                prep(k)
            elif s == "maps":
                maps(k)
            else:
                b, h = s
                {"M": ssm, "F0": ffn0, "A1": attn1, "F1": lambda k, h: ffn(k, 1, h), "F2": lambda k, h: ffn(k, 2, h),
                 "F3": lambda k, h: ffn(k, 3, h), "A2": lambda k, h: attn_map(k, 2, h),
                 "A3": lambda k, h: attn_map(k, 3, h)}[b](k, h)

    @block.gpsimd
    def _(pool):
        G = nc.gpsimd
        n_rstd = [0]

        def rstd_of():
            n_rstd[0] += 1
            pool.wait_ge(S("ln_var"), n_rstd[0])
            G.tensor_tensor(rstd[:, :], ve[:, :], mhalf[:, :], ALU.pow).then_inc(S("ln_rstd"), 1)

        pool.wait_ge(S("mhalf_set"), 1)
        rstd_of()
        rstd_of()
        for k, s in enumerate(ORDER):
            if s in ("prep", "maps"):
                continue
            b, h = s
            if b == "M":
                begin(pool, k)
                for n in range(NS):
                    g = h * NS + n
                    pool.wait_ge(S("m_Bcopy"), g + 1)
                    pool.wait_ge(S("m_du"), h + 1)
                    if n >= 2:
                        pool.wait_ge(S("m_h"), g - 1)
                    G.tensor_tensor(dBu[n % 2][:, :, :], du[:, :, :], bc(Bs[n % 2][:, :].unsqueeze(1), [P, 2, HALF]),
                                    ALU.mult).then_inc(S("m_dBu"), 1)
                pool.wait_ge(S("m_dBu"), (h + 1) * NS)
                G.tensor_copy(mask_small[:, 16:17], mhalf[:, 0:1]).then_inc(S("pool_step"), 1)
            elif b == "A1":
                begin(pool, k)
                for i in range(HEADS):
                    g = h * HEADS + i
                    pool.wait_ge(S("a_ks"), g + 1)
                    if i:
                        pool.wait_ge(S("a_kn"), g)
                    G.tensor_tensor(ksq[:, :], kT[:, :], kT[:, :], ALU.mult).then_inc(S("a_ksq"), 1)
                    pool.wait_ge(S("a_qs"), g + 1)
                    if i:
                        pool.wait_ge(S("a_qn"), g)
                    G.tensor_tensor(qsq[:, :], qT[:, :], qT[:, :], ALU.mult).then_inc(S("a_qsq"), 1)
                pool.wait_ge(S("a_qsq"), (h + 1) * HEADS)
                G.tensor_copy(mask_small[:, 16:17], mhalf[:, 0:1]).then_inc(S("pool_step"), 1)
            if b != "F3":
                rstd_of()

    stack.close()


def kernel(**inputs):
    import numpy as np
    import ml_dtypes
    import concourse.bacc as bacc
    from concourse import mybir
    from concourse.bass_utils import run_bass_kernel_spmd

    f = {k: np.asarray(v) for k, v in inputs.items()}
    P = 128

    def rows(w):
        return w.reshape(-1, P, w.shape[1]).transpose(1, 0, 2)

    def pad_rows(w):
        n = -(-w.shape[0] // P) * P
        return np.concatenate([w, np.zeros((n - w.shape[0], w.shape[1]), w.dtype)])

    x = f["x"].reshape(1024, 256)
    ctx = f["ctx_1024"].reshape(1024, 128)
    small = np.zeros((P, 64), np.float32)
    small[:, 0:4] = f["g_xattn"][None, :]
    small[:, 4:8] = f["g_ffn"][None, :]
    small[:, 8:16] = rows(f["L0_xattn_conv_w"]).reshape(P, 8)
    small[:, 16:18] = f["L0_xattn_conv_b"].reshape(2, P).T
    small[:, 18:20] = f["L0_xattn_dt_proj_b"].reshape(2, P).T
    small[:, 20:52] = rows(f["L0_xattn_A_log"]).reshape(P, 32)
    small[:, 52:54] = f["L0_xattn_D"].reshape(2, P).T
    for c, name in enumerate(["L1_xattn_gq", "L1_xattn_gk", "L2_xattn_bq", "L2_xattn_bk", "L3_xattn_bq", "L3_xattn_bk"]):
        small[:, 54 + c] = f[name]

    def selector(owner, width, parts, rows_=96):
        s = np.zeros((rows_, width), np.float32)
        for p in parts:
            s[p + owner, np.arange(width)] = 1.0
        return s.astype(ml_dtypes.bfloat16)

    def experts(e, fdim, shared_width):
        n = e * fdim + shared_width
        owner = np.minimum(np.arange(n) // fdim, e)
        full = -(-n // P) * P
        s = np.zeros((96, full), ml_dtypes.bfloat16)
        s[:, :n] = selector(owner, n, (0, 32, 64))
        return s.reshape(96, -1, P)

    bc_owner = np.repeat(np.arange(32), P)
    had = np.array([[1.0]], np.float32)
    while had.shape[0] < P:
        had = np.block([[had, had], [had, -had]])

    xp = f["L0_xattn_x_proj_w"]
    bcw = np.concatenate([xp[8:40]] * 3).T
    gu1, gu3 = f["L1_ffn_expert_gate_up"], f["L3_ffn_gate_up_weights"]
    s1, s3 = f["L1_ffn_shared_gate_up"], f["L3_ffn_shared_gate_up"]

    def side_by_side(gu, shared, part):
        w = gu.shape[1] // 2
        ws = shared.shape[0] // 2
        both = [gu[:, part * w:(part + 1) * w].reshape(-1, 256), shared[part * ws:(part + 1) * ws]]
        return rows(np.concatenate(both).T)

    def downs(d, shared):
        return rows(pad_rows(np.concatenate([d.transpose(0, 2, 1).reshape(-1, 256), shared.T])))

    arrays = {
        "x": rows(x), "ctk": rows(ctx), "ctxT": ctx.T, "small": small,
        "ident": np.eye(P, dtype=np.float32), "identb": np.eye(P, dtype=np.float32).astype(ml_dtypes.bfloat16),
        "had": had,
        "sel_bc": selector(bc_owner, 32 * P, (0, 32, 64)).reshape(96, 32, P),
        "sel1": experts(16, 176, 704), "sel3": experts(8, 176, 352),
        "w0raw": np.stack([rows(f["L0_ffn_w_gate"].T).reshape(P, -1), rows(f["L0_ffn_w_up"].T).reshape(P, -1),
                           rows(f["L0_ffn_w_down"].T).reshape(P, -1)], 1),
        "m_in": f["L0_xattn_in_proj_w"].T, "m_bc": rows(bcw), "m_dt": rows(xp[0:8].T), "m_dtw": f["L0_xattn_dt_proj_w"].T,
        "wq": rows(f["L1_xattn_Wq"]), "wk": f["L1_xattn_Wk"],
        "wvT": f["L1_xattn_Wv"].reshape(128, 16, 128).transpose(2, 1, 0), "wo": rows(f["L1_xattn_Wo"]),
        "f1g": side_by_side(gu1, s1, 0), "f1u": side_by_side(gu1, s1, 1),
        "f1d": downs(f["L1_ffn_expert_down"], f["L1_ffn_shared_down"]),
        "f1r": rows(np.concatenate([f["L1_ffn_gate_w"], f["L1_ffn_shared_gate_vec"]]).T),
        "m2q": f["L2_xattn_Wq"].T, "m2k": f["L2_xattn_Wk"].T, "m3q": f["L3_xattn_Wq"].T, "m3k": f["L3_xattn_Wk"].T,
        "w1t": rows(f["L2_ffn_W1"].T), "w3t": rows(f["L2_ffn_W3"].T), "w2t": rows(f["L2_ffn_W2"].T),
        "f3g": side_by_side(gu3, s3, 0), "f3u": side_by_side(gu3, s3, 1),
        "f3d": downs(f["L3_ffn_down_weights"], f["L3_ffn_shared_down"]),
        "f3r": rows(f["L3_ffn_gate_weight"].T),
    }
    nc = bacc.Bacc("TRN2", target_bir_lowering=False, num_devices=1)
    dram, given = {}, {}
    for name, a in arrays.items():
        a = np.ascontiguousarray(a)
        given["in_" + name] = a
        t = nc.dram_tensor("in_" + name, a.shape, mybir.dt.from_np(a.dtype), kind="ExternalInput").ap()
        dram[name] = t
    out = nc.dram_tensor("out_x", (P, 8, 256), mybir.dt.float32, kind="ExternalOutput").ap()
    flamingo_kernel(nc, dram, out)
    r = run_bass_kernel_spmd(nc, [given], core_ids=[0])
    return np.asarray(r.results[0]["out_x"]).transpose(1, 0, 2).reshape(4, 256, 256)
```

```python
def flamingo_kernel(nc, dram, out):
    import concourse.bass as bass
    from concourse import mybir
    from contextlib import ExitStack

    f32, bf16, f32r = mybir.dt.float32, mybir.dt.bfloat16, mybir.dt.float32r
    ALU, ACT = mybir.AluOpType, mybir.ActivationFunctionType
    AX = mybir.AxisListType.X

    P = 128
    DM, TOK, HALF = 256, 1024, 512
    NT, TH = TOK // P, HALF // P
    KC = DM // P
    NS = 16
    HEADS = 16
    I0, I2 = 1024, 1024
    E1, F1, TOP1 = 16, 176, 4
    E3, F3, TOP3 = 8, 176, 2
    I1, I3 = 20 * F1, 10 * F3
    NJ = {1: -(-I1 // P), 2: I2 // P, 3: -(-I3 // P)}
    GU, WJ = 2 * KC * P, 2 * KC * P + DM
    J1A = 22
    MAGIC = 1.5 * 2.0 ** 23
    EPS = 1e-5
    SCALE = float(P) ** -0.5

    at = {"fixed": -(-nc.sbuf_base // 64) * 64}
    limit = nc.sbuf_usable_end

    def place(region, name, shape, dt=f32):
        size = 2 if dt == bf16 else 4
        for n in shape[1:]:
            size *= n
        size = -(-size // 64) * 64
        t = nc.alloc_sbuf_tensor_at(name, shape, dt, offset=at[region])
        at[region] += size
        assert at[region] <= limit, (name, at[region], limit)
        return t

    x = place("fixed", "x_res", [P, NT, DM])
    xn = [place("fixed", f"x_norm{h}", [P, TH, DM]) for h in range(2)]
    xTh = place("fixed", "x_norm_T_hi", [P, KC, HALF], f32r)
    xTl = place("fixed", "x_norm_T_lo", [P, KC, HALF], f32r)
    ctxT = place("fixed", "ctx_T", [P, TOK])
    ctk = place("fixed", "ctx_tok", [P, NT, P])
    small = place("fixed", "small_params", [P, 64])
    ident = place("fixed", "ident_f", [P, P])
    identb = place("fixed", "ident_b", [P, P], bf16)
    had = place("fixed", "hadamard", [P, P])
    ones = place("fixed", "ones", [P, P])
    tg = place("fixed", "tanh_gates", [P, 8])
    negA = place("fixed", "neg_A", [P, 2, NS])
    wabs = place("fixed", "w_abs", [P, 3])
    wscale = place("fixed", "w_scale", [P, 3])
    winv = place("fixed", "w_inv", [P, 3])
    epsc = place("fixed", "eps_col", [P, 1])
    magic = place("fixed", "magic_col", [P, 1])
    mhalf = place("fixed", "minus_half", [P, TH])
    gqk = place("fixed", "g_qk", [P, 1])
    bst = place("fixed", "bn_st", [P, TH, 6])
    mv = place("fixed", "bn_mv", [P, TH, 2])
    ve = place("fixed", "var_eps", [P, TH])
    rstd = place("fixed", "rstd", [P, TH])
    mask_small = place("fixed", "scratch_small", [P, 64])
    mask_q = place("fixed", "q_scales", [P, 8 * TH])
    mask_q2 = place("fixed", "q_tile_scales", [P, 4])

    at["A1"] = at["A2"] = at["fixed"]
    wq = place("A1", "a1_wq", [P, KC, HEADS * P])
    wk = place("A1", "a1_wk", [P, HEADS * P])
    wvo = place("A1", "a1_wvo", [P, HEADS, DM])
    f2w = place("A2", "f2_w", [P, NJ[2], WJ])
    attT = {l: place("A2", f"att_T{l}", [P, KC, 2, HALF]) for l in (2, 3)}
    at["B"] = max(at["A1"], at["A2"])
    at["B0"] = at["B1"] = at["B3"] = at["B"]
    sel = {1: place("B1", "sel1", [96, NJ[1], P], bf16)}
    fr = {1: place("B1", "f1_router", [P, KC, 32])}
    f1a = place("B1", "f1_wa", [P, J1A, WJ])
    at["B1a"] = at["B1"]
    f1b = place("B1", "f1_wb", [P, NJ[1] - J1A, WJ])
    f3w = place("B3", "f3_w", [P, NJ[3], WJ])
    sel[3] = place("B3", "sel3", [96, NJ[3], P], bf16)
    fr[3] = place("B3", "f3_router", [P, KC, 32])
    w0raw = place("B0", "w0_raw", [P, 3, KC * I0])
    at["Bp"] = at["Bm"] = at["Bf"] = at["B0"]
    xpad = place("Bm", "m_xpad", [P, 2, 2, DM + 3])
    u = place("Bm", "m_u", [P, 2, HALF])
    dlt = place("Bm", "m_delta", [P, 2, HALF])
    du = place("Bm", "m_du", [P, 2, HALF])
    zs = place("Bm", "m_z", [P, TH, DM])
    dA = [place("Bm", f"m_dA{i}", [P, 2, HALF]) for i in range(2)]
    dBu = [place("Bm", f"m_dBu{i}", [P, 2, HALF]) for i in range(2)]
    Bs = [place("Bm", f"m_Bs{i}", [P, HALF]) for i in range(2)]
    hst = place("Bm", "m_h", [P, 2, HALF])
    hC = [place("Bm", f"m_hC{i}", [P, 2, HALF]) for i in range(2)]
    bcs = place("Bm", "m_bc_split", [96, HALF], bf16)
    dts = place("Bm", "m_dt", [8, HALF])
    m_in = place("Bm", "m_in_w", [P, DM])
    m_bc = place("Bm", "m_bc_w", [P, 2, 96])
    m_dt = place("Bm", "m_dt_w", [P, 2, 8])
    m_dtw = place("Bm", "m_dtw", [8, DM])
    xq = place("Bf", "q_x", [P, TH, DM], bf16)
    xqa = place("Bf", "q_xa", [P, TH, DM])
    xqT = place("Bf", "q_xT", [P, KC, HALF], bf16)
    sg0 = [place("Bf", f"q_sg{i}", [P, I0]) for i in range(2)]
    h0 = place("Bf", "q_h", [P, I0])
    h0a = place("Bf", "q_ha", [P, I0])
    hq = place("Bf", "q_hq", [P, I0], bf16)
    hqT = place("Bf", "q_hqT", [P, I0 // P, P], bf16)
    wtmp = place("Bf", "w_tmp", [P, 2, KC * I0])
    at["W"] = max(at["B1"], at["B3"], at["Bm"], at["Bf"])
    at["W0"] = at["Wd"] = at["W1"] = at["W2"] = at["W4"] = at["W"]
    w0q = [place("W0", f"w0_quant{i}", [P, KC * I0], bf16) for i in range(3)]
    w_values = place("Wd", "w_abs_values", [P, KC * I0])
    wvT = place("W0", "a1_wvT", [P, HEADS // 2, P])
    sel_bc = place("W0", "sel_bc", [96, 2 * NS, P], bf16)
    wo = place("W0", "a1_wo", [P, HEADS // 2, DM])
    Pm = [place("W1", f"a_P{i}", [P, TH, DM]) for i in range(2)]
    PT = place("W1", "a_PT", [P, 2, HALF])
    qh, ql = ([place("W1", f"a_qT_{n}{i}", [P, HALF], f32r) for i in range(2)] for n in ("hi", "lo"))
    kh, kl = (place("W1", f"a_kT_{n}", [P, HALF], f32r) for n in ("hi", "lo"))
    ah, al = (place("W1", f"a_AC_{n}", [P, HALF], f32r) for n in ("hi", "lo"))
    qsq = place("W1", "a_qsq", [P, HALF])
    ksq = place("W1", "a_ksq", [P, HALF])
    ktok = place("W1", "a_k_tok", [P, HALF])
    rk, rks, rqs, nb, mx, rs, ri = (place("W1", f"a_{n}", [P, TH]) for n in
                                    ("rk", "k_sum", "q_sum", "neg_max", "max", "row_sum", "row_inv"))
    rq = [place("W1", f"a_rq{i}", [P, TH]) for i in range(2)]
    ch, cl = (place("B1a", f"a_ctxT_{n}", [P, HALF], f32r) for n in ("hi", "lo"))
    AQ = KC * P + P
    awh, awl = ([place("B1a", f"a_w_{n}{i}", [P, AQ], f32r) for i in range(2)] for n in ("hi", "lo"))
    voh, vol = ([place("B1a", f"a_wvo_{n}{i}", [P, DM], f32r) for i in range(2)] for n in ("hi", "lo"))
    assert at["B1a"] <= at["B1"]
    sg = [place("W2", f"f_silu{i}", [P, HALF]) for i in range(2)]
    hh, hl = ([place("W2", f"f_h_{n}{i}", [P, HALF], f32r) for i in range(2)] for n in ("hi", "lo"))
    wgh, wgl = ([place("W2", f"f_wgu_{n}{i}", [P, GU], f32r) for i in range(2)] for n in ("hi", "lo"))
    wdh, wdl = ([place("W2", f"f_wd_{n}{i}", [P, DM], f32r) for i in range(3)] for n in ("hi", "lo"))
    wrh, wrl = (place("W2", f"r_w_{n}", [P, KC, 32], f32r) for n in ("hi", "lo"))
    cmb = place("W2", "r_combine", [P, TH, 96], bf16)
    cmbT = place("W2", "r_combine_T", [96, HALF], bf16)
    rl = place("W2", "r_logits", [P, TH, 24])
    rp = place("W2", "r_probs", [P, TH, 24])
    rr = place("W2", "r_replaced", [P, TH, 24])
    rt = place("W2", "r_top", [P, TH, 8])
    rw = place("W2", "r_weights", [P, TH, 24])
    rr2 = rr
    rc = place("W2", "r_columns", [P, 4, TH])
    aw = [place("W2", f"am_w{n}", [P, P]) for n in "qk"]
    aP = place("W2", "am_P", [P, DM])
    am = place("W2", "am_cols", [P, 8])
    at["W3"] = at["W2"]
    aqk = [place("W2", f"am_{n}", [P, TOK]) for n in "qk"]
    wmix = place("W3", "w2_mix", [P, NJ[2], DM])
    xnT = place("W4", "x_norm_T", [P, KC, HALF])
    qs = mask_q
    qt = mask_q2

    c_gate, c_cw, c_cb, c_dtb, c_al, c_D, c_gq, c_gk, c_b = 0, 8, 16, 18, 20, 52, 54, 55, 56

    stack = ExitStack()
    ps = stack.enter_context(nc.psum_tensor("psum", [P, 8, 512], f32))
    psb = ps[:, :, :].bitcast(bf16)
    sems = {}

    def S(name):
        if name not in sems:
            sems[name] = stack.enter_context(nc.semaphore(name))
        return sems[name]

    LOADS = [
        ("x", x, 0, "x"), ("small", small, 0, "small"), ("ctxT", ctxT, 0, "ctx"), ("m_in", m_in, 0, "ctx"),
        ("m_bc", m_bc, 0, "ssm"), ("m_dt", m_dt, 0, "ssm"), ("m_dtw", m_dtw, 0, "ssm"), ("sel_bc", sel_bc, 0, "ssm"),
        ("ident", ident, 0, "ident"), ("w0raw", w0raw, 0, "w0"), ("wvT0", wvT, 0, "value"), ("wo0", wo, 0, "value"),
        ("identb", identb, 0, "const"), ("ctk", ctk, 0, "const"), ("had", had, 0, "const"),
        ("wk", wk, 0, "qk"), ("wq", wq, 0, "qk"),
        ("wvT1", wvT, 2, "value"), ("wo1", wo, 2, "value"),
        ("sel1", sel[1], 5, "route"), ("f1r", fr[1], 5, "route"), ("f1a", f1a, 5, "f1a"),
        ("f1b", f1b, 7, "f1b"), ("am2q", aw[0], 7, "map"), ("am2k", aw[1], 7, "map"), ("f2w", f2w, 7, "f2"),
        ("am3q", aw[0], 8, "map"), ("am3k", aw[1], 8, "map"),
        ("sel3", sel[3], 9, "route"), ("f3r", fr[3], 9, "route"), ("f3w", f3w, 9, "f3"),
    ]
    load_count = {name: (group, 16 * sum(1 for _, _, s2, g2 in LOADS if g2 == group and s2 <= step))
                  for name, _, step, group in LOADS}

    ORDER = ["prep"] + [(b, h) for b in ("M", "F0", "A1", "F1") for h in range(2)] + \
            [(b, h) for b in ("A2", "F2", "A3", "F3") for h in range(2)]
    POOL_STEPS = [k for k, s in enumerate(ORDER) if s != "prep" and s[0] in ("M", "A1", "F1", "F2", "F3")]

    def begin(eng, k):
        if k:
            eng.wait_ge(S("pe_step"), k)
            eng.wait_ge(S("act_step"), k)
            eng.wait_ge(S("dve_step"), k)
            done = sum(1 for s in POOL_STEPS if s < k)
            if done:
                eng.wait_ge(S("pool_step"), done)

    def loaded(eng, *names):
        for n in names:
            group, count = load_count[n]
            eng.wait_ge(S("ld_" + group), count)

    def chain(eng, sem):
        n = [0]

        def link(ins):
            n[0] += 1
            ins.then_inc(S(sem), 1)
            eng.wait_ge(S(sem), n[0])
        return link

    def bc(ap, shape):
        return ap.to_broadcast(shape)

    gate_col = {"M": 0, "F0": 4, "A1": 1, "F1": 5, "A2": 2, "F2": 6, "A3": 3, "F3": 7}
    ln_index = {}
    n_ln = 2
    for s in ORDER[1:]:
        if s != "maps":
            ln_index[s] = len(ln_index) + 1
    xt_index = {s: i + 1 for i, s in enumerate(s for s in ORDER if s not in ("prep", "maps") and s[0] not in ("M", "F0"))}
    split_index = {s: i + 1 for i, s in enumerate(s for s in ORDER if s[0] in ("A1", "F1", "F2", "F3"))}
    map_index = {s: i + 1 for i, s in enumerate(s for s in ORDER if s[0] in ("A2", "A3"))}

    G0 = {1: 0, 2: 2 * NJ[1], 3: 2 * (NJ[1] + NJ[2])}
    D0 = {1: 0, 2: 2 * NJ[1] - 2, 3: 2 * (NJ[1] + NJ[2]) - 4}
    C0 = {1: 0, 3: 2 * NJ[1]}
    R0 = {1: 0, 3: 2}

    def raw_w(l, j):
        if l == 1:
            return f1a[:, j, :] if j < J1A else f1b[:, j - J1A, :]
        return (f2w if l == 2 else f3w)[:, j, :]

    block = stack.enter_context(nc.Block())

    @block.sync
    def _(sp):
        reached = 0
        for name, dst, step, group in LOADS:
            if step > reached:
                begin(sp, step)
                reached = step
            full = tuple(slice(None) for _ in dst.shape)
            sp.dma_start(dst[full], dram[name]).then_inc(S("ld_" + group), 16)
        for h in range(2):
            sp.wait_ge(S("x_final"), h + 1)
            sp.dma_start(out[:, h * TH:(h + 1) * TH, :], x[:, h * TH:(h + 1) * TH, :]).then_inc(S("stored"), 16)
        sp.wait_ge(S("stored"), 32)

    @block.tensor
    def _(pe):
        mm = nc.tensor.matmul

        def transpose_norm(h, s, banks=(2, 3)):
            pe.wait_ge(S("ln_done"), ln_index[s])
            for c in range(KC):
                for t in range(TH):
                    last = nc.tensor.transpose(ps[:, banks[c], t * P:(t + 1) * P], xn[h][:, t, c * P:(c + 1) * P], ident[:, :])
            last.then_inc(S("xT_psum"), 1)

        def mm3(out, wh, wl, xh, xl, start, stop, **kw):
            mm(out, wh, xh, start=start, stop=False, **kw)
            mm(out, wh, xl, start=False, stop=False, **kw)
            return mm(out, wl, xh, start=False, stop=stop, **kw)

        def prep(k):
            pe.wait_ge(S("ones_set"), 1)
            mm(ps[:, 0, 0:2], ones[:, :], ones[:, 0:2], start=True, stop=True).then_inc(S("pe_step"), 1)

        def ssm(k, h):
            toks = slice(h * HALF, (h + 1) * HALF)
            loaded(pe, "ctxT", "m_in", "sel_bc")
            for e in range(2):
                last = mm(ps[:, e, :], m_in[:, e * P:(e + 1) * P], ctxT[:, toks], start=True, stop=True)
            last.then_inc(S("m_x"), 1)
            loaded(pe, "m_bc", "m_dt", "m_dtw")
            pe.wait_ge(S("m_u"), h + 1)
            for e in range(2):
                mm(ps[0:96, 2, :], m_bc[:, e, :], u[:, e, :], start=e == 0, stop=e == 1)
            for e in range(2):
                last = mm(ps[0:8, 3, :], m_dt[:, e, :], u[:, e, :], start=e == 0, stop=e == 1)
            last.then_inc(S("m_dbl"), 1)
            pe.wait_ge(S("m_dts"), h + 1)
            for e in range(2):
                last = mm(ps[:, e, :], m_dtw[:, e * P:(e + 1) * P], dts[:, :], start=True, stop=True)
            last.then_inc(S("m_dpre"), 1)
            pe.wait_ge(S("m_bcs"), h + 1)
            pe.wait_ge(S("m_xs"), h + 1)
            if h:
                mm(ps[:, 7, 256:259], ones[:, :], wabs[:, 0:3], start=True, stop=True).then_inc(S("wabs_sum"), 1)

            def broadcast_B(n):
                if n >= 2:
                    pe.wait_ge(S("m_Bcopy"), h * NS + n - 1)
                mm(ps[:, 2 + n % 2, :], sel_bc[:, n, :], bcs[:, :], start=True, stop=True).then_inc(S("m_B"), 1)

            loaded(pe, f"wvT{h}", f"wo{h}")
            broadcast_B(0)
            for n in range(NS + 1):
                g = h * NS + n
                if n + 1 < NS:
                    broadcast_B(n + 1)
                if n < NS:
                    if n >= 2:
                        pe.wait_ge(S("m_hC"), g - 1)
                    mm(ps[:, 4 + n % 2, :], sel_bc[:, NS + n, :], bcs[:, :], start=True, stop=True).then_inc(S("m_C"), 1)
                if n < NS and n % 2 == 0:
                    v = n // 2
                    if h or v:
                        pe.wait_ge(S("wvo_copied"), h * 8 + v)
                    mm(ps[:, 6, 0:DM], wvT[:, v, :], wo[:, v, :], start=True, stop=True).then_inc(S("wvo_psum"), 1)
                if n:
                    pe.wait_ge(S("m_hC"), g)
                    for e in range(2):
                        last = mm(ps[:, e, :], ident[:, :], hC[(n - 1) % 2][:, e, :], start=n == 1, stop=n == NS)
                    last.then_inc(S("m_y"), 1)
            pe.wait_ge(S("wvo_copied"), h * 8 + 8)
            pe.wait_ge(S("m_yz"), h + 1)
            for t in range(TH):
                b, lb = t // 2, t % 2
                for e in range(2):
                    last = nc.tensor.transpose(ps[:, 6 + t // 2, (t % 2) * DM + e * P:(t % 2) * DM + (e + 1) * P],
                                               u[:, e, b * DM + lb * P:b * DM + (lb + 1) * P], ident[:, :])
            last.then_inc(S("pe_step"), 1)

        def ffn0(k, h):
            loaded(pe, "identb")
            pe.wait_ge(S("q_xq"), h + 1)
            for c in range(KC):
                for t in range(TH):
                    last = nc.tensor.transpose(psb[:, 2, c * HALF + t * P:c * HALF + (t + 1) * P],
                                               xq[:, t, c * P:(c + 1) * P], identb[:, :])
            last.then_inc(S("q_xTp"), 1)
            pe.wait_ge(S("q_xT"), h + 1)
            def down(t):
                g = h * TH + t
                pe.wait_ge(S("q_hq"), g + 1)
                if g:
                    pe.wait_ge(S("q_hT"), g)
                for j in range(I0 // P):
                    last = nc.tensor.transpose(psb[:, 7, j * P:(j + 1) * P], hq[:, j * P:(j + 1) * P], identb[:, :])
                last.then_inc(S("q_hTp"), 1)
                pe.wait_ge(S("q_hT"), g + 1)
                if t >= 2:
                    pe.wait_ge(S("q_out"), g - 1)
                if h == t == 0:
                    pe.wait_ge(S("w0_ready"), 3)
                for j in range(I0 // P):
                    last = mm(ps[:, t % 2, 0:DM], hqT[:, j, :], w0q[2][:, j * DM:(j + 1) * DM], start=j == 0, stop=j == I0 // P - 1)
                last.then_inc(S("q_down"), 1)
                return last
            for t in range(TH):
                for n in range(2):
                    g = 2 * (h * TH + t) + n
                    for w, b0, free in ((0, 3, "q_sg"), (1, 5, "q_h")):
                        if h == t == n == 0:
                            pe.wait_ge(S("w0_ready"), w + 1)
                        if t:
                            pe.wait_ge(S(free), g - 1)
                        for c in range(KC):
                            last = mm(ps[:, b0 + n, :], xqT[:, c, t * P:(t + 1) * P],
                                      w0q[w][:, c * I0 + n * 512:c * I0 + (n + 1) * 512], start=c == 0, stop=c == KC - 1)
                        last.then_inc(S("q_gate" if w == 0 else "q_up"), 1)
                if t:
                    down(t - 1)
            down(TH - 1)
            pe.wait_ge(S("q_down"), (h + 1) * TH)
            nc.tensor.transpose(psb[:, 2, 0:P], identb[:, :], identb[:, :]).then_inc(S("pe_step"), 1)

        def attn1(k, h):
            loaded(pe, "wq", "wk", "ctk")
            transpose_norm(h, ("A1", h), (6, 7))
            pe.wait_ge(S("xT_hi"), split_index[("A1", h)])
            pe.wait_ge(S("xT_ready"), split_index[("A1", h)])
            pe.wait_ge(S("a_ctx"), h + 1)

            def keys_queries(i):
                g = h * HEADS + i
                hi, lo = awh[i % 2], awl[i % 2]
                pe.wait_ge(S("a_w"), g + 1)
                if i:
                    pe.wait_ge(S("a_kT"), g)
                for t in range(TH):
                    sl = slice(t * P, (t + 1) * P)
                    last = mm3(ps[:, 7, sl], ch[:, sl], cl[:, sl], hi[:, KC * P:AQ], lo[:, KC * P:AQ], True, True)
                last.then_inc(S("a_k"), 1)
                if i:
                    pe.wait_ge(S("a_rqs"), g)
                for c in range(KC):
                    last = mm3(ps[:, 6, :], hi[:, c * P:(c + 1) * P], lo[:, c * P:(c + 1) * P], xTh[:, c, :], xTl[:, c, :],
                               c == 0, c == KC - 1)
                last.then_inc(S("a_q"), 1)

            def norm_transpose(i):
                g = h * HEADS + i
                pe.wait_ge(S("a_qsq"), g + 1)
                pe.wait_ge(S("a_ql"), g + 1)
                for t in range(TH):
                    last = mm(ps[:, 6, t:t + 1], qsq[:, t * P:(t + 1) * P], ones[:, 0:1], start=True, stop=True)
                last.then_inc(S("a_qn"), 1)
                pe.wait_ge(S("a_ktok"), g + 1)
                for t in range(TH):
                    last = nc.tensor.transpose(ps[:, 7, t * P:(t + 1) * P], ktok[:, t * P:(t + 1) * P], ident[:, :])
                last.then_inc(S("a_kt"), 1)

            keys_queries(0)
            norm_transpose(0)
            for i in range(HEADS + 2):
                g = h * HEADS + i
                if i + 1 < HEADS:
                    keys_queries(i + 1)
                if i >= 2:
                    pe.wait_ge(S("a_al"), g - 1)
                    pe.wait_ge(S("a_vol"), g - 1)
                    for t in range(TH):
                        sl = slice(t * P, (t + 1) * P)
                        last = mm3(ps[:, t // 2, (t % 2) * DM:(t % 2 + 1) * DM], ah[:, sl], al[:, sl],
                                   voh[i % 2][:, :], vol[i % 2][:, :],
                                   i == 2 and t % 2 == 0, i == HEADS + 1, skip_group_check=True)
                    if i < HEADS + 1:
                        last.then_inc(S("a_out"), 1)
                if i < HEADS:
                    pe.wait_ge(S("a_kT"), g + 1)
                    pe.wait_ge(S("a_ql"), g + 1)
                    if i:
                        pe.wait_ge(S("a_exp"), g)
                    for t in range(TH):
                        sl = slice(t * P, (t + 1) * P)
                        kv = slice((t // 2) * DM, (t // 2 + 1) * DM)
                        last = mm3(ps[:, 2 + t // 2, (t % 2) * DM:(t % 2 + 1) * DM], qh[i % 2][:, sl], ql[i % 2][:, sl],
                                   kh[:, kv], kl[:, kv], True, True)
                    last.then_inc(S("a_s"), 1)
                if 1 <= i <= HEADS:
                    pe.wait_ge(S("a_pn"), g)
                    if i > 1:
                        pe.wait_ge(S("a_al"), g - 1)
                    for t in range(TH):
                        b, qb = t // 2, t % 2
                        for kv in range(2):
                            last = nc.tensor.transpose(ps[:, 4 + b, kv * DM + qb * P:kv * DM + (qb + 1) * P],
                                                       Pm[(i - 1) % 2][:, t, kv * P:(kv + 1) * P], ident[:, :])
                    last.then_inc(S("a_pt"), 1)
                if i + 1 < HEADS:
                    norm_transpose(i + 1)
                if 1 <= i <= HEADS:
                    pe.wait_ge(S("a_pts"), g)
                    for b in range(2):
                        for kv in range(2):
                            last = mm(ps[:, 4, b * DM:(b + 1) * DM], ctk[:, h * TH + 2 * b + kv, :],
                                      PT[:, b, kv * DM:(kv + 1) * DM], start=kv == 0, stop=kv == 1)
                    last.then_inc(S("a_ac"), 1)
            last.then_inc(S("pe_step"), 1)

        def ffn(k, l, h):
            J = NJ[l]
            routed = l != 2
            transpose_norm(h, (f"F{l}", h))
            pe.wait_ge(S("xT_hi"), split_index[(f"F{l}", h)])
            pe.wait_ge(S("xT_ready"), split_index[(f"F{l}", h)])
            if routed:
                loaded(pe, f"sel{l}")
                pe.wait_ge(S("r_w"), R0[l] + h + 1)
                for t in range(TH):
                    sl = slice(t * P, (t + 1) * P)
                    for c in range(KC):
                        last = mm3(ps[:, 7, t * 32:(t + 1) * 32], xTh[:, c, sl], xTl[:, c, sl], wrh[:, c, :], wrl[:, c, :],
                                   c == 0, c == KC - 1)
                last.then_inc(S("f_logits"), 1)

            def gate_up(j):
                g = G0[l] + h * J + j
                pe.wait_ge(S("f_wg"), g + 1)
                if j >= 2:
                    pe.wait_ge(S("f_sg"), g - 1)
                    pe.wait_ge(S("f_m"), g - 1)
                for b in range(2):
                    for c in range(KC):
                        sl = slice((b * KC + c) * P, (b * KC + c + 1) * P)
                        last = mm3(ps[:, 2 + 2 * (j % 2) + b, :], wgh[j % 2][:, sl], wgl[j % 2][:, sl], xTh[:, c, :], xTl[:, c, :],
                                   c == 0, c == KC - 1)
                last.then_inc(S("f_gu"), 1)

            def combine(i):
                if i == 0:
                    pe.wait_ge(S("f_cmbT"), R0[l] + h + 1)
                else:
                    pe.wait_ge(S("f_h"), C0[l] + h * J + i)
                mm(ps[:, 6, :], sel[l][:, i, :], cmbT[:, :], start=True, stop=True).then_inc(S("f_cw"), 1)

            def down(i):
                g = G0[l] + h * J + i
                pe.wait_ge(S("f_wd"), g + 1)
                pe.wait_ge(S("f_hl"), g + 1)
                for t in range(TH):
                    sl = slice(t * P, (t + 1) * P)
                    last = mm3(ps[:, t // 2, (t % 2) * DM:(t % 2 + 1) * DM], hh[i % 2][:, sl], hl[i % 2][:, sl],
                               wdh[i % 3][:, :], wdl[i % 3][:, :], i == 0 and t % 2 == 0, i == J - 1, skip_group_check=True)
                if i < J - 1:
                    last.then_inc(S("f_down"), 1)
                return last

            for j in range(J + 2):
                if j < J:
                    gate_up(j)
                if routed and j == 1:
                    pe.wait_ge(S("f_cmb"), R0[l] + h + 1)
                    for t in range(TH):
                        last = nc.tensor.transpose(psb[0:96, 6, t * P:(t + 1) * P], cmb[:, t, :], identb[:, :])
                    last.then_inc(S("f_cmbTp"), 1)
                if routed and 1 <= j <= J:
                    combine(j - 1)
                if j >= 2:
                    last = down(j - 2)
                if l == 1:
                    beside(j - 3, h)
            last.then_inc(S("pe_step"), 1)

        def beside(s, h):
            n0 = 13 * h
            if 0 <= s <= 12:
                if s == 0:
                    loaded(pe, f"am{2 + h}q", f"am{2 + h}k")
                if n0 + s:
                    pe.wait_ge(S("am_free"), n0 + s + (4 if h else 0))
                if s < 4:
                    last = mm(ps[:, 7, :], aw[s // 2][:, :], ctxT[:, (s % 2) * HALF:(s % 2 + 1) * HALF], start=True, stop=True)
                else:
                    if s > 4:
                        pe.wait_ge(S("am_pn"), 8 * h + s - 4)
                        for kv in range(2):
                            last = nc.tensor.transpose(ps[:, 7, DM + kv * P:DM + (kv + 1) * P], aP[:, kv * P:(kv + 1) * P], ident[:, :])
                    if s < 12:
                        t = s - 4
                        last = mm(ps[:, 7, 0:DM], aqk[0][:, t * P:(t + 1) * P], aqk[1][:, (t // 2) * DM:(t // 2 + 1) * DM],
                                  start=True, stop=True)
                last.then_inc(S("am_psum"), 1)
            elif h == 0 and 13 <= s <= 16:
                j = 2 * (s - 13)
                if s == 13:
                    loaded(pe, "had", "f2w")
                pe.wait_ge(S("am_free"), s)
                mm(ps[:, 7, 0:DM], had[:, :], f2w[:, j, GU:WJ], start=True, stop=True)
                mm(ps[:, 7, DM:2 * DM], had[:, :], f2w[:, j + 1, GU:WJ], start=True, stop=True).then_inc(S("am_psum"), 1)

        def attn_map(k, l, h):
            transpose_norm(h, (f"A{l}", h))
            pe.wait_ge(S("xT_map"), map_index[(f"A{l}", h)])
            for t in range(TH):
                for c in range(KC):
                    last = mm(ps[:, t // 2, (t % 2) * DM:(t % 2 + 1) * DM], xnT[:, c, t * P:(t + 1) * P],
                              attT[l][:, c, h, (t // 2) * DM:(t // 2 + 1) * DM], start=c == 0, stop=c == KC - 1)
            last.then_inc(S("pe_step"), 1)

        loaded(pe, "ident")
        for k, s in enumerate(ORDER):
            begin(pe, k)
            if s == "prep":
                prep(k)
            else:
                b, h = s
                {"M": ssm, "F0": ffn0, "A1": attn1, "F1": lambda k, h: ffn(k, 1, h), "F2": lambda k, h: ffn(k, 2, h),
                 "F3": lambda k, h: ffn(k, 3, h), "A2": lambda k, h: attn_map(k, 2, h),
                 "A3": lambda k, h: attn_map(k, 3, h)}[b](k, h)

    @block.scalar
    def _(act):
        A = nc.scalar.activation
        link = chain(act, "act_chain")


        def copy(out_, in_):
            return A(out_, in_, ACT.Copy)

        def norm_T(s, banks=(2, 3), dst=None):
            act.wait_ge(S("xT_psum"), xt_index[s])
            for c in range(KC):
                last = copy((xTh if dst is None else dst)[:, c, :], ps[:, banks[c], :])
            last.then_inc(S("xT_hi" if dst is None else "xT_map"), 1)

        def prep(k):
            loaded(act, "small")
            A(tg[:, :], small[:, c_gate:c_gate + 8], ACT.Tanh)
            link(A(negA[:, :, :], small[:, c_al:c_al + 32].rearrange("p (e n) -> p e n", e=2), ACT.Exp))
            link(A(negA[:, :, :], negA[:, :, :], ACT.Copy, scale=-1.0))
            copy(mask_small[:, 0:8], tg[:, :]).then_inc(S("act_step"), 1)

        def ssm(k, h):
            act.wait_ge(S("ln_done"), ln_index[("M", h)])
            A(zs[:, :, :], xn[h][:, :, :], ACT.Silu)
            act.wait_ge(S("m_conv"), h + 1)
            for e in range(2):
                last = A(u[:, e, :], dlt[:, e, :], ACT.Silu, bias=small[:, c_cb + e:c_cb + e + 1])
            last.then_inc(S("m_u"), 1)
            act.wait_ge(S("m_xs"), h + 1)
            link(A(dA[0][:, :, :], dlt[:, :, :], ACT.Abs))
            A(dA[1][:, :, :], dA[0][:, :, :], ACT.Exp, scale=-1.0).then_inc(S("m_ex"), 1)
            act.wait_ge(S("m_w"), h + 1)
            link(A(hC[0][:, :, :], dBu[0][:, :, :], ACT.Ln))
            A(hC[1][:, :, :], hC[0][:, :, :], ACT.Exp, scale=-1.0).then_inc(S("m_lnw"), 1)
            def copy_B(n):
                g = h * NS + n
                act.wait_ge(S("m_B"), g + 1)
                if n >= 2:
                    act.wait_ge(S("m_dBu"), g - 1)
                copy(Bs[n % 2][:, :], ps[:, 2 + n % 2, :]).then_inc(S("m_Bcopy"), 1)

            act.wait_ge(S("m_bcs"), h + 1)
            copy_B(0)
            act.wait_ge(S("m_du"), h + 1)
            for n in range(NS):
                g = h * NS + n
                if n >= 2:
                    act.wait_ge(S("m_h"), g - 1)
                for e in range(2):
                    last = A(dA[n % 2][:, e, :].rearrange("p (b l) -> p b l", b=2)[:, :, 1:DM],
                             dlt[:, e, :].rearrange("p (b l) -> p b l", b=2)[:, :, 1:DM],
                             ACT.Exp, scale=negA[:, e, n:n + 1])
                last.then_inc(S("m_dA"), 1)
                if n + 1 < NS:
                    copy_B(n + 1)
                if n % 2 == 0:
                    v = h * 8 + n // 2
                    act.wait_ge(S("wvo_psum"), v + 1)
                    copy(wvo[:, v, :], ps[:, 6, 0:DM]).then_inc(S("wvo_copied"), 1)
            if h == 0:
                loaded(act, "w0raw")
                for i in range(3):
                    last = A(w_values[:, :], w0raw[:, i, :], ACT.Abs, accum_out=wabs[:, i:i + 1])
                    if i < 2:
                        link(last)
                last.then_inc(S("wabs_part"), 1)
            copy(mask_small[:, 0:8], tg[:, :]).then_inc(S("act_step"), 1)

        def ffn0(k, h):
            act.wait_ge(S("q_xTp"), h + 1)
            copy(xqT[:, :, :].rearrange("p c t -> p (c t)"), psb[:, 2, :]).then_inc(S("q_xT"), 1)
            act.wait_ge(S("q_s"), h + 1)
            for t in range(TH + 1):
                g = h * TH + t
                if t < TH:
                    if g >= 2:
                        act.wait_ge(S("q_h"), 2 * (g - 1))
                    for n in range(2):
                        act.wait_ge(S("q_gate"), 2 * g + n + 1)
                        A(sg0[g % 2][:, n * 512:(n + 1) * 512], ps[:, 3 + n, :], ACT.Silu,
                          scale=qs[:, t:t + 1]).then_inc(S("q_sg"), 1)
                if t:
                    act.wait_ge(S("q_hTp"), g)
                    if g > 1:
                        act.wait_ge(S("q_down"), g - 1)
                    copy(hqT[:, :, :].rearrange("p j t -> p (j t)"), psb[:, 7, :]).then_inc(S("q_hT"), 1)
                if t < TH:
                    act.wait_ge(S("q_inv"), g + 1)
                    A(h0a[:, :], h0[:, :], ACT.Identity, scale=qt[:, 2:3], bias=magic[:, :]).then_inc(S("q_r"), 1)
            copy(mask_small[:, 0:8], tg[:, :]).then_inc(S("act_step"), 1)

        def attn1(k, h):
            copy(ch[:, :], ctxT[:, h * HALF:(h + 1) * HALF]).then_inc(S("a_ch"), 1)

            def parts(i):
                g = h * HEADS + i
                if i >= 2:
                    act.wait_ge(S("a_q"), g - 1)
                    act.wait_ge(S("a_w"), g - 1)
                copy(awh[i % 2][:, 0:KC * P].rearrange("p (c n) -> p c n", c=KC), wq[:, :, i * P:(i + 1) * P])
                copy(awh[i % 2][:, KC * P:AQ], wk[:, i * P:(i + 1) * P]).then_inc(S("a_wh"), 1)

            def value_parts(i):
                g = h * HEADS + i
                if i >= 2:
                    act.wait_ge(S("a_out"), h * (HEADS - 1) + i - 1)
                copy(voh[i % 2][:, :], wvo[:, i, :]).then_inc(S("a_voh"), 1)

            def squares(i):
                g = h * HEADS + i
                act.wait_ge(S("a_k"), g + 1)
                if i:
                    act.wait_ge(S("a_rks"), g)
                A(ksq[:, :], ps[:, 7, :], ACT.Square).then_inc(S("a_ksq"), 1)
                act.wait_ge(S("a_q"), g + 1)
                if i:
                    act.wait_ge(S("a_qn"), g)
                A(qsq[:, :], ps[:, 6, :], ACT.Square).then_inc(S("a_qsq"), 1)
                if i > 1:
                    act.wait_ge(S("a_s"), g - 1)
                copy(qh[i % 2][:, :], ps[:, 6, :]).then_inc(S("a_qh"), 1)

            def keys_hi(i):
                g = h * HEADS + i
                act.wait_ge(S("a_kt"), g + 1)
                act.wait_ge(S("gqk_ready"), 1)
                A(kh[:, :], ps[:, 7, :], ACT.Copy, scale=gqk[:, :]).then_inc(S("a_kh"), 1)

            def ac_hi(i):
                g = h * HEADS + i
                act.wait_ge(S("a_ac"), g + 1)
                if i:
                    act.wait_ge(S("a_out"), (HEADS - 1) * h + i)
                copy(ah[:, :], ps[:, 4, :]).then_inc(S("a_ah"), 1)

            parts(0)
            norm_T(("A1", h), (6, 7))
            parts(1)
            squares(0)
            keys_hi(0)
            for i in range(HEADS + 1):
                g = h * HEADS + i
                if i >= 2:
                    ac_hi(i - 2)
                if i + 1 < HEADS:
                    squares(i + 1)
                if i + 2 < HEADS:
                    parts(i + 2)
                if i:
                    value_parts(i - 1)
                if i:
                    act.wait_ge(S("a_pt"), g)
                    if i > 1:
                        act.wait_ge(S("a_ac"), g - 1)
                    copy(PT[:, :, :], ps[:, 4:6, :]).then_inc(S("a_pts"), 1)
                if i + 1 < HEADS:
                    keys_hi(i + 1)
                if i < HEADS:
                    act.wait_ge(S("a_nb"), g + 1)
                    if i > 1:
                        act.wait_ge(S("a_pt"), g - 1)
                    if i:
                        act.wait_ge(S("a_ri"), g)
                    for t in range(TH):
                        last = A(Pm[i % 2][:, t, :], ps[:, 2 + t // 2, (t % 2) * DM:(t % 2 + 1) * DM], ACT.Exp,
                                 bias=nb[:, t:t + 1], scale=rq[i % 2][:, t:t + 1], accum_out=rs[:, t:t + 1])
                    last.then_inc(S("a_exp"), 1)
            ac_hi(HEADS - 1)
            copy(mask_small[:, 0:8], tg[:, :]).then_inc(S("act_step"), 1)

        def ffn(k, l, h):
            J = NJ[l]
            routed = l != 2

            def gu_hi(j):
                g = G0[l] + h * J + j
                if l == 1 and j == J1A:
                    loaded(act, "f1b")
                if j >= 2:
                    act.wait_ge(S("f_gu"), g - 1)
                copy(wgh[j % 2][:, :], raw_w(l, j)[:, 0:GU]).then_inc(S("f_wgh"), 1)

            def d_hi(j):
                g = G0[l] + h * J + j
                if j >= 3:
                    act.wait_ge(S("f_down"), D0[l] + h * (J - 1) + j - 2)
                copy(wdh[j % 3][:, :], raw_w(l, j)[:, GU:WJ]).then_inc(S("f_wdh"), 1)

            loaded(act, {1: "f1a", 2: "f2w", 3: "f3w"}[l])
            if routed:
                loaded(act, f"f{l}r")
                copy(wrh[:, :, :], fr[l][:, :, :]).then_inc(S("r_wh"), 1)
            gu_hi(0)
            norm_T((f"F{l}", h))
            gu_hi(1)
            d_hi(0)
            if routed:
                e = E1 if l == 1 else E3
                act.wait_ge(S("f_shift"), R0[l] + h + 1)
                if l == 1:
                    A(rc[:, 3, :], rl[:, :, e], ACT.Exp, scale=-1.0)
                A(rp[:, :, 0:e], rw[:, :, 0:e], ACT.Exp).then_inc(S("f_ex"), 1)
            for j in range(J + 1):
                g = G0[l] + h * J + j
                if j < J:
                    act.wait_ge(S("f_gu"), g + 1)
                    if j >= 2:
                        act.wait_ge(S("f_hl"), g - 1)
                    A(sg[j % 2][:, :], ps[:, 2 + 2 * (j % 2), :], ACT.Silu).then_inc(S("f_sg"), 1)
                if j:
                    act.wait_ge(S("f_h" if routed else "f_m"), C0[l] + h * J + j if routed else g)
                    if j >= 3:
                        act.wait_ge(S("f_down"), D0[l] + h * (J - 1) + j - 2)
                    copy(hh[(j - 1) % 2][:, :], sg[(j - 1) % 2][:, :]).then_inc(S("f_hh"), 1)
                if j + 2 < J:
                    gu_hi(j + 2)
                if j + 1 < J:
                    d_hi(j + 1)
                if l == 1:
                    beside(j - 3, h)
            copy(mask_small[:, 0:8], tg[:, :]).then_inc(S("act_step"), 1)

        def beside(s, h):
            if 0 <= s < 4:
                act.wait_ge(S("am_psum"), 17 * h + s + 1)
                A(aqk[s // 2][:, (s % 2) * HALF:(s % 2 + 1) * HALF], ps[:, 7, :], ACT.Identity,
                  bias=small[:, c_b + 2 * h + s // 2:c_b + 2 * h + s // 2 + 1]).then_inc(S("am_qk"), 1)
            elif 4 <= s < 12:
                act.wait_ge(S("am_nb"), 8 * h + s - 3)
                A(aP[:, :], ps[:, 7, 0:DM], ACT.Exp, bias=am[:, 1:2], accum_out=am[:, 2:3]).then_inc(S("am_exp"), 1)

        def attn_map(k, l, h):
            norm_T((f"A{l}", h), dst=xnT)
            copy(mask_small[:, 0:8], tg[:, :]).then_inc(S("act_step"), 1)

        for k, s in enumerate(ORDER):
            begin(act, k)
            if s == "prep":
                prep(k)
            else:
                b, h = s
                {"M": ssm, "F0": ffn0, "A1": attn1, "F1": lambda k, h: ffn(k, 1, h), "F2": lambda k, h: ffn(k, 2, h),
                 "F3": lambda k, h: ffn(k, 3, h), "A2": lambda k, h: attn_map(k, 2, h),
                 "A3": lambda k, h: attn_map(k, 3, h)}[b](k, h)

    @block.vector
    def _(dve):
        V = nc.vector
        link = chain(dve, "dve_chain")
        n_tail = [0]

        def tail(h):
            n_tail[0] += 1
            for t in range(TH):
                last = V.bn_stats(bst[:, t, :], x[:, h * TH + t, :])
            link(last)
            for t in range(TH):
                last = V.bn_aggr(mv[:, t, :], bst[:, t, :])
            link(last)
            V.tensor_scalar(ve[:, :], mv[:, :, 1], EPS, None, ALU.add).then_inc(S("ln_var"), 1)
            dve.wait_ge(S("ln_rstd"), n_tail[0])
            for t in range(TH):
                last = V.tensor_scalar(xn[h][:, t, :], x[:, h * TH + t, :], mv[:, t, 0:1], rstd[:, t:t + 1],
                                       ALU.subtract, ALU.mult)
            last.then_inc(S("ln_done"), 1)

        def residual(s, h, k, bank=0):
            dve.wait_ge(S("pe_step"), k + 1)
            xv = x[:, h * TH:(h + 1) * TH, :].rearrange("p t d -> p (t d)")
            c = gate_col[s]
            link(V.scalar_tensor_tensor(xv, ps[:, bank:bank + 2, :].rearrange("p a n -> p (a n)"), tg[:, c:c + 1], xv, ALU.mult, ALU.add))

        def done(s, h, k):
            V.tensor_copy(mask_small[:, 8:9], epsc[:, :]).then_inc(S("dve_step"), 1)
            dve.wait_ge(S("act_step"), k + 1)
            if s != "F3":
                tail(h)

        def x_lo(s, banks=(2, 3)):
            dve.wait_ge(S("xT_hi"), split_index[s])
            for c in range(KC):
                last = V.tensor_tensor(xTl[:, c, :], ps[:, banks[c], :], xTh[:, c, :].bitcast(f32), ALU.subtract)
            last.then_inc(S("xT_ready"), 1)

        def prep(k):
            V.memset(ones[:, :], 1.0).then_inc(S("ones_set"), 1)
            V.memset(epsc[:, :], EPS)
            V.memset(magic[:, :], MAGIC)
            V.memset(mhalf[:, :], -0.5).then_inc(S("mhalf_set"), 1)
            loaded(dve, "x")
            tail(0)
            tail(1)
            loaded(dve, "small")
            V.tensor_scalar(gqk[:, :], small[:, c_gq:c_gq + 1], small[:, c_gk:c_gk + 1], SCALE, ALU.mult, ALU.mult).then_inc(S("gqk_ready"), 1)
            V.tensor_copy(mask_small[:, 8:9], epsc[:, :]).then_inc(S("dve_step"), 1)

        def quantise_weights():
            dve.wait_ge(S("wabs_sum"), 1)
            link(V.tensor_scalar(wscale[:, :], ps[:, 7, 256:259], 1.0 / (DM * I0), EPS, ALU.mult, ALU.add))
            link(V.reciprocal(winv[:, :], wscale[:, :]))

        def quantise(i):
            link(V.tensor_scalar(wtmp[:, 0, :], w0raw[:, i, :], winv[:, i:i + 1], MAGIC, ALU.mult, ALU.add))
            link(V.tensor_scalar(wtmp[:, 1, :], wtmp[:, 0, :], MAGIC, 1.0, ALU.subtract, ALU.min))
            V.tensor_scalar(w0q[i][:, :], wtmp[:, 1, :], -1.0, None, ALU.max).then_inc(S("w0_ready"), 1)
            dve.wait_ge(S("w0_ready"), i + 1)

        def ssm(k, h):
            if h == 0:
                V.memset(xpad[:, :, :, 0:3], 0.0)
            dve.wait_ge(S("m_x"), h + 1)
            for e in range(2):
                last = V.tensor_copy(xpad[:, e, :, 3:DM + 3], ps[:, e, :].rearrange("p (b l) -> p b l", b=2))
            link(last)
            for e in range(2):
                for c in range(4):
                    w = small[:, c_cw + 4 * e + c:c_cw + 4 * e + c + 1]
                    src = xpad[:, e, :, c:c + DM]
                    dst = (dA[0], dlt)[c % 2][:, e, :].rearrange("p (b l) -> p b l", b=2)
                    prev = (dA[0], dlt)[(c + 1) % 2][:, e, :].rearrange("p (b l) -> p b l", b=2)
                    if c == 0:
                        link(V.tensor_scalar(dst, src, w, None, ALU.mult))
                    elif c < 3 or e == 0:
                        link(V.scalar_tensor_tensor(dst, src, w, prev, ALU.mult, ALU.add))
                    else:
                        V.scalar_tensor_tensor(dst, src, w, prev, ALU.mult, ALU.add).then_inc(S("m_conv"), 1)
            dve.wait_ge(S("m_dbl"), h + 1)
            V.tensor_copy(dts[:, :], ps[0:8, 3, :]).then_inc(S("m_dts"), 1)
            r1, r2 = dBu[1][0:96, 0, :], dBu[1][0:96, 1, :]
            p1, p2 = Bs[0][0:96, 0:256].bitcast(bf16), Bs[0][0:96, 256:512].bitcast(bf16)
            link(V.tensor_copy(p1, ps[0:96, 2, :]))
            link(V.tensor_tensor(r1, ps[0:96, 2, :], p1, ALU.subtract))
            link(V.tensor_copy(p2, r1))
            link(V.tensor_tensor(r2, r1, p2, ALU.subtract))
            V.tensor_copy(bcs[0:32, :], p1[0:32, :])
            V.tensor_copy(bcs[32:64, :], p2[32:64, :])
            V.tensor_copy(bcs[64:96, :], r2[64:96, :]).then_inc(S("m_bcs"), 1)
            dve.wait_ge(S("m_dpre"), h + 1)
            for e in range(2):
                last = V.tensor_scalar(dlt[:, e, :], ps[:, e, :], small[:, c_dtb + e:c_dtb + e + 1], None, ALU.add)
            last.then_inc(S("m_xs"), 1)
            if h:
                quantise_weights()
            dve.wait_ge(S("m_ex"), h + 1)
            V.tensor_scalar(dBu[0][:, :, :], dA[1][:, :, :], 1.0, None, ALU.add).then_inc(S("m_w"), 1)
            dve.wait_ge(S("m_w"), h + 1)
            link(V.scalar_tensor_tensor(du[:, :, :], dBu[0][:, :, :], 1.0, dA[1][:, :, :], ALU.subtract, ALU.subtract))
            dve.wait_ge(S("m_lnw"), h + 1)
            link(V.tensor_tensor(du[:, :, :], du[:, :, :], hC[1][:, :, :], ALU.mult))
            link(V.scalar_tensor_tensor(dlt[:, :, :], dlt[:, :, :], 0.0, hC[0][:, :, :], ALU.max, ALU.add))
            link(V.tensor_tensor(dlt[:, :, :], dlt[:, :, :], du[:, :, :], ALU.subtract))
            for i in range(2):
                V.memset(dA[i][:, :, :].rearrange("p e (b l) -> p (e b) l", b=2)[:, :, 0:1], 0.0)
            V.tensor_tensor(du[:, :, :], dlt[:, :, :], u[:, :, :], ALU.mult).then_inc(S("m_du"), 1)
            for n in range(NS):
                g = h * NS + n
                dve.wait_ge(S("m_dA"), g + 1)
                dve.wait_ge(S("m_dBu"), g + 1)
                if n:
                    dve.wait_ge(S("m_hC"), g)
                flat = "p e t -> p (e t)"
                V.tensor_tensor_scan(hst[:, :, :].rearrange(flat), dA[n % 2][:, :, :].rearrange(flat),
                                     dBu[n % 2][:, :, :].rearrange(flat), 0.0, ALU.mult, ALU.add).then_inc(S("m_h"), 1)
                dve.wait_ge(S("m_h"), g + 1)
                dve.wait_ge(S("m_C"), g + 1)
                if n >= 2:
                    dve.wait_ge(S("m_y"), g - 1)
                V.tensor_tensor(hC[n % 2][:, :, :], hst[:, :, :], bc(ps[:, 4 + n % 2, :].unsqueeze(1), [P, 2, HALF]),
                                ALU.mult).then_inc(S("m_hC"), 1)
            dve.wait_ge(S("m_y"), (h + 1) * NS)
            for e in range(2):
                last = V.scalar_tensor_tensor(dlt[:, e, :], u[:, e, :], small[:, c_D + e:c_D + e + 1], ps[:, e, :], ALU.mult, ALU.add)
            link(last)
            for e in range(2):
                last = V.tensor_tensor(u[:, e, :].rearrange("p (b l) -> p b l", b=2), dlt[:, e, :].rearrange("p (b l) -> p b l", b=2),
                                       zs[:, :, :].rearrange("p (b e) l -> p e b l", e=2)[:, e], ALU.mult)
            last.then_inc(S("m_yz"), 1)
            residual("M", h, k, 6)
            done("M", h, k)

        def ffn0(k, h):
            x_h = xn[h]
            am_, s_, r_, su = qs[:, 4:8], qs[:, 8:12], qs[:, 12:16], qs[:, 16:20]
            dve.wait_ge(S("ln_done"), ln_index[("F0", h)])
            link(V.tensor_reduce(am_, x_h[:, :, :], AX, ALU.max, apply_absolute_value=True))
            link(V.tensor_scalar(s_, am_, 1.0 / 127.0, EPS, ALU.mult, ALU.add))
            link(V.reciprocal(r_, s_))
            V.tensor_scalar(qs[:, 0:4], s_, wscale[:, 0:1], None, ALU.mult).then_inc(S("q_s"), 1)
            V.tensor_scalar(su, s_, wscale[:, 1:2], None, ALU.mult)
            for t in range(TH):
                last = V.tensor_scalar(xqa[:, t, :], x_h[:, t, :], qs[:, 12 + t:13 + t], MAGIC, ALU.mult, ALU.add)
            link(last)
            link(V.tensor_scalar(xqa[:, :, :], xqa[:, :, :], MAGIC, 127.0, ALU.subtract, ALU.min))
            V.tensor_scalar(xq[:, :, :], xqa[:, :, :], -128.0, None, ALU.max).then_inc(S("q_xq"), 1)
            def out(t):
                g = h * TH + t
                dve.wait_ge(S("q_down"), g + 1)
                xv = x[:, g, :]
                V.scalar_tensor_tensor(xv, ps[:, t % 2, 0:DM], qs[:, 20 + t:21 + t], xv, ALU.mult, ALU.add).then_inc(S("q_out"), 1)
            if h == 0:
                for i in range(3):
                    quantise(i)
            for t in range(TH):
                g = h * TH + t
                for n in range(2):
                    sl = slice(n * 512, (n + 1) * 512)
                    dve.wait_ge(S("q_up"), 2 * g + n + 1)
                    dve.wait_ge(S("q_sg"), 2 * g + n + 1)
                    if g:
                        dve.wait_ge(S("q_r"), g)
                    V.scalar_tensor_tensor(h0[:, sl], ps[:, 5 + n, :], qs[:, 16 + t:17 + t],
                                           sg0[g % 2][:, sl], ALU.mult, ALU.mult).then_inc(S("q_h"), 1)
                dve.wait_ge(S("q_h"), 2 * g + 2)
                link(V.tensor_reduce(qt[:, 0:1], h0[:, :], AX, ALU.max, apply_absolute_value=True))
                link(V.tensor_scalar(qt[:, 1:2], qt[:, 0:1], 1.0 / 127.0, EPS, ALU.mult, ALU.add))
                V.reciprocal(qt[:, 2:3], qt[:, 1:2]).then_inc(S("q_inv"), 1)
                V.tensor_scalar(qs[:, 20 + t:21 + t], qt[:, 1:2], wscale[:, 2:3], tg[:, gate_col["F0"]:gate_col["F0"] + 1], ALU.mult, ALU.mult)
                if t:
                    out(t - 1)
                dve.wait_ge(S("q_r"), g + 1)
                link(V.tensor_scalar(h0a[:, :], h0a[:, :], MAGIC, 127.0, ALU.subtract, ALU.min))
                if g:
                    dve.wait_ge(S("q_hTp"), g)
                V.tensor_scalar(hq[:, :], h0a[:, :], -128.0, None, ALU.max).then_inc(S("q_hq"), 1)
            out(TH - 1)
            dve.wait_ge(S("q_out"), (h + 1) * TH)
            dve.wait_ge(S("pe_step"), k + 1)
            done("F0", h, k)

        def attn1(k, h):
            dve.wait_ge(S("a_ch"), h + 1)
            V.tensor_tensor(cl[:, :], ctxT[:, h * HALF:(h + 1) * HALF], ch[:, :].bitcast(f32), ALU.subtract).then_inc(S("a_ctx"), 1)
            x_lo(("A1", h), (6, 7))

            def key_norms(i):
                g = h * HEADS + i
                dve.wait_ge(S("a_ksq"), g + 1)
                if i:
                    dve.wait_ge(S("a_rk"), g)
                V.tensor_reduce(rks[:, :], ksq[:, :].rearrange("p (t d) -> p t d", t=TH), AX, ALU.add).then_inc(S("a_rks"), 1)

            def queries_lo(i):
                g = h * HEADS + i
                dve.wait_ge(S("a_qh"), g + 1)
                V.tensor_tensor(ql[i % 2][:, :], ps[:, 6, :], qh[i % 2][:, :].bitcast(f32), ALU.subtract).then_inc(S("a_ql"), 1)

            def keys_scaled(i):
                g = h * HEADS + i
                dve.wait_ge(S("a_rk"), g + 1)
                if i:
                    dve.wait_ge(S("a_kt"), g)
                V.tensor_tensor(ktok[:, :].rearrange("p (t d) -> p t d", t=TH), ps[:, 7, :].rearrange("p (t d) -> p t d", t=TH),
                                bc(rk[:, :].unsqueeze(2), [P, TH, P]), ALU.mult).then_inc(S("a_ktok"), 1)

            def query_norms(i):
                g = h * HEADS + i
                dve.wait_ge(S("a_qn"), g + 1)
                if i:
                    dve.wait_ge(S("a_rq"), g)
                V.tensor_copy(rqs[:, :], ps[:, 6, 0:TH]).then_inc(S("a_rqs"), 1)

            def keys_lo(i):
                g = h * HEADS + i
                dve.wait_ge(S("a_kh"), g + 1)
                V.scalar_tensor_tensor(kl[:, :], ps[:, 7, :], gqk[:, :], kh[:, :].bitcast(f32), ALU.mult, ALU.subtract).then_inc(S("a_kT"), 1)

            def ac_lo(i):
                dve.wait_ge(S("a_ah"), h * HEADS + i + 1)
                V.tensor_tensor(al[:, :], ps[:, 4, :], ah[:, :].bitcast(f32), ALU.subtract).then_inc(S("a_al"), 1)

            key_norms(0)
            queries_lo(0)
            keys_scaled(0)
            query_norms(0)
            keys_lo(0)
            for i in range(HEADS):
                g = h * HEADS + i
                if i >= 2:
                    ac_lo(i - 2)
                if i + 1 < HEADS:
                    key_norms(i + 1)
                    queries_lo(i + 1)
                    keys_scaled(i + 1)
                dve.wait_ge(S("a_s"), g + 1)
                link(V.tensor_reduce(mx[:, :], ps[:, 2:4, :].rearrange("p a (b n) -> p (a b) n", b=2), AX, ALU.max))
                dve.wait_ge(S("a_rq"), g + 1)
                if i:
                    dve.wait_ge(S("a_exp"), g)
                V.scalar_tensor_tensor(nb[:, :], mx[:, :], -1.0, rq[i % 2][:, :], ALU.mult, ALU.mult).then_inc(S("a_nb"), 1)
                if i + 1 < HEADS:
                    query_norms(i + 1)
                    keys_lo(i + 1)
                dve.wait_ge(S("a_exp"), g + 1)
                if i:
                    dve.wait_ge(S("a_pn"), g)
                V.reciprocal(ri[:, :], rs[:, :]).then_inc(S("a_ri"), 1)
            ac_lo(HEADS - 2)
            ac_lo(HEADS - 1)
            residual("A1", h, k)
            done("A1", h, k)

        def router(l, h):
            x_lo((f"F{l}", h))
            e, top = (E1, TOP1) if l == 1 else (E3, TOP3)
            n = e + 1
            dve.wait_ge(S("f_logits"), R0[l] + h + 1)
            nl = e + 1 if l == 1 else e
            link(V.tensor_copy(rl[:, :, 0:nl], ps[:, 7, 0:TH * 32].rearrange("p (t n) -> p t n", t=TH)[:, :, 0:nl]))
            V.memset(rp[:, :, e:24], -1.0)
            link(V.tensor_reduce(rc[:, 0, :], rl[:, :, 0:e], AX, ALU.max))
            V.tensor_tensor(rw[:, :, 0:e], rl[:, :, 0:e], bc(rc[:, 0, :].unsqueeze(2), [P, TH, e]), ALU.subtract).then_inc(S("f_shift"), 1)
            dve.wait_ge(S("f_ex"), R0[l] + h + 1)
            link(V.tensor_reduce(rc[:, 1, :], rp[:, :, 0:e], AX, ALU.add))
            link(V.reciprocal(rc[:, 1, :], rc[:, 1, :]))
            link(V.tensor_tensor(rp[:, :, 0:e], rp[:, :, 0:e], bc(rc[:, 1, :].unsqueeze(2), [P, TH, e]), ALU.mult))
            for t in range(TH):
                last = V.max(rt[:, t, :], rp[:, t, 0:e])
            link(last)
            link(V.memset(rt[:, :, top:8], -1.0))
            for t in range(TH):
                last = V.match_replace(rr[:, t, :], rt[:, t, :], rp[:, t, :], 0.0)
            link(last)
            link(V.tensor_tensor(rw[:, :, 0:e], rp[:, :, 0:e], rr[:, :, 0:e], ALU.subtract))
            if l == 1:
                link(V.tensor_reduce(rc[:, 2, :], rw[:, :, 0:e], AX, ALU.add))
                link(V.reciprocal(rc[:, 2, :], rc[:, 2, :]))
                link(V.tensor_tensor(rw[:, :, 0:e], rw[:, :, 0:e], bc(rc[:, 2, :].unsqueeze(2), [P, TH, e]), ALU.mult))
                link(V.tensor_scalar(rc[:, 3, :], rc[:, 3, :], 1.0, None, ALU.add))
                link(V.reciprocal(rw[:, :, e], rc[:, 3, :]))
            else:
                link(V.memset(rw[:, :, e:n], 1.0))
            link(V.memset(cmb[:, :, :], 0.0))
            link(V.tensor_copy(cmb[:, :, 0:n], rw[:, :, 0:n]))
            link(V.tensor_tensor(rr2[:, :, 0:n], rw[:, :, 0:n], cmb[:, :, 0:n], ALU.subtract))
            link(V.tensor_copy(cmb[:, :, 32:32 + n], rr2[:, :, 0:n]))
            V.tensor_tensor(cmb[:, :, 64:64 + n], rr2[:, :, 0:n], cmb[:, :, 32:32 + n], ALU.subtract).then_inc(S("f_cmb"), 1)

        def ffn(k, l, h):
            J = NJ[l]
            routed = l != 2
            if routed:
                router(l, h)
            else:
                x_lo((f"F{l}", h))
            for j in range(J + 1):
                g = G0[l] + h * J + j
                if routed and j:
                    if j == 1:
                        dve.wait_ge(S("f_cmbTp"), R0[l] + h + 1)
                        V.tensor_copy(cmbT[:, :], psb[0:96, 6, 0:HALF]).then_inc(S("f_cmbT"), 1)
                    i = j - 1
                    dve.wait_ge(S("f_m"), g)
                    dve.wait_ge(S("f_cw"), C0[l] + h * J + j)
                    V.tensor_tensor(sg[i % 2][:, :], sg[i % 2][:, :], ps[:, 6, :], ALU.mult).then_inc(S("f_h"), 1)
                if j < J:
                    dve.wait_ge(S("f_sg"), g + 1)
                    V.tensor_tensor(sg[j % 2][:, :], sg[j % 2][:, :], ps[:, 3 + 2 * (j % 2), :], ALU.mult).then_inc(S("f_m"), 1)
                if j:
                    i = j - 1
                    dve.wait_ge(S("f_hh"), g)
                    if j >= 3:
                        dve.wait_ge(S("f_down"), D0[l] + h * (J - 1) + j - 2)
                    V.tensor_tensor(hl[i % 2][:, :], sg[i % 2][:, :], hh[i % 2][:, :].bitcast(f32), ALU.subtract).then_inc(S("f_hl"), 1)
                if l == 1:
                    beside(j - 3, h)
            residual(f"F{l}", h, k)
            if l == 3:
                V.tensor_copy(mask_small[:, 10 + h:11 + h], epsc[:, :]).then_inc(S("x_final"), 1)
            done(f"F{l}", h, k)

        def beside(s, h):
            n0 = 17 * h
            if 0 <= s < 4:
                dve.wait_ge(S("am_qk"), 4 * h + s + 1)
                V.tensor_copy(am[:, 6:7], epsc[:, :]).then_inc(S("am_free"), 1)
                dve.wait_ge(S("am_free"), n0 + s + 1)
            elif 4 <= s <= 12:
                dve.wait_ge(S("am_psum"), n0 + s + 1)
                if s < 12:
                    link(V.tensor_reduce(am[:, 0:1], ps[:, 7, 0:DM], AX, ALU.max))
                if s > 4:
                    t = s - 5
                    last = V.tensor_copy(attT[2 + h][:, :, t // 4, (t % 4) * P:(t % 4 + 1) * P],
                                         ps[:, 7, DM:2 * DM].rearrange("p (c m) -> p c m", c=KC))
                    if s == 12:
                        last.then_inc(S("am_free"), 1)
                        return
                    link(last)
                V.tensor_scalar(am[:, 1:2], am[:, 0:1], -1.0, None, ALU.mult).then_inc(S("am_nb"), 1)
                dve.wait_ge(S("am_exp"), 8 * h + s - 3)
                link(V.reciprocal(am[:, 3:4], am[:, 2:3]))
                V.tensor_scalar(aP[:, :], aP[:, :], am[:, 3:4], None, ALU.mult).then_inc(S("am_pn"), 1)
                dve.wait_ge(S("am_pn"), 8 * h + s - 3)
                V.tensor_copy(am[:, 6:7], epsc[:, :]).then_inc(S("am_free"), 1)
                dve.wait_ge(S("am_free"), n0 + s + 1)
            elif h == 0 and 13 <= s <= 16:
                j = 2 * (s - 13)
                dve.wait_ge(S("am_psum"), s + 1)
                V.tensor_scalar(wmix[:, j:j + 2, :], ps[:, 7, :].rearrange("p (a d) -> p a d", a=2), float(I2) ** -0.5, None, ALU.mult).then_inc(S("am_free"), 1)
                dve.wait_ge(S("am_free"), s + 1)
            elif h == 0 and 17 <= s <= 22:
                st, sign = 1 << ((s - 17) // 2), (s - 17) % 2
                src, dst = (wmix[:, :, :], f2w[:, :, GU:WJ])[::1 if st != 2 else -1]
                for b in range(0, NJ[2], 2 * st):
                    last = V.tensor_tensor(dst[:, b + sign * st:b + (sign + 1) * st, :], src[:, b:b + st, :], src[:, b + st:b + 2 * st, :],
                                           ALU.subtract if sign else ALU.add)
                link(last)

        def attn_map(k, l, h):
            residual(f"A{l}", h, k)
            done(f"A{l}", h, k)

        for k, s in enumerate(ORDER):
            begin(dve, k)
            if s == "prep":
                prep(k)
            else:
                b, h = s
                {"M": ssm, "F0": ffn0, "A1": attn1, "F1": lambda k, h: ffn(k, 1, h), "F2": lambda k, h: ffn(k, 2, h),
                 "F3": lambda k, h: ffn(k, 3, h), "A2": lambda k, h: attn_map(k, 2, h),
                 "A3": lambda k, h: attn_map(k, 3, h)}[b](k, h)

    @block.gpsimd
    def _(pool):
        G = nc.gpsimd
        n_rstd = [0]

        def rstd_of():
            n_rstd[0] += 1
            pool.wait_ge(S("ln_var"), n_rstd[0])
            G.tensor_tensor(rstd[:, :], ve[:, :], mhalf[:, :], ALU.pow).then_inc(S("ln_rstd"), 1)

        def parts(h, i):
            g = h * HEADS + i
            pool.wait_ge(S("a_wh"), g + 1)
            G.tensor_tensor(awl[i % 2][:, 0:KC * P].rearrange("p (c n) -> p c n", c=KC), wq[:, :, i * P:(i + 1) * P],
                            awh[i % 2][:, 0:KC * P].bitcast(f32).rearrange("p (c n) -> p c n", c=KC), ALU.subtract)
            G.tensor_tensor(awl[i % 2][:, KC * P:AQ], wk[:, i * P:(i + 1) * P], awh[i % 2][:, KC * P:AQ].bitcast(f32),
                            ALU.subtract).then_inc(S("a_w"), 1)

        def value_parts(h, i):
            pool.wait_ge(S("a_voh"), h * HEADS + i + 1)
            G.tensor_tensor(vol[i % 2][:, :], wvo[:, i, :], voh[i % 2][:, :].bitcast(f32), ALU.subtract).then_inc(S("a_vol"), 1)

        def norms(h, i):
            g = h * HEADS + i
            pool.wait_ge(S("a_rks"), g + 1)
            if i:
                pool.wait_ge(S("a_ktok"), g)
            G.tensor_scalar(rk[:, :], rks[:, :], 1.0 / P, EPS, ALU.mult, ALU.add).then_inc(S("a_rk_var"), 1)
            pool.wait_ge(S("a_rk_var"), g + 1)
            G.tensor_tensor(rk[:, :], rk[:, :], mhalf[:, :], ALU.pow).then_inc(S("a_rk"), 1)

        def norm_q(h, i):
            g = h * HEADS + i
            pool.wait_ge(S("a_rqs"), g + 1)
            if i > 1:
                pool.wait_ge(S("a_exp"), g - 1)
            G.tensor_scalar(rq[i % 2][:, :], rqs[:, :], 1.0 / P, EPS, ALU.mult, ALU.add).then_inc(S("a_rq_var"), 1)
            pool.wait_ge(S("a_rq_var"), g + 1)
            G.tensor_tensor(rq[i % 2][:, :], rq[i % 2][:, :], mhalf[:, :], ALU.pow).then_inc(S("a_rq"), 1)

        def gu_lo(l, h, j):
            g = G0[l] + h * NJ[l] + j
            pool.wait_ge(S("f_wgh"), g + 1)
            G.tensor_tensor(wgl[j % 2][:, :], raw_w(l, j)[:, 0:GU], wgh[j % 2][:, :].bitcast(f32), ALU.subtract).then_inc(S("f_wg"), 1)

        def d_lo(l, h, j):
            g = G0[l] + h * NJ[l] + j
            pool.wait_ge(S("f_wdh"), g + 1)
            G.tensor_tensor(wdl[j % 3][:, :], raw_w(l, j)[:, GU:WJ], wdh[j % 3][:, :].bitcast(f32), ALU.subtract).then_inc(S("f_wd"), 1)

        pool.wait_ge(S("mhalf_set"), 1)
        rstd_of()
        rstd_of()
        for k, s in enumerate(ORDER):
            if s in ("prep", "maps"):
                continue
            b, h = s
            if b == "M":
                begin(pool, k)
                for n in range(NS):
                    g = h * NS + n
                    pool.wait_ge(S("m_Bcopy"), g + 1)
                    pool.wait_ge(S("m_du"), h + 1)
                    if n >= 2:
                        pool.wait_ge(S("m_h"), g - 1)
                    G.tensor_tensor(dBu[n % 2][:, :, :], du[:, :, :], bc(Bs[n % 2][:, :].unsqueeze(1), [P, 2, HALF]),
                                    ALU.mult).then_inc(S("m_dBu"), 1)
                pool.wait_ge(S("m_dBu"), (h + 1) * NS)
                G.tensor_copy(mask_small[:, 16:17], mhalf[:, 0:1]).then_inc(S("pool_step"), 1)
            elif b == "A1":
                begin(pool, k)
                parts(h, 0)
                parts(h, 1)
                norms(h, 0)
                norm_q(h, 0)
                for i in range(HEADS + 1):
                    g = h * HEADS + i
                    if i + 1 < HEADS:
                        norms(h, i + 1)
                    if i + 2 < HEADS:
                        parts(h, i + 2)
                    if i:
                        value_parts(h, i - 1)
                    if i + 1 < HEADS:
                        norm_q(h, i + 1)
                    if i < HEADS:
                        pool.wait_ge(S("a_ri"), g + 1)
                        G.tensor_tensor(Pm[i % 2][:, :, :], Pm[i % 2][:, :, :], bc(ri[:, :].unsqueeze(2), [P, TH, DM]), ALU.mult).then_inc(S("a_pn"), 1)
                pool.wait_ge(S("a_pn"), (h + 1) * HEADS)
                G.tensor_copy(mask_small[:, 16:17], mhalf[:, 0:1]).then_inc(S("pool_step"), 1)
            elif b[0] == "F" and b != "F0":
                begin(pool, k)
                l = int(b[1])
                J = NJ[l]
                if l != 2:
                    i = R0[l] + h + 1
                    pool.wait_ge(S("r_wh"), i)
                    G.tensor_tensor(wrl[:, :, :], fr[l][:, :, :], wrh[:, :, :].bitcast(f32), ALU.subtract).then_inc(S("r_w"), 1)
                gu_lo(l, h, 0)
                gu_lo(l, h, 1)
                d_lo(l, h, 0)
                for j in range(J):
                    if j + 2 < J:
                        gu_lo(l, h, j + 2)
                    if j + 1 < J:
                        d_lo(l, h, j + 1)
                pool.wait_ge(S("f_wd"), G0[l] + (h + 1) * J)
                G.tensor_copy(mask_small[:, 16:17], mhalf[:, 0:1]).then_inc(S("pool_step"), 1)
            if b != "F3":
                rstd_of()

    stack.close()


def kernel(**inputs):
    import numpy as np
    import ml_dtypes
    import concourse.bacc as bacc
    from concourse import mybir
    from concourse.bass_utils import run_bass_kernel_spmd

    f = {k: np.asarray(v) for k, v in inputs.items()}
    P = 128

    def rows(w):
        return w.reshape(-1, P, w.shape[1]).transpose(1, 0, 2)

    def pad_rows(w):
        n = -(-w.shape[0] // P) * P
        return np.concatenate([w, np.zeros((n - w.shape[0], w.shape[1]), w.dtype)])

    x = f["x"].reshape(1024, 256)
    ctx = f["ctx_1024"].reshape(1024, 128)
    small = np.zeros((P, 64), np.float32)
    small[:, 0:4] = f["g_xattn"][None, :]
    small[:, 4:8] = f["g_ffn"][None, :]
    small[:, 8:16] = rows(f["L0_xattn_conv_w"]).reshape(P, 8)
    small[:, 16:18] = f["L0_xattn_conv_b"].reshape(2, P).T
    small[:, 18:20] = f["L0_xattn_dt_proj_b"].reshape(2, P).T
    small[:, 20:52] = rows(f["L0_xattn_A_log"]).reshape(P, 32)
    small[:, 52:54] = f["L0_xattn_D"].reshape(2, P).T
    for c, name in enumerate(["L1_xattn_gq", "L1_xattn_gk", "L2_xattn_bq", "L2_xattn_bk", "L3_xattn_bq", "L3_xattn_bk"]):
        small[:, 54 + c] = f[name]

    def selector(owner, width, parts, rows_=96):
        s = np.zeros((rows_, width), np.float32)
        for p in parts:
            s[p + owner, np.arange(width)] = 1.0
        return s.astype(ml_dtypes.bfloat16)

    def experts(e, fdim, shared_width):
        n = e * fdim + shared_width
        owner = np.minimum(np.arange(n) // fdim, e)
        full = -(-n // P) * P
        s = np.zeros((96, full), ml_dtypes.bfloat16)
        s[:, :n] = selector(owner, n, (0, 32, 64))
        return s.reshape(96, -1, P)

    bc_owner = np.repeat(np.arange(32), P)
    had = np.array([[1.0]], np.float32)
    while had.shape[0] < P:
        had = np.block([[had, had], [had, -had]])

    xp = f["L0_xattn_x_proj_w"]
    bcw = np.concatenate([xp[8:40]] * 3).T

    def tiles(gate, up, down):
        n = -(-gate.shape[0] // P)
        g, u_, d = (pad_rows(w) for w in (gate, up, down))
        gu = [w.reshape(n, P, 2, P).transpose(3, 0, 2, 1).reshape(P, n, 256) for w in (g, u_)]
        return np.concatenate(gu + [d.reshape(n, P, 256).transpose(1, 0, 2)], 2)

    def experts_and_shared(gu, shared_gu, down, shared_down):
        w, ws = gu.shape[1] // 2, shared_gu.shape[0] // 2
        gate, up = (np.concatenate([gu[:, p * w:(p + 1) * w].reshape(-1, 256), shared_gu[p * ws:(p + 1) * ws]]) for p in (0, 1))
        return tiles(gate, up, np.concatenate([down.transpose(0, 2, 1).reshape(-1, 256), shared_down.T]))

    def router(w):
        return rows(np.concatenate([w, np.zeros((32 - w.shape[0], 256), w.dtype)]).T)

    wvT = f["L1_xattn_Wv"].reshape(128, 16, 128).transpose(2, 1, 0)
    wo = rows(f["L1_xattn_Wo"])
    f1w = experts_and_shared(f["L1_ffn_expert_gate_up"], f["L1_ffn_shared_gate_up"], f["L1_ffn_expert_down"], f["L1_ffn_shared_down"])

    arrays = {
        "x": rows(x), "ctk": rows(ctx), "ctxT": ctx.T, "small": small,
        "ident": np.eye(P, dtype=np.float32), "identb": np.eye(P, dtype=np.float32).astype(ml_dtypes.bfloat16),
        "had": had,
        "sel_bc": selector(bc_owner, 32 * P, (0, 32, 64)).reshape(96, 32, P),
        "sel1": experts(16, 176, 704), "sel3": experts(8, 176, 352),
        "w0raw": np.stack([rows(f["L0_ffn_w_gate"].T).reshape(P, -1), rows(f["L0_ffn_w_up"].T).reshape(P, -1),
                           rows(f["L0_ffn_w_down"].T).reshape(P, -1)], 1),
        "m_in": f["L0_xattn_in_proj_w"].T, "m_bc": rows(bcw), "m_dt": rows(xp[0:8].T), "m_dtw": f["L0_xattn_dt_proj_w"].T,
        "wq": rows(f["L1_xattn_Wq"]), "wk": f["L1_xattn_Wk"],
        "wvT0": wvT[:, :8], "wvT1": wvT[:, 8:], "wo0": wo[:, :8], "wo1": wo[:, 8:],
        "f1a": f1w[:, :22], "f1b": f1w[:, 22:],
        "f1r": router(np.concatenate([f["L1_ffn_gate_w"], f["L1_ffn_shared_gate_vec"]])),
        "am2q": f["L2_xattn_Wq"].T, "am2k": f["L2_xattn_Wk"].T, "am3q": f["L3_xattn_Wq"].T, "am3k": f["L3_xattn_Wk"].T,
        "f2w": tiles(f["L2_ffn_W1"], f["L2_ffn_W3"], f["L2_ffn_W2"].T),
        "f3w": experts_and_shared(f["L3_ffn_gate_up_weights"], f["L3_ffn_shared_gate_up"], f["L3_ffn_down_weights"], f["L3_ffn_shared_down"]),
        "f3r": router(f["L3_ffn_gate_weight"]),
    }
    nc = bacc.Bacc("TRN2", target_bir_lowering=False, num_devices=1)
    dram, given = {}, {}
    for name, a in arrays.items():
        a = np.ascontiguousarray(a)
        given["in_" + name] = a
        t = nc.dram_tensor("in_" + name, a.shape, mybir.dt.from_np(a.dtype), kind="ExternalInput").ap()
        dram[name] = t
    out = nc.dram_tensor("out_x", (P, 8, 256), mybir.dt.float32, kind="ExternalOutput").ap()
    flamingo_kernel(nc, dram, out)
    r = run_bass_kernel_spmd(nc, [given], core_ids=[0])
    return np.asarray(r.results[0]["out_x"]).transpose(1, 0, 2).reshape(4, 256, 256)
```

```python
def flamingo_kernel(nc, dram, out):
    import concourse.bass as bass
    from concourse import mybir
    from contextlib import ExitStack

    f32, bf16, f32r = mybir.dt.float32, mybir.dt.bfloat16, mybir.dt.float32r
    ALU, ACT = mybir.AluOpType, mybir.ActivationFunctionType
    AX = mybir.AxisListType.X

    P = 128
    DM, TOK, HALF = 256, 1024, 512
    NT, TH = TOK // P, HALF // P
    KC = DM // P
    NS = 16
    HEADS = 16
    HEADS2 = 2 * HEADS
    I0, I2 = 1024, 1024
    E1, F1, TOP1 = 16, 176, 4
    E3, F3, TOP3 = 8, 176, 2
    I1, I3 = 20 * F1, 10 * F3
    NJ = {1: -(-I1 // P), 2: I2 // P, 3: -(-I3 // P)}
    GU, WJ = 2 * KC * P, 2 * KC * P + DM
    J1A = 22
    MAGIC = 1.5 * 2.0 ** 23
    EPS = 1e-5
    SCALE = float(P) ** -0.5

    at = {"fixed": -(-nc.sbuf_base // 64) * 64}
    limit = nc.sbuf_usable_end

    def place(region, name, shape, dt=f32):
        size = 2 if dt == bf16 else 4
        for n in shape[1:]:
            size *= n
        size = -(-size // 64) * 64
        t = nc.alloc_sbuf_tensor_at(name, shape, dt, offset=at[region])
        at[region] += size
        assert at[region] <= limit, (name, at[region], limit)
        return t

    x = place("fixed", "x_res", [P, NT, DM])
    at["X0"] = at["fixed"]
    xn = [place("fixed", f"x_norm{h}", [P, TH, DM]) for h in range(2)]
    xnT = place("X0", "x_norm_T", [P, KC, HALF])
    xTh = place("fixed", "x_norm_T_hi", [P, KC, HALF], f32r)
    xTl = place("fixed", "x_norm_T_lo", [P, KC, HALF], f32r)
    ctxT = place("fixed", "ctx_T", [P, TOK])
    at["X1"] = at["fixed"]
    ctk = place("fixed", "ctx_tok", [P, NT, P])
    xTh1 = place("X1", "x_norm_T1_hi", [P, KC, HALF], f32r)
    small = place("fixed", "small_params", [P, 64])
    ident = place("fixed", "ident_f", [P, P])
    identb = place("fixed", "ident_b", [P, P], bf16)
    had = place("fixed", "hadamard", [P, P])
    ones = place("fixed", "ones", [P, P])
    tg = place("fixed", "tanh_gates", [P, 8])
    negA = place("fixed", "neg_A", [P, 2, NS])
    wabs = place("fixed", "w_abs", [P, 3])
    wscale = place("fixed", "w_scale", [P, 3])
    winv = place("fixed", "w_inv", [P, 3])
    epsc = place("fixed", "eps_col", [P, 1])
    magic = place("fixed", "magic_col", [P, 1])
    nmagic = place("fixed", "minus_magic_col", [P, 1])
    mhalf = place("fixed", "minus_half", [P, TH])
    gqk = place("fixed", "g_qk", [P, 1])
    bst = place("fixed", "bn_st", [P, TH, 6])
    mv = place("fixed", "bn_mv", [P, TH, 2])
    ve = place("fixed", "var_eps", [P, TH])
    rstd = place("fixed", "rstd", [P, TH])
    scratch = place("fixed", "scratch", [P, 64])
    qs = [place("fixed", f"q_scales{h}", [P, 8 * TH]) for h in range(2)]
    qt = [place("fixed", f"q_tile_scales{i}", [P, 4]) for i in range(2)]

    at["A1"] = at["A2"] = at["fixed"]
    wq = place("A1", "a1_wq", [P, KC, HEADS * P])
    wk = place("A1", "a1_wk", [P, HEADS * P])
    wvo = place("A1", "a1_wvo", [P, HEADS, DM])
    f2w = place("A2", "f2_w", [P, NJ[2], WJ])
    attT = {l: place("A2", f"att_T{l}", [P, KC, 2, HALF]) for l in (2, 3)}
    at["AW2"], at["AW3"] = at["A2"] - 2 * KC * 4 * HALF - 2 * P * 4, at["A2"] - 2 * P * 4
    aw = [place(f"AW{l}", f"am_w{n}{l}", [P, P]) for l in (2, 3) for n in "qk"]
    at["B"] = max(at["A1"], at["A2"])
    at["B0"] = at["B1"] = at["B3"] = at["B"]
    sel = {1: place("B1", "sel1", [96, NJ[1], P], bf16)}
    fr = {1: place("B1", "f1_router", [P, KC, 32])}
    f1a = place("B1", "f1_wa", [P, J1A, WJ])
    at["B1a"] = at["B1"]
    f1b = place("B1", "f1_wb", [P, NJ[1] - J1A, WJ])
    f3w = place("B3", "f3_w", [P, NJ[3], WJ])
    sel[3] = place("B3", "sel3", [96, NJ[3], P], bf16)
    fr[3] = place("B3", "f3_router", [P, KC, 32])
    w0raw = place("B0", "w0_raw", [P, 3, KC * I0])
    at["Bp"] = at["Bm"] = at["Bf"] = at["B0"]
    xpad0 = place("Bm", "m_xpad0", [P, 2, 2, DM + 3])
    u = [place("Bm", f"m_u{h}", [P, 2, HALF]) for h in range(2)]
    dlt = [place("Bm", f"m_delta{h}", [P, 2, HALF]) for h in range(2)]
    du0 = place("Bm", "m_du0", [P, 2, HALF])
    dA = [place("Bm", f"m_dA{i}", [P, 2, HALF]) for i in range(2)]
    dBu = [place("Bm", f"m_dBu{i}", [P, 2, HALF]) for i in range(2)]
    Bs = [place("Bm", f"m_Bs{i}", [P, HALF]) for i in range(3)]
    hst0 = place("Bm", "m_h", [P, 2, HALF])
    hC = [place("Bm", f"m_hC{i}", [P, 2, HALF]) for i in range(2)]
    bcs = [place("Bm", f"m_bc_split{h}", [96, HALF], bf16) for h in range(2)]
    zinv = place("Bm", "m_inv1", [P, 2, HALF])
    hst = [hst0, zinv]
    dts = zinv[0:8, 0, :]
    m_in = place("Bm", "m_in_w", [P, DM])
    m_bc = place("Bm", "m_bc_w", [P, 2, 96])
    m_dt = place("Bm", "m_dt_w", [P, 2, 8])
    m_dtw = place("Bm", "m_dtw", [8, DM])
    xq = [place("Bf", f"q_x{h}", [P, TH, DM], bf16) for h in range(2)]
    xqa = place("Bf", "q_xa", [P, TH, DM])
    xqT = [place("Bf", f"q_xT{h}", [P, KC, HALF], bf16) for h in range(2)]
    sg0 = [place("Bf", f"q_sg{i}", [P, I0]) for i in range(2)]
    h0 = [place("Bf", f"q_h{i}", [P, I0]) for i in range(2)]
    h0a = [place("Bf", f"q_ha{i}", [P, I0]) for i in range(2)]
    hq = place("Bf", "q_hq", [P, I0], bf16)
    hqT = place("Bf", "q_hqT", [P, I0 // P, P], bf16)
    at["W"] = max(at["B1"], at["B3"], at["Bm"], at["Bf"])
    at["W0"] = at["Wd"] = at["W1"] = at["W2"] = at["W4"] = at["W"]
    w0q = [place("W0", f"w0_quant{i}", [P, KC * I0], bf16) for i in range(3)]
    w_values = place("Wd", "w_abs_values", [P, KC * I0])
    wvT = place("W0", "a1_wvT", [P, HEADS // 2, P])
    sel_bc = place("W0", "sel_bc", [96, 2 * NS, P], bf16)
    wo = place("W0", "a1_wo", [P, HEADS // 2, DM])
    du = [du0, place("W0", "m_du1", [P, 2, HALF])]
    xpad = [xpad0, place("W0", "m_xpad1", [P, 2, 2, DM + 3])]
    Pm = [place("W1", f"a_P{i}", [P, TH, DM]) for i in range(2)]
    PT = place("W1", "a_PT", [P, 2, HALF])
    qh, ql = ([place("W1", f"a_qT_{n}{i}", [P, HALF], f32r) for i in range(2)] for n in ("hi", "lo"))
    kh, kl = (place("W1", f"a_kT_{n}", [P, HALF], f32r) for n in ("hi", "lo"))
    ah, al = (place("W1", f"a_AC_{n}", [P, HALF], f32r) for n in ("hi", "lo"))
    qsq = place("W1", "a_qsq", [P, HALF])
    ksq = qsq
    xTa = [place("W1", f"a_xT_{n}1", [P, KC, HALF], f32r) for n in ("hi", "lo")]
    ktok = place("W1", "a_k_tok", [P, HALF])
    rk, rks, rqs, nb, mx, rs, ri = (place("W1", f"a_{n}", [P, TH]) for n in
                                    ("rk", "k_sum", "q_sum", "neg_max", "max", "row_sum", "row_inv"))
    rq = [place("W1", f"a_rq{i}", [P, TH]) for i in range(2)]
    ch, cl = (place("B1a", f"a_ctxT_{n}", [P, TOK], f32r) for n in ("hi", "lo"))
    AQ = KC * P + P
    awh, awl = ([place("B1a", f"a_w_{n}{i}", [P, AQ], f32r) for i in range(2)] for n in ("hi", "lo"))
    voh, vol = ([place("B1a", f"a_wvo_{n}{i}", [P, DM], f32r) for i in range(2)] for n in ("hi", "lo"))
    assert at["B1a"] <= at["B1"]
    sg = [place("W2", f"f_silu{i}", [P, HALF]) for i in range(2)]
    hh, hl = ([place("W2", f"f_h_{n}{i}", [P, HALF], f32r) for i in range(2)] for n in ("hi", "lo"))
    wgh, wgl = ([place("W2", f"f_wgu_{n}{i}", [P, GU], f32r) for i in range(2)] for n in ("hi", "lo"))
    wdh, wdl = ([place("W2", f"f_wd_{n}{i}", [P, DM], f32r) for i in range(3)] for n in ("hi", "lo"))
    wrh, wrl = (place("W2", f"r_w_{n}", [P, KC, 32], f32r) for n in ("hi", "lo"))
    cmb = place("W2", "r_combine", [P, TH, 96], bf16)
    cmbT = [place("W2", f"r_combine_T{i}", [96, HALF], bf16) for i in range(2)]
    xTl1 = place("W2", "x_norm_T1_lo", [P, KC, HALF], f32r)
    rl = place("W2", "r_logits", [P, TH, 24])
    rp = place("W2", "r_probs", [P, TH, 24])
    rr = place("W2", "r_replaced", [P, TH, 24])
    rt = place("W2", "r_top", [P, TH, 8])
    rw = place("W2", "r_weights", [P, TH, 24])
    rc = place("W2", "r_columns", [P, 4, TH])
    aP = place("W2", "am_P", [P, DM])
    am = place("W2", "am_cols", [P, 8])
    at["W3"] = at["W2"]
    aqk = [place("W2", f"am_{n}", [P, HALF]) for n in "qk"]
    wmix = place("W3", "w2_mix", [P, NJ[2] // 2, DM])
    xTp = [(xTh, xTl), (xTh1, xTl1)]

    SOFTPLUS = [(dA[0][:, :, :], dBu[0][:, :, :], hC[0][:, :, :], dA[1][:, :, :]),
                (hst0[:, :, :], dBu[1][:, :, :], hC[1][:, :, :], zinv[:, :, :])]

    BC_PARTS = [[Bs[h][0:96, 256 * p:256 * (p + 1)].bitcast(bf16) for p in range(2)] for h in range(2)]

    c_gate, c_cw, c_cb, c_dtb, c_al, c_D, c_gq, c_gk, c_b = 0, 8, 16, 18, 20, 52, 54, 55, 56

    stack = ExitStack()
    ps = stack.enter_context(nc.psum_tensor("psum", [P, 8, 512], f32))
    psb = ps[:, :, :].bitcast(bf16)
    sems = {}

    def S(name):
        if name not in sems:
            sems[name] = stack.enter_context(nc.semaphore(name))
        return sems[name]

    LOADS = [
        ("ctxT", ctxT, 0, "ctx"), ("m_in", m_in, 0, "ctx"), ("small", small, 0, "small"),
        ("m_bc", m_bc, 0, "ssm"), ("m_dt", m_dt, 0, "ssm"), ("m_dtw", m_dtw, 0, "ssm"), ("x", x, 0, "x"),
        ("sel_bc", sel_bc, 0, "sel_bc"),
        ("ident", ident, 0, "ident"), ("w0raw", w0raw, 0, "w0"), ("wvT0", wvT, 0, "value"), ("wo0", wo, 0, "value"),
        ("identb", identb, 0, "const"), ("ctk", ctk, 0, "const"), ("had", had, 0, "const"),
        ("wk", wk, 0, "qk"), ("wq", wq, 0, "qk"),
        ("wvT1", wvT, 0.5, "value"), ("wo1", wo, 0.5, "value"),
        ("sel1", sel[1], 2, "route"), ("f1r", fr[1], 2, "route"), ("f1a", f1a, 2, "f1a"),
        ("f1b", f1b, 3, "f1b"), ("am2q", aw[0], 3, "map"), ("am2k", aw[1], 3, "map"), ("f2w", f2w, 3, "f2"),
        ("am3q", aw[2], 3, "map"), ("am3k", aw[3], 3, "map"),
        ("sel3", sel[3], 4, "route"), ("f3r", fr[3], 4, "route"), ("f3w", f3w, 4, "f3"),
    ]
    load_count = {name: (group, 16 * sum(1 for _, _, s2, g2 in LOADS if g2 == group and s2 <= step))
                  for name, _, step, group in LOADS}

    ORDER = ["M", "F0", "A1", "F"]
    POOL_STEPS = [k for k, s in enumerate(ORDER) if s in ("M", "A1")]

    def begin(eng, k):
        if k:
            eng.wait_ge(S("pe_step"), k)
            eng.wait_ge(S("act_step"), k)
            eng.wait_ge(S("dve_step"), k)
            done = sum(1 for s in POOL_STEPS if s < k)
            if done:
                eng.wait_ge(S("pool_step"), done)

    def loaded(eng, *names):
        for n in names:
            group, count = load_count[n]
            eng.wait_ge(S("ld_" + group), count)

    def chain(eng, sem):
        n = [0]

        def link(ins):
            n[0] += 1
            ins.then_inc(S(sem), 1)
            eng.wait_ge(S(sem), n[0])
        return link

    def bc(ap, shape):
        return ap.to_broadcast(shape)

    gate_col = {"M": 0, "F0": 4, "A1": 1, "F1": 5, "A2": 2, "F2": 6, "A3": 3, "F3": 7}
    ln_index = {s: i + 1 for i, s in enumerate([(b, h) for b in ("M", "F0", "A1", "F1") for h in range(2)])}
    for l in (2, 3):
        for h in range(2):
            ln_index[(f"A{l}", h)] = len(ln_index) + 1
            ln_index[(f"F{l}", h)] = len(ln_index) + 1

    G0 = {1: 0, 2: 2 * NJ[1], 3: 2 * (NJ[1] + NJ[2])}
    FT = [(l, h, 2 * (l - 1) + h, j) for l in (1, 2, 3) for h in range(2) for j in range(NJ[l])]
    FN = len(FT)
    FIRST = [G0[l] + h * NJ[l] for l in (1, 2, 3) for h in range(2)] + [FN]
    ROUTED = [2 * NJ[1] if 2 * NJ[1] <= g < G0[3] else g if g < 2 * NJ[1] else g - 2 * NJ[2] for g in range(FN + 1)]

    beside = {}

    def put(place_, *what):
        beside.setdefault(place_, []).append(what)

    def put_norm(p, l, h, d=1):
        put(p, "stats", (f"F{l}", h))
        put(p + d, "normalise", (f"F{l}", h))
        put(p + 2 * d + 1, "xT", l, h, 0)
        put(p + 3 * d + 1, "xT", l, h, 1)
        if l != 2:
            put(p + 4 * d + 1, "logits", l, h)
            put(p + 5 * d + 1, "route", l, h)
            put(p + 7 * d + 1, "cmbT", l, h)

    def put_attention(p, l, h, d=1):
        put(p - 1, "residual", l - 1, h)
        put(p, "stats", (f"A{l}", h))
        put(p + 2 * d, "normalise", (f"A{l}", h))
        put(p + 3 * d, "aT", l, h, 0)
        put(p + 4 * d, "aT", l, h, 1)
        put(p + 5 * d, "apply", l, h, 0)
        put(p + 6 * d, "apply", l, h, 1)
        put_norm(p + 6 * d, l, h, d)

    def put_map(p, l):
        for s_ in range(14):
            put(p, "map", l, s_)
            if 2 <= s_ % 7 < 6:
                put(p + 1, "map_norm", l, s_)
                p += 2
            p += 2

    put(-1, "logits", 1, 0)
    put(-1, "route", 1, 0)
    put(2, "cmbT", 1, 0)
    put_norm(3, 1, 1, 1)
    put_map(12, 2)
    for s_ in range(4):
        put(2 * FIRST[1] - 3 + 2 * s_, "mix", 2 * s_)
    put(2 * FIRST[1] + 6, "butterfly", 2)
    put(2 * FIRST[1] + 10, "butterfly", 4)
    put_attention(2 * FIRST[1] + 3, 2, 0, 4)
    put_map(2 * FIRST[1] + 12, 3)
    put_attention(2 * FIRST[2] + 3, 2, 1)
    put_attention(2 * FIRST[3] + 3, 3, 0)
    put(2 * FIRST[3] + 2, "router_w", 3)
    put_attention(2 * FIRST[4] + 3, 3, 1, 2)
    put(2 * FIRST[5] + 3, "residual", 3, 0)
    bank7 = [w for p in sorted(beside) for w in beside[p] if w[0] in ("xT", "logits", "cmbT", "map", "mix", "aT", "apply")]

    VALUE_AT = [2 * v for v in range(HEADS // 2)] + [NS + 6 + v for v in range(HEADS // 2)]

    def raw_w(l, j):
        if l == 1:
            return f1a[:, j, :] if j < J1A else f1b[:, j - J1A, :]
        return (f2w if l == 2 else f3w)[:, j, :]

    block = stack.enter_context(nc.Block())

    @block.sync
    def _(sp):
        reached = 0
        for name, dst, step, group in LOADS:
            if step > reached:
                if step == 4:
                    sp.wait_ge(S("f_wg"), G0[2])
                    sp.wait_ge(S("f_wd"), G0[2])
                    sp.wait_ge(S("f_cw"), G0[2])
                elif step == 0.5:
                    sp.wait_ge(S("wvo_copied"), HEADS // 2)
                else:
                    begin(sp, step)
                reached = step
            full = tuple(slice(None) for _ in dst.shape)
            sp.dma_start(dst[full], dram[name]).then_inc(S("ld_" + group), 16)
        for h in range(2):
            sp.wait_ge(S("x_final"), h + 1)
            sp.dma_start(out[:, h * TH:(h + 1) * TH, :], x[:, h * TH:(h + 1) * TH, :]).then_inc(S("stored"), 16)
        sp.wait_ge(S("stored"), 32)

    @block.tensor
    def _(pe):
        mm = nc.tensor.matmul

        def transpose_norm(h, s, banks=(2, 3)):
            pe.wait_ge(S("ln_done"), ln_index[s])
            for c in range(KC):
                for t in range(TH):
                    last = nc.tensor.transpose(ps[:, banks[c], t * P:(t + 1) * P], xn[h][:, t, c * P:(c + 1) * P], ident[:, :])
            last.then_inc(S("xT_psum"), 1)

        def mm3(out, wh, wl, xh, xl, start, stop, **kw):
            mm(out, wh, xh, start=start, stop=False, **kw)
            mm(out, wh, xl, start=False, stop=False, **kw)
            return mm(out, wl, xh, start=False, stop=stop, **kw)

        def ssm(k):
            loaded(pe, "ctxT", "m_in")
            for h in range(2):
                for e in range(2):
                    last = mm(ps[:, 4 * h + e, :], m_in[:, e * P:(e + 1) * P], ctxT[:, h * HALF:(h + 1) * HALF], start=True, stop=True)
                last.then_inc(S("m_x"), 1)
            loaded(pe, "m_bc", "m_dt", "m_dtw")
            for h in range(2):
                pe.wait_ge(S("m_u"), h + 1)
                for e in range(2):
                    mm(ps[0:96, 2 + 4 * h, :], m_bc[:, e, :], u[h][:, e, :], start=e == 0, stop=e == 1)
                for e in range(2):
                    last = mm(ps[0:8, 3 + 4 * h, :], m_dt[:, e, :], u[h][:, e, :], start=e == 0, stop=e == 1)
                last.then_inc(S("m_dbl"), 1)
                pe.wait_ge(S("m_dts"), h + 1)
                for e in range(2):
                    last = mm(ps[:, 4 * h + e, :], m_dtw[:, e * P:(e + 1) * P], dts[:, :], start=True, stop=True)
                last.then_inc(S("m_dpre"), 1)
            pe.wait_ge(S("m_bcs"), 2)
            pe.wait_ge(S("m_xs"), 2)
            loaded(pe, "sel_bc", "ident")

            def broadcast_B(g):
                if g >= 2:
                    pe.wait_ge(S("m_Bcopy"), g - 1)
                mm(ps[:, 2 + g % 2, :], sel_bc[:, g % NS, :], bcs[g // NS][:, :], start=True, stop=True).then_inc(S("m_B"), 1)

            def output(h):
                pe.wait_ge(S("m_yz"), h + 1)
                for t in range(TH):
                    b, lb = t // 2, t % 2
                    for e in range(2):
                        last = nc.tensor.transpose(ps[:, 6 + t // 2, (t % 2) * DM + e * P:(t % 2) * DM + (e + 1) * P],
                                                   u[h][:, e, b * DM + lb * P:b * DM + (lb + 1) * P], ident[:, :])
                return last

            loaded(pe, "wvT0", "wo0")
            broadcast_B(0)
            broadcast_B(1)
            broadcast_B(2)
            for g in range(2 * NS + 1):
                if g + 3 < 2 * NS:
                    broadcast_B(g + 3)
                if g < 2 * NS:
                    if g >= 2:
                        pe.wait_ge(S("m_hC"), g - 1)
                    mm(ps[:, 4 + g % 2, :], sel_bc[:, NS + g % NS, :], bcs[g // NS][:, :], start=True, stop=True).then_inc(S("m_C"), 1)
                if g:
                    pe.wait_ge(S("m_hC"), g)
                    if g == NS + 1:
                        pe.wait_ge(S("m_y_read"), 1)
                    for e in range(2):
                        last = mm(ps[:, e, :], ident[:, :], hC[(g - 1) % 2][:, e, :], start=(g - 1) % NS == 0, stop=(g - 1) % NS == NS - 1)
                    last.then_inc(S("m_y"), 1)
                if g in VALUE_AT:
                    v = VALUE_AT.index(g)
                    if v == HEADS // 2:
                        loaded(pe, "wvT1", "wo1")
                        pe.wait_ge(S("m_res"), 1)
                    if v >= 2:
                        pe.wait_ge(S("wvo_copied"), v - 1)
                    if v == 3:
                        pe.wait_ge(S("w_scales"), 1)
                    mm(ps[:, 6 + v % 2, 0:DM], wvT[:, v % (HEADS // 2), :], wo[:, v % (HEADS // 2), :], start=True, stop=True).then_inc(S("wvo_psum"), 1)
                if g == 5:
                    pe.wait_ge(S("wvo_copied"), 2)
                    pe.wait_ge(S("wabs_part"), 1)
                    pe.wait_ge(S("ones_set"), 1)
                    mm(ps[:, 7, 256:259], ones[:, :], wabs[:, 0:3], start=True, stop=True).then_inc(S("wabs_sum"), 1)
                if g == NS + 2:
                    pe.wait_ge(S("wvo_copied"), HEADS // 2)
                    output(0).then_inc(S("m_out"), 1)
            pe.wait_ge(S("wvo_copied"), HEADS)
            output(1).then_inc(S("pe_step"), 1)

        def ffn0(k):
            def inputs(h):
                pe.wait_ge(S("q_xq"), h + 1)
                for c in range(KC):
                    for t in range(TH):
                        last = nc.tensor.transpose(psb[:, 2, c * HALF + t * P:c * HALF + (t + 1) * P],
                                                   xq[h][:, t, c * P:(c + 1) * P], identb[:, :])
                last.then_inc(S("q_xTp"), 1)

            def gate_up(t):
                h = t // TH
                if t % TH == 0:
                    pe.wait_ge(S("q_xT"), h + 1)
                for n in range(2):
                    for w, b0, free in ((0, 3, "q_sg"), (1, 5, "q_h")):
                        if t == n == 0:
                            pe.wait_ge(S("w0_ready"), w + 1)
                        if t:
                            pe.wait_ge(S(free), 2 * (t - 1) + n + 1)
                        for c in range(KC):
                            last = mm(ps[:, b0 + n, :], xqT[h][:, c, (t % TH) * P:(t % TH + 1) * P],
                                      w0q[w][:, c * I0 + n * 512:c * I0 + (n + 1) * 512], start=c == 0, stop=c == KC - 1)
                        last.then_inc(S("q_gate" if w == 0 else "q_up"), 1)

            def down(t):
                pe.wait_ge(S("q_hT"), t + 1)
                if t >= 2:
                    pe.wait_ge(S("q_out"), t - 1)
                if t == 0:
                    pe.wait_ge(S("w0_ready"), 3)
                for j in range(I0 // P):
                    last = mm(ps[:, t % 2, 0:DM], hqT[:, j, :], w0q[2][:, j * DM:(j + 1) * DM], start=j == 0, stop=j == I0 // P - 1)
                last.then_inc(S("q_down"), 1)

            def hidden_T(t):
                pe.wait_ge(S("q_hq"), t + 1)
                if t:
                    pe.wait_ge(S("q_hT"), t)
                for j in range(I0 // P):
                    last = nc.tensor.transpose(psb[:, 7, j * P:(j + 1) * P], hq[:, j * P:(j + 1) * P], identb[:, :])
                last.then_inc(S("q_hTp"), 1)

            loaded(pe, "identb")
            inputs(0)
            for t in range(NT + 3):
                if t == 3:
                    inputs(1)
                if t < NT:
                    gate_up(t)
                if t >= 3:
                    down(t - 3)
                if 2 <= t < NT + 2:
                    hidden_T(t - 2)
            pe.wait_ge(S("q_down"), NT)
            nc.tensor.transpose(psb[:, 2, 0:P], identb[:, :], identb[:, :]).then_inc(S("pe_step"), 1)

        def attn1(k):
            loaded(pe, "wq", "wk", "ctk")
            transpose_norm(0, ("A1", 0), (6, 7))
            pe.wait_ge(S("xT_ready"), 1)
            pe.wait_ge(S("a_ctx"), 1)

            def keys_queries(i):
                hi, lo = awh[i % 2], awl[i % 2]
                xh, xl = (xTh, xTl) if i < HEADS else xTa
                pe.wait_ge(S("a_w"), i + 1)
                if i:
                    pe.wait_ge(S("a_kT"), i)
                if i == HEADS:
                    pe.wait_ge(S("xT_ready"), 2)
                for t in range(TH):
                    sl = slice((i // HEADS) * HALF + t * P, (i // HEADS) * HALF + (t + 1) * P)
                    ksl = slice(t * P, (t + 1) * P)
                    last = mm3(ps[:, 7, ksl], ch[:, sl], cl[:, sl], hi[:, KC * P:AQ], lo[:, KC * P:AQ], True, True)
                last.then_inc(S("a_k"), 1)
                if i:
                    pe.wait_ge(S("a_rqs"), i)
                for c in range(KC):
                    last = mm3(ps[:, 6, :], hi[:, c * P:(c + 1) * P], lo[:, c * P:(c + 1) * P], xh[:, c, :], xl[:, c, :],
                               c == 0, c == KC - 1)
                last.then_inc(S("a_q"), 1)

            def norm_transpose(i):
                pe.wait_ge(S("a_qsq"), i + 1)
                pe.wait_ge(S("a_ql"), i + 1)
                for t in range(TH):
                    last = mm(ps[:, 6, t:t + 1], qsq[:, t * P:(t + 1) * P], ones[:, 0:1], start=True, stop=True)
                last.then_inc(S("a_qn"), 1)
                pe.wait_ge(S("a_ktok"), i + 1)
                for t in range(TH):
                    last = nc.tensor.transpose(ps[:, 7, t * P:(t + 1) * P], ktok[:, t * P:(t + 1) * P], ident[:, :])
                last.then_inc(S("a_kt"), 1)

            keys_queries(0)
            norm_transpose(0)
            for i in range(HEADS2 + 2):
                if i + 1 < HEADS2:
                    keys_queries(i + 1)
                if i == 2:
                    pe.wait_ge(S("xT_ready"), 2)
                if i >= 2:
                    pe.wait_ge(S("a_al"), i - 1)
                    pe.wait_ge(S("a_vol"), i - 1)
                    if i == HEADS + 2:
                        pe.wait_ge(S("a_res"), 1)
                    for t in range(TH):
                        sl = slice(t * P, (t + 1) * P)
                        last = mm3(ps[:, t // 2, (t % 2) * DM:(t % 2 + 1) * DM], ah[:, sl], al[:, sl],
                                   voh[i % 2][:, :], vol[i % 2][:, :],
                                   (i - 2) % HEADS == 0 and t % 2 == 0, (i - 2) % HEADS == HEADS - 1, skip_group_check=True)
                    last.then_inc(S("a_out"), 1)
                if i == 0:
                    transpose_norm(1, ("A1", 1), (0, 1))
                if i < HEADS2:
                    pe.wait_ge(S("a_kT"), i + 1)
                    pe.wait_ge(S("a_ql"), i + 1)
                    if i:
                        pe.wait_ge(S("a_exp"), i)
                    for t in range(TH):
                        sl = slice(t * P, (t + 1) * P)
                        kv = slice((t // 2) * DM, (t // 2 + 1) * DM)
                        last = mm3(ps[:, 2 + t // 2, (t % 2) * DM:(t % 2 + 1) * DM], qh[i % 2][:, sl], ql[i % 2][:, sl],
                                   kh[:, kv], kl[:, kv], True, True)
                    last.then_inc(S("a_s"), 1)
                if 1 <= i <= HEADS2:
                    pe.wait_ge(S("a_pn"), i)
                    if i > 1:
                        pe.wait_ge(S("a_al"), i - 1)
                    for t in range(TH):
                        b, qb = t // 2, t % 2
                        for kv in range(2):
                            last = nc.tensor.transpose(ps[:, 4 + b, kv * DM + qb * P:kv * DM + (qb + 1) * P],
                                                       Pm[(i - 1) % 2][:, t, kv * P:(kv + 1) * P], ident[:, :])
                    last.then_inc(S("a_pt"), 1)
                if i == HEADS2:
                    pe.wait_ge(S("a_exp"), HEADS2)
                    transpose_norm(0, ("F1", 0), (2, 3))
                if i + 1 < HEADS2:
                    norm_transpose(i + 1)
                if 1 <= i <= HEADS2:
                    pe.wait_ge(S("a_pts"), i)
                    for b in range(2):
                        for kv in range(2):
                            last = mm(ps[:, 4, b * DM:(b + 1) * DM], ctk[:, ((i - 1) // HEADS) * TH + 2 * b + kv, :],
                                      PT[:, b, kv * DM:(kv + 1) * DM], start=kv == 0, stop=kv == 1)
                    last.then_inc(S("a_ac"), 1)
            pe.wait_ge(S("a_out"), HEADS2)
            nc.tensor.transpose(psb[:, 6, 0:P], identb[:, :], identb[:, :]).then_inc(S("pe_step"), 1)

        def use_bank7(w):
            n = bank7.index(w)
            if n:
                pe.wait_ge(S("b7_free"), n)

        def side(place_):
            for w in beside.get(place_, ()):
                kind = w[0]
                if kind == "xT" or kind == "aT":
                    _, l, h, c = w
                    use_bank7(w)
                    pe.wait_ge(S("ln_done"), ln_index[("F" if kind == "xT" else "A") + str(l), h])
                    for t in range(TH):
                        last = nc.tensor.transpose(ps[:, 7, t * P:(t + 1) * P], xn[1][:, t, c * P:(c + 1) * P], ident[:, :])
                elif kind == "logits":
                    _, l, h = w
                    xh, xl = xTp[h]
                    use_bank7(w)
                    if place_ == -1:
                        pe.wait_ge(S("xT_ready"), 3)
                    pe.wait_ge(S("r_w"), 1 if l == 1 else 2)
                    for t in range(TH):
                        sl = slice(t * P, (t + 1) * P)
                        for c in range(KC):
                            last = mm3(ps[:, 7, t * 32:(t + 1) * 32], xh[:, c, sl], xl[:, c, sl], wrh[:, c, :], wrl[:, c, :],
                                       c == 0, c == KC - 1)
                elif kind == "cmbT":
                    _, l, h = w
                    use_bank7(w)
                    pe.wait_ge(S("f_cmb"), (0 if l == 1 else 2) + h + 1)
                    for t in range(TH):
                        last = nc.tensor.transpose(psb[0:96, 7, t * P:(t + 1) * P], cmb[:, t, :], identb[:, :])
                elif kind == "map":
                    _, l, s_ = w
                    b, s_ = s_ // 7, s_ % 7
                    use_bank7(w)
                    if s_ < 2:
                        loaded(pe, "am3k")
                        last = mm(ps[:, 7, :], aw[2 * (l - 2) + s_][:, :], ctxT[:, b * HALF:(b + 1) * HALF], start=True, stop=True)
                    if s_ > 2:
                        pe.wait_ge(S("am_pn"), 8 * (l - 2) + 4 * b + s_ - 2)
                        for kv in range(2):
                            last = nc.tensor.transpose(ps[:, 7, DM + kv * P:DM + (kv + 1) * P], aP[:, kv * P:(kv + 1) * P], ident[:, :])
                    if 2 <= s_ < 6:
                        t = s_ - 2
                        last = mm(ps[:, 7, 0:DM], aqk[0][:, t * P:(t + 1) * P], aqk[1][:, (t // 2) * DM:(t // 2 + 1) * DM],
                                  start=True, stop=True)
                elif kind == "mix":
                    j = w[1]
                    use_bank7(w)
                    loaded(pe, "had", "f2w")
                    mm(ps[:, 7, 0:DM], had[:, :], f2w[:, j, GU:WJ], start=True, stop=True)
                    last = mm(ps[:, 7, DM:2 * DM], had[:, :], f2w[:, j + 1, GU:WJ], start=True, stop=True)
                elif kind == "apply":
                    _, l, h, b = w
                    use_bank7(w)
                    for t in (2 * b, 2 * b + 1):
                        for c in range(KC):
                            last = mm(ps[:, 7, (t % 2) * DM:(t % 2 + 1) * DM], xnT[:, c, t * P:(t + 1) * P],
                                      attT[l][:, c, h, b * DM:(b + 1) * DM], start=c == 0, stop=c == KC - 1)
                else:
                    continue
                last.then_inc(S("b7_put"), 1)

        def ffns(k):
            def gate_up(g):
                l, h, q, j = FT[g]
                xh, xl = xTp[h]
                if g == 0:
                    pe.wait_ge(S("xT_ready"), 3)
                elif j == 0:
                    pe.wait_ge(S("b7_free"), bank7.index(("xT", l, h, 1)) + 1)
                pe.wait_ge(S("f_wg"), g + 1)
                if g >= 2:
                    pe.wait_ge(S("f_sg"), g - 1)
                    pe.wait_ge(S("f_m"), g - 1)
                for b in range(2):
                    for c in range(KC):
                        sl = slice((b * KC + c) * P, (b * KC + c + 1) * P)
                        last = mm3(ps[:, 2 + 2 * (g % 2) + b, :], wgh[g % 2][:, sl], wgl[g % 2][:, sl], xh[:, c, :], xl[:, c, :],
                                   c == 0, c == KC - 1)
                last.then_inc(S("f_gu"), 1)

            def combine(g):
                l, h, q, j = FT[g]
                if l == 2:
                    return
                if j == 0:
                    pe.wait_ge(S("b7_free"), bank7.index(("cmbT", l, h)) + 1)
                    loaded(pe, f"sel{l}")
                if ROUTED[g]:
                    pe.wait_ge(S("f_h"), ROUTED[g])
                mm(ps[:, 6, :], sel[l][:, j, :], cmbT[h][:, :], start=True, stop=True).then_inc(S("f_cw"), 1)

            def down(g):
                l, h, q, j = FT[g]
                if j == 0 and q:
                    pe.wait_ge(S("x_added"), q)
                pe.wait_ge(S("f_wd"), g + 1)
                pe.wait_ge(S("f_hl"), g + 1)
                for t in range(TH):
                    sl = slice(t * P, (t + 1) * P)
                    last = mm3(ps[:, t // 2, (t % 2) * DM:(t % 2 + 1) * DM], hh[g % 2][:, sl], hl[g % 2][:, sl],
                               wdh[g % 3][:, :], wdl[g % 3][:, :], j == 0 and t % 2 == 0, j == NJ[l] - 1, skip_group_check=True)
                last.then_inc(S("f_down"), 1)

            side(-1)
            for g in range(FN + 2):
                if 1 <= g <= FN and FT[g - 1][3]:
                    combine(g - 1)
                if g < FN:
                    gate_up(g)
                side(2 * g)
                if 1 <= g <= FN and not FT[g - 1][3]:
                    combine(g - 1)
                if g >= 2:
                    down(g - 2)
                side(2 * g + 1)

        for k, s in enumerate(ORDER):
            begin(pe, k)
            if s == "A1":
                attn1(k)
            elif s == "M":
                ssm(k)
            elif s == "F":
                ffns(k)
            else:
                ffn0(k)

    @block.scalar
    def _(act):
        A = nc.scalar.activation
        link = chain(act, "act_chain")


        def copy(out_, in_):
            return A(out_, in_, ACT.Copy)

        def parts(i):
            if i >= 2:
                act.wait_ge(S("a_q"), i - 1)
                act.wait_ge(S("a_w"), i - 1)
            copy(awh[i % 2][:, 0:KC * P].rearrange("p (c n) -> p c n", c=KC), wq[:, :, (i % HEADS) * P:(i % HEADS + 1) * P])
            copy(awh[i % 2][:, KC * P:AQ], wk[:, (i % HEADS) * P:(i % HEADS + 1) * P]).then_inc(S("a_wh"), 1)

        def norm_T(n, banks, dst):
            act.wait_ge(S("xT_psum"), n)
            for c in range(KC):
                last = copy(dst[:, c, :], ps[:, banks[c], :])
            last.then_inc(S("xT_hi"), 1)

        def ssm(k):
            for h in range(2):
                act.wait_ge(S("m_x"), h + 1)
                act.wait_ge(S("m_pad"), 1)
                for e in range(2):
                    last = copy(xpad[h][:, e, :, 3:DM + 3], ps[:, 4 * h + e, :].rearrange("p (b l) -> p b l", b=2))
                last.then_inc(S("m_xcopy"), 1)
            loaded(act, "small")
            A(tg[:, :], small[:, c_gate:c_gate + 8], ACT.Tanh)
            link(A(negA[:, :, :], small[:, c_al:c_al + 32].rearrange("p (e n) -> p e n", e=2), ACT.Exp))
            link(A(negA[:, :, :], negA[:, :, :], ACT.Copy, scale=-1.0))
            for h in range(2):
                act.wait_ge(S("m_conv"), h + 1)
                for e in range(2):
                    last = A(u[h][:, e, :], dlt[h][:, e, :], ACT.Silu, bias=small[:, c_cb + e:c_cb + e + 1])
                last.then_inc(S("m_u"), 1)
            def sum_weights(i):
                loaded(act, "w0raw")
                return A(w_values[:, :], w0raw[:, i, :], ACT.Abs, accum_out=wabs[:, i:i + 1])

            for h in range(2):
                act.wait_ge(S("m_dbl"), h + 1)
                if h:
                    act.wait_ge(S("m_dpre"), h)
                copy(dts[:, :], ps[0:8, 3 + 4 * h, :]).then_inc(S("m_dts"), 1)
                copy(BC_PARTS[h][0], ps[0:96, 2 + 4 * h, :]).then_inc(S("m_p1"), 1)
                if h:
                    for i in range(2):
                        act.wait_ge(S("ln_done"), i + 1)
                        A(xn[i][:, :, :], xn[i][:, :, :], ACT.Silu).then_inc(S("m_z"), 1)
                act.wait_ge(S("m_dpre"), h + 1)
                for e in range(2):
                    last = A(dlt[h][:, e, :], ps[:, 4 * h + e, :], ACT.Identity, bias=small[:, c_dtb + e:c_dtb + e + 1])
                last.then_inc(S("m_xs"), 1)
                if h == 0:
                    link(sum_weights(0))
            for h in range(2):
                y, w, lnw, inv = SOFTPLUS[h]
                act.wait_ge(S("m_xs"), h + 1)
                link(A(y, dlt[h][:, :, :], ACT.Abs))
                A(y, y, ACT.Exp, scale=-1.0).then_inc(S("m_ex"), 1)
            for h in range(2):
                y, w, lnw, inv = SOFTPLUS[h]
                act.wait_ge(S("m_w"), h + 1)
                A(lnw, w, ACT.Ln).then_inc(S("m_ln"), 1)
            for h in range(2):
                y, w, lnw, inv = SOFTPLUS[h]
                act.wait_ge(S("m_ln"), h + 1)
                A(inv, lnw, ACT.Exp, scale=-1.0).then_inc(S("m_lnw"), 1)

            def copy_B(g):
                act.wait_ge(S("m_B"), g + 1)
                if g >= 3:
                    act.wait_ge(S("m_dBu"), g - 2)
                copy(Bs[g % 3][:, :], ps[:, 2 + g % 2, :]).then_inc(S("m_Bcopy"), 1)

            act.wait_ge(S("m_bcs"), 2)
            copy_B(0)
            copy_B(1)
            link(sum_weights(1))
            sum_weights(2).then_inc(S("wabs_part"), 1)
            for g in range(2 * NS):
                h, n = g // NS, g % NS
                if n == 0:
                    act.wait_ge(S("m_du"), h + 1)
                if g >= 2:
                    act.wait_ge(S("m_h"), g - 1)
                for e in range(2):
                    last = A(dA[g % 2][:, e, :].rearrange("p (b l) -> p b l", b=2)[:, :, 1:DM],
                             dlt[h][:, e, :].rearrange("p (b l) -> p b l", b=2)[:, :, 1:DM],
                             ACT.Exp, scale=negA[:, e, n:n + 1])
                last.then_inc(S("m_dA"), 1)
                if g + 2 < 2 * NS:
                    copy_B(g + 2)
                if g - 2 in VALUE_AT:
                    v = VALUE_AT.index(g - 2)
                    act.wait_ge(S("wvo_psum"), v + 1)
                    copy(wvo[:, v, :], ps[:, 6 + v % 2, 0:DM]).then_inc(S("wvo_copied"), 1)
            act.wait_ge(S("w_scales"), 1)
            for i in range(3):
                link(A(w0raw[:, i, :], w0raw[:, i, :], ACT.Identity, scale=winv[:, i:i + 1], bias=magic[:, :]))
                A(w0raw[:, i, :], w0raw[:, i, :], ACT.Identity, bias=nmagic[:, :]).then_inc(S("w0_round"), 1)
            copy(scratch[:, 0:8], tg[:, :]).then_inc(S("act_step"), 1)

        def ffn0(k):
            def inputs(h):
                act.wait_ge(S("q_xTp"), h + 1)
                copy(xqT[h][:, :, :].rearrange("p c t -> p (c t)"), psb[:, 2, :]).then_inc(S("q_xT"), 1)

            inputs(0)
            for t in range(NT + 2):
                if t < NT:
                    if t % TH == 0:
                        act.wait_ge(S("q_s"), t // TH + 1)
                    if t >= 2:
                        act.wait_ge(S("q_h"), 2 * (t - 1))
                    for n in range(2):
                        act.wait_ge(S("q_gate"), 2 * t + n + 1)
                        A(sg0[t % 2][:, n * 512:(n + 1) * 512], ps[:, 3 + n, :], ACT.Silu,
                          scale=qs[t // TH][:, t % TH:t % TH + 1]).then_inc(S("q_sg"), 1)
                if t == 3:
                    inputs(1)
                if t == NT - 2:
                    copy(ch[:, :], ctxT[:, :]).then_inc(S("a_ch"), 1)
                    loaded(act, "wq", "wk")
                    parts(0)
                    parts(1)
                if 1 <= t <= NT:
                    i = t - 1
                    act.wait_ge(S("q_inv"), i + 1)
                    if i >= 2:
                        act.wait_ge(S("q_hq"), i - 1)
                    link(A(h0a[i % 2][:, :], h0[i % 2][:, :], ACT.Identity, scale=qt[i % 2][:, 2:3], bias=magic[:, :]))
                    A(h0a[i % 2][:, :], h0a[i % 2][:, :], ACT.Identity, bias=nmagic[:, :]).then_inc(S("q_r"), 1)
                if t >= 2:
                    act.wait_ge(S("q_hTp"), t - 1)
                    if t >= 3:
                        act.wait_ge(S("q_down"), t - 2)
                    copy(hqT[:, :, :].rearrange("p j t -> p (j t)"), psb[:, 7, :]).then_inc(S("q_hT"), 1)
            copy(scratch[:, 0:8], tg[:, :]).then_inc(S("act_step"), 1)

        def attn1(k):

            def value_parts(i):
                if i >= 2:
                    act.wait_ge(S("a_out"), i - 1)
                copy(voh[i % 2][:, :], wvo[:, i % HEADS, :]).then_inc(S("a_voh"), 1)

            def squares(i):
                act.wait_ge(S("a_k"), i + 1)
                if i:
                    act.wait_ge(S("a_qn"), i)
                A(ksq[:, :], ps[:, 7, :], ACT.Square).then_inc(S("a_ksq"), 1)
                act.wait_ge(S("a_q"), i + 1)
                act.wait_ge(S("a_rks"), i + 1)
                A(qsq[:, :], ps[:, 6, :], ACT.Square).then_inc(S("a_qsq"), 1)
                if i > 1:
                    act.wait_ge(S("a_s"), i - 1)
                copy(qh[i % 2][:, :], ps[:, 6, :]).then_inc(S("a_qh"), 1)

            def keys_hi(i):
                act.wait_ge(S("a_kt"), i + 1)
                act.wait_ge(S("gqk_ready"), 1)
                A(kh[:, :], ps[:, 7, :], ACT.Copy, scale=gqk[:, :]).then_inc(S("a_kh"), 1)

            def ac_hi(i):
                act.wait_ge(S("a_ac"), i + 1)
                if i:
                    act.wait_ge(S("a_out"), i)
                copy(ah[:, :], ps[:, 4, :]).then_inc(S("a_ah"), 1)

            norm_T(1, (6, 7), xTh)
            squares(0)
            keys_hi(0)
            for i in range(HEADS2 + 1):
                if i >= 2:
                    ac_hi(i - 2)
                if i + 1 < HEADS2:
                    squares(i + 1)
                if i + 2 < HEADS2:
                    parts(i + 2)
                if i:
                    value_parts(i - 1)
                if i == 1:
                    norm_T(2, (0, 1), xTa[0])
                if i:
                    act.wait_ge(S("a_pt"), i)
                    if i > 1:
                        act.wait_ge(S("a_ac"), i - 1)
                    copy(PT[:, :, :], ps[:, 4:6, :]).then_inc(S("a_pts"), 1)
                if i + 1 < HEADS2:
                    keys_hi(i + 1)
                if i < HEADS2:
                    act.wait_ge(S("a_nb"), i + 1)
                    if i > 1:
                        act.wait_ge(S("a_pt"), i - 1)
                    if i:
                        act.wait_ge(S("a_ri"), i)
                    for t in range(TH):
                        last = A(Pm[i % 2][:, t, :], ps[:, 2 + t // 2, (t % 2) * DM:(t % 2 + 1) * DM], ACT.Exp,
                                 bias=nb[:, t:t + 1], scale=rq[i % 2][:, t:t + 1], accum_out=rs[:, t:t + 1])
                    last.then_inc(S("a_exp"), 1)
            norm_T(3, (2, 3), xTh)
            ac_hi(HEADS2 - 1)
            copy(scratch[:, 0:8], tg[:, :]).then_inc(S("act_step"), 1)

        def bank7_put(w):
            act.wait_ge(S("b7_put"), bank7.index(w) + 1)

        def side(place_):
            for w in beside.get(place_, ()):
                kind = w[0]
                if kind == "xT":
                    _, l, h, c = w
                    bank7_put(w)
                    copy(xTp[h][0][:, c, :], ps[:, 7, :]).then_inc(S("f_xT_hi"), 1)
                elif kind == "aT":
                    bank7_put(w)
                    copy(xnT[:, w[3], :], ps[:, 7, :]).then_inc(S("b7_free"), 1)
                elif kind == "route":
                    _, l, h = w
                    e = E1 if l == 1 else E3
                    act.wait_ge(S("f_shift"), (0 if l == 1 else 2) + h + 1)
                    if l == 1:
                        A(rc[:, 3, :], rl[:, :, e], ACT.Exp, scale=-1.0)
                    A(rp[:, :, 0:e], rw[:, :, 0:e], ACT.Exp).then_inc(S("f_ex"), 1)
                elif kind == "router_w":
                    loaded(act, "f3r")
                    copy(wrh[:, :, :], fr[3][:, :, :]).then_inc(S("r_wh"), 1)
                elif kind == "map":
                    _, l, s_ = w
                    b, s_ = s_ // 7, s_ % 7
                    if s_ < 2:
                        bank7_put(w)
                        A(aqk[s_][:, :], ps[:, 7, :], ACT.Identity,
                          bias=small[:, c_b + 2 * (l - 2) + s_:c_b + 2 * (l - 2) + s_ + 1]).then_inc(S("b7_free"), 1)
                    elif s_ < 6:
                        act.wait_ge(S("am_nb"), 8 * (l - 2) + 4 * b + s_ - 1)
                        A(aP[:, :], ps[:, 7, 0:DM], ACT.Exp, bias=am[:, 1:2], accum_out=am[:, 2:3]).then_inc(S("am_exp"), 1)

        def ffns(k):
            def gu_hi(g):
                l, h, q, j = FT[g]
                if j == 0:
                    loaded(act, {1: "f1a", 2: "f2w", 3: "f3w"}[l])
                if l == 1 and j == J1A:
                    loaded(act, "f1b")
                if g >= 2:
                    act.wait_ge(S("f_gu"), g - 1)
                copy(wgh[g % 2][:, :], raw_w(l, j)[:, 0:GU]).then_inc(S("f_wgh"), 1)

            def d_hi(g):
                l, h, q, j = FT[g]
                if l == 2 and j == 0:
                    act.wait_ge(S("w2_mixed"), 2)
                if g >= 3:
                    act.wait_ge(S("f_down"), g - 2)
                copy(wdh[g % 3][:, :], raw_w(l, j)[:, GU:WJ]).then_inc(S("f_wdh"), 1)

            def rows_hi(g):
                if FT[g][0] == 2:
                    act.wait_ge(S("f_m"), g + 1)
                else:
                    act.wait_ge(S("f_h"), ROUTED[g] + 1)
                if g >= 2:
                    act.wait_ge(S("f_down"), g - 1)
                copy(hh[g % 2][:, :], sg[g % 2][:, :]).then_inc(S("f_hh"), 1)

            loaded(act, "f1r")
            copy(wrh[:, :, :], fr[1][:, :, :]).then_inc(S("r_wh"), 1)
            gu_hi(0)
            gu_hi(1)
            d_hi(0)
            side(-1)
            for g in range(FN + 1):
                first = g and FT[g - 1][0] != 2 and not FT[g - 1][3]
                if g and not first:
                    rows_hi(g - 1)
                if g < FN:
                    act.wait_ge(S("f_gu"), g + 1)
                    if g >= 2:
                        act.wait_ge(S("f_hl"), g - 1)
                    A(sg[g % 2][:, :], ps[:, 2 + 2 * (g % 2), :], ACT.Silu).then_inc(S("f_sg"), 1)
                side(2 * g)
                if first:
                    rows_hi(g - 1)
                if g + 2 < FN:
                    gu_hi(g + 2)
                if g + 1 < FN:
                    d_hi(g + 1)
                side(2 * g + 1)

        for k, s in enumerate(ORDER):
            begin(act, k)
            if s == "A1":
                attn1(k)
            elif s == "M":
                ssm(k)
            elif s == "F":
                ffns(k)
            else:
                ffn0(k)

    @block.vector
    def _(dve):
        V = nc.vector
        link = chain(dve, "dve_chain")
        n_tail = [0]

        def stats(h):
            n_tail[0] += 1
            for t in range(TH):
                last = V.bn_stats(bst[:, t, :], x[:, h * TH + t, :])
            link(last)
            for t in range(TH):
                last = V.bn_aggr(mv[:, t, :], bst[:, t, :])
            link(last)
            V.tensor_scalar(ve[:, :], mv[:, :, 1], EPS, None, ALU.add).then_inc(S("ln_var"), 1)

        def normalise(h, dst):
            dve.wait_ge(S("ln_rstd"), n_tail[0])
            for t in range(TH):
                last = V.tensor_scalar(dst[:, t, :], x[:, h * TH + t, :], mv[:, t, 0:1], rstd[:, t:t + 1],
                                       ALU.subtract, ALU.mult)
            last.then_inc(S("ln_done"), 1)

        def tail(h):
            stats(h)
            normalise(h, xn[h])

        def residual(s, h, bank=0):
            xv = x[:, h * TH:(h + 1) * TH, :].rearrange("p t d -> p (t d)")
            c = gate_col[s]
            link(V.scalar_tensor_tensor(xv, ps[:, bank:bank + 2, :].rearrange("p a n -> p (a n)"), tg[:, c:c + 1], xv, ALU.mult, ALU.add))

        def x_lo(n, banks, hi, lo):
            dve.wait_ge(S("xT_hi"), n)
            for c in range(KC):
                last = V.tensor_tensor(lo[:, c, :], ps[:, banks[c], :], hi[:, c, :].bitcast(f32), ALU.subtract)
            last.then_inc(S("xT_ready"), 1)

        def quantise_weights():
            dve.wait_ge(S("wabs_sum"), 1)
            link(V.tensor_scalar(wscale[:, :], ps[:, 7, 256:259], 1.0 / (DM * I0), EPS, ALU.mult, ALU.add))
            V.reciprocal(winv[:, :], wscale[:, :]).then_inc(S("w_scales"), 1)
            dve.wait_ge(S("w_scales"), 1)

        def quantise(i):
            dve.wait_ge(S("w0_round"), i + 1)
            V.tensor_scalar(w0q[i][:, :], w0raw[:, i, :], 1.0, -1.0, ALU.min, ALU.max).then_inc(S("w0_ready"), 1)
            dve.wait_ge(S("w0_ready"), i + 1)

        def ssm(k):
            for h in range(2):
                last = V.memset(xpad[h][:, :, :, 0:3], 0.0)
            last.then_inc(S("m_pad"), 1)
            V.memset(ones[:, :], 1.0).then_inc(S("ones_set"), 1)
            V.memset(epsc[:, :], EPS)
            V.memset(magic[:, :], MAGIC)
            V.memset(nmagic[:, :], -MAGIC)
            V.memset(mhalf[:, :], -0.5).then_inc(S("mhalf_set"), 1)
            loaded(dve, "small")
            V.tensor_scalar(gqk[:, :], small[:, c_gq:c_gq + 1], small[:, c_gk:c_gk + 1], SCALE, ALU.mult, ALU.mult).then_inc(S("gqk_ready"), 1)
            for h in range(2):
                dve.wait_ge(S("m_xcopy"), h + 1)
                other = (dA[0], dA[1])[h]
                for e in range(2):
                    for c in range(4):
                        w = small[:, c_cw + 4 * e + c:c_cw + 4 * e + c + 1]
                        src = xpad[h][:, e, :, c:c + DM]
                        dst = (other, dlt[h])[c % 2][:, e, :].rearrange("p (b l) -> p b l", b=2)
                        prev = (other, dlt[h])[(c + 1) % 2][:, e, :].rearrange("p (b l) -> p b l", b=2)
                        if c == 0:
                            link(V.tensor_scalar(dst, src, w, None, ALU.mult))
                        elif c < 3 or e == 0:
                            link(V.scalar_tensor_tensor(dst, src, w, prev, ALU.mult, ALU.add))
                        else:
                            V.scalar_tensor_tensor(dst, src, w, prev, ALU.mult, ALU.add).then_inc(S("m_conv"), 1)
            loaded(dve, "x")
            tail(0)
            for h in range(2):
                r1, r2 = dBu[1][0:96, 0, :], dBu[1][0:96, 1, :]
                p1, p2 = BC_PARTS[h]
                dve.wait_ge(S("m_p1"), h + 1)
                link(V.tensor_tensor(r1, ps[0:96, 2 + 4 * h, :], p1, ALU.subtract))
                link(V.tensor_copy(p2, r1))
                link(V.tensor_tensor(r2, r1, p2, ALU.subtract))
                V.tensor_copy(bcs[h][0:32, :], p1[0:32, :])
                V.tensor_copy(bcs[h][32:64, :], p2[32:64, :])
                V.tensor_copy(bcs[h][64:96, :], r2[64:96, :]).then_inc(S("m_bcs"), 1)
                dve.wait_ge(S("m_bcs"), h + 1)
                if h == 0:
                    tail(1)
            for h in range(2):
                y, w, lnw, inv = SOFTPLUS[h]
                dve.wait_ge(S("m_ex"), h + 1)
                V.tensor_scalar(w, y, 1.0, None, ALU.add).then_inc(S("m_w"), 1)
                dve.wait_ge(S("m_w"), h + 1)
                link(V.scalar_tensor_tensor(du[h][:, :, :], w, 1.0, y, ALU.subtract, ALU.subtract))
            for h in range(2):
                y, w, lnw, inv = SOFTPLUS[h]
                dve.wait_ge(S("m_ln"), h + 1)
                link(V.scalar_tensor_tensor(dlt[h][:, :, :], dlt[h][:, :, :], 0.0, lnw, ALU.max, ALU.add))
            def delta(h):
                y, w, lnw, inv = SOFTPLUS[h]
                dve.wait_ge(S("m_lnw"), h + 1)
                link(V.tensor_tensor(du[h][:, :, :], du[h][:, :, :], inv, ALU.mult))
                link(V.tensor_tensor(dlt[h][:, :, :], dlt[h][:, :, :], du[h][:, :, :], ALU.subtract))
                if h == 0:
                    for i in range(2):
                        V.memset(dA[i][:, :, :].rearrange("p e (b l) -> p (e b) l", b=2)[:, :, 0:1], 0.0)
                V.tensor_tensor(du[h][:, :, :], dlt[h][:, :, :], u[h][:, :, :], ALU.mult).then_inc(S("m_du"), 1)

            delta(0)
            delta(1)

            def gated(h):
                dve.wait_ge(S("m_y"), (h + 1) * NS)
                for e in range(2):
                    last = V.scalar_tensor_tensor(dlt[h][:, e, :], u[h][:, e, :], small[:, c_D + e:c_D + e + 1], ps[:, e, :], ALU.mult, ALU.add)
                last.then_inc(S("m_y_read"), 1)
                dve.wait_ge(S("m_y_read"), h + 1)
                dve.wait_ge(S("m_z"), h + 1)
                for e in range(2):
                    last = V.tensor_tensor(u[h][:, e, :].rearrange("p (b l) -> p b l", b=2), dlt[h][:, e, :].rearrange("p (b l) -> p b l", b=2),
                                           xn[h][:, :, :].rearrange("p (b e) l -> p e b l", e=2)[:, e], ALU.mult)
                last.then_inc(S("m_yz"), 1)

            flat = "p e t -> p (e t)"
            for g in range(2 * NS + 1):
                if g < 2 * NS:
                    dve.wait_ge(S("m_dA"), g + 1)
                    dve.wait_ge(S("m_dBu"), g + 1)
                    if g >= 2:
                        dve.wait_ge(S("m_hC"), g - 1)
                    V.tensor_tensor_scan(hst[g % 2][:, :, :].rearrange(flat), dA[g % 2][:, :, :].rearrange(flat),
                                         dBu[g % 2][:, :, :].rearrange(flat), 0.0, ALU.mult, ALU.add).then_inc(S("m_h"), 1)
                if g:
                    dve.wait_ge(S("m_h"), g)
                    dve.wait_ge(S("m_C"), g)
                    if g >= 3:
                        dve.wait_ge(S("m_y"), g - 2)
                    V.tensor_tensor(hC[(g - 1) % 2][:, :, :], hst[(g - 1) % 2][:, :, :], bc(ps[:, 4 + (g - 1) % 2, :].unsqueeze(1), [P, 2, HALF]),
                                    ALU.mult).then_inc(S("m_hC"), 1)
                if g == 6:
                    quantise_weights()
                if g == NS + 1:
                    gated(0)
                if g == NS + 4:
                    dve.wait_ge(S("m_out"), 1)
                    residual("M", 0, 6)
                    V.tensor_copy(scratch[:, 12:13], epsc[:, :]).then_inc(S("m_res"), 1)
                if g == NS + 5:
                    stats(0)
                if g == NS + 8:
                    normalise(0, xn[0])
            gated(1)
            quantise(0)
            dve.wait_ge(S("pe_step"), k + 1)
            residual("M", 1, 6)
            V.tensor_copy(scratch[:, 8:9], epsc[:, :]).then_inc(S("dve_step"), 1)

        def ffn0(k):
            def quantise_x(h):
                q = qs[h]
                am_, s_, r_, su = q[:, 4:8], q[:, 8:12], q[:, 12:16], q[:, 16:20]
                link(V.tensor_reduce(am_, xn[h][:, :, :], AX, ALU.max, apply_absolute_value=True))
                link(V.tensor_scalar(s_, am_, 1.0 / 127.0, EPS, ALU.mult, ALU.add))
                link(V.reciprocal(r_, s_))
                V.tensor_scalar(q[:, 0:4], s_, wscale[:, 0:1], None, ALU.mult).then_inc(S("q_s"), 1)
                V.tensor_scalar(su, s_, wscale[:, 1:2], None, ALU.mult)
                for t in range(TH):
                    last = V.tensor_scalar(xqa[:, t, :], xn[h][:, t, :], q[:, 12 + t:13 + t], MAGIC, ALU.mult, ALU.add)
                link(last)
                link(V.tensor_scalar(xqa[:, :, :], xqa[:, :, :], MAGIC, 127.0, ALU.subtract, ALU.min))
                V.tensor_scalar(xq[h][:, :, :], xqa[:, :, :], -128.0, None, ALU.max).then_inc(S("q_xq"), 1)
                dve.wait_ge(S("q_xq"), h + 1)

            def output(t):
                dve.wait_ge(S("q_down"), t + 1)
                V.scalar_tensor_tensor(x[:, t, :], ps[:, t % 2, 0:DM], qs[t // TH][:, 20 + t % TH:21 + t % TH], x[:, t, :],
                                       ALU.mult, ALU.add).then_inc(S("q_out"), 1)

            def within_8_bits(t):
                dve.wait_ge(S("q_r"), t + 1)
                if t:
                    dve.wait_ge(S("q_hTp"), t)
                V.tensor_scalar(hq[:, :], h0a[t % 2][:, :], 127.0, -128.0, ALU.min, ALU.max).then_inc(S("q_hq"), 1)

            dve.wait_ge(S("ln_done"), ln_index[("F0", 0)])
            quantise_x(0)
            quantise(1)
            for t in range(NT):
                q, r = qs[t // TH], qt[t % 2]
                if t >= 2:
                    dve.wait_ge(S("q_r"), t - 1)
                for n in range(2):
                    sl = slice(n * 512, (n + 1) * 512)
                    dve.wait_ge(S("q_up"), 2 * t + n + 1)
                    dve.wait_ge(S("q_sg"), 2 * t + n + 1)
                    V.scalar_tensor_tensor(h0[t % 2][:, sl], ps[:, 5 + n, :], q[:, 16 + t % TH:17 + t % TH],
                                           sg0[t % 2][:, sl], ALU.mult, ALU.mult).then_inc(S("q_h"), 1)
                dve.wait_ge(S("q_h"), 2 * t + 2)
                link(V.tensor_reduce(r[:, 0:1], h0[t % 2][:, :], AX, ALU.max, apply_absolute_value=True))
                link(V.tensor_scalar(r[:, 1:2], r[:, 0:1], 1.0 / 127.0, EPS, ALU.mult, ALU.add))
                V.reciprocal(r[:, 2:3], r[:, 1:2]).then_inc(S("q_inv"), 1)
                link(V.tensor_scalar(q[:, 20 + t % TH:21 + t % TH], r[:, 1:2], wscale[:, 2:3], tg[:, gate_col["F0"]:gate_col["F0"] + 1], ALU.mult, ALU.mult))
                if t == 0:
                    quantise(2)
                    stats(1)
                if t == 1:
                    normalise(1, xn[1])
                    dve.wait_ge(S("ln_done"), ln_index[("F0", 1)])
                    quantise_x(1)
                if t:
                    within_8_bits(t - 1)
                if t >= 3:
                    output(t - 3)
                if t == NT - 1:
                    dve.wait_ge(S("q_out"), TH)
                    stats(0)
            within_8_bits(NT - 1)
            for t in range(NT - 3, NT):
                output(t)
            normalise(0, xn[0])
            dve.wait_ge(S("q_out"), NT)
            dve.wait_ge(S("pe_step"), k + 1)
            V.tensor_copy(scratch[:, 8:9], epsc[:, :]).then_inc(S("dve_step"), 1)

        def attn1(k):
            x_lo(1, (6, 7), xTh, xTl)
            stats(1)

            def key_norms(i):
                dve.wait_ge(S("a_ksq"), i + 1)
                if i:
                    dve.wait_ge(S("a_rk"), i)
                V.tensor_reduce(rks[:, :], ksq[:, :].rearrange("p (t d) -> p t d", t=TH), AX, ALU.add).then_inc(S("a_rks"), 1)

            def queries_lo(i):
                dve.wait_ge(S("a_qh"), i + 1)
                V.tensor_tensor(ql[i % 2][:, :], ps[:, 6, :], qh[i % 2][:, :].bitcast(f32), ALU.subtract).then_inc(S("a_ql"), 1)

            def keys_scaled(i):
                dve.wait_ge(S("a_rk"), i + 1)
                if i:
                    dve.wait_ge(S("a_kt"), i)
                V.tensor_tensor(ktok[:, :].rearrange("p (t d) -> p t d", t=TH), ps[:, 7, :].rearrange("p (t d) -> p t d", t=TH),
                                bc(rk[:, :].unsqueeze(2), [P, TH, P]), ALU.mult).then_inc(S("a_ktok"), 1)

            def query_norms(i):
                dve.wait_ge(S("a_qn"), i + 1)
                if i:
                    dve.wait_ge(S("a_rq"), i)
                V.tensor_copy(rqs[:, :], ps[:, 6, 0:TH]).then_inc(S("a_rqs"), 1)

            def keys_lo(i):
                dve.wait_ge(S("a_kh"), i + 1)
                V.scalar_tensor_tensor(kl[:, :], ps[:, 7, :], gqk[:, :], kh[:, :].bitcast(f32), ALU.mult, ALU.subtract).then_inc(S("a_kT"), 1)

            def ac_lo(i):
                dve.wait_ge(S("a_ah"), i + 1)
                V.tensor_tensor(al[:, :], ps[:, 4, :], ah[:, :].bitcast(f32), ALU.subtract).then_inc(S("a_al"), 1)

            key_norms(0)
            queries_lo(0)
            keys_scaled(0)
            query_norms(0)
            keys_lo(0)
            normalise(1, xn[1])
            for i in range(HEADS2):
                if i >= 2:
                    ac_lo(i - 2)
                if i + 1 < HEADS2:
                    key_norms(i + 1)
                    queries_lo(i + 1)
                    keys_scaled(i + 1)
                if i == 1:
                    x_lo(2, (0, 1), xTa[0], xTa[1])
                dve.wait_ge(S("a_s"), i + 1)
                link(V.tensor_reduce(mx[:, :], ps[:, 2:4, :].rearrange("p a (b n) -> p (a b) n", b=2), AX, ALU.max))
                dve.wait_ge(S("a_rq"), i + 1)
                if i:
                    dve.wait_ge(S("a_exp"), i)
                V.scalar_tensor_tensor(nb[:, :], mx[:, :], -1.0, rq[i % 2][:, :], ALU.mult, ALU.mult).then_inc(S("a_nb"), 1)
                if i + 1 < HEADS2:
                    query_norms(i + 1)
                    keys_lo(i + 1)
                dve.wait_ge(S("a_exp"), i + 1)
                if i:
                    dve.wait_ge(S("a_pn"), i)
                V.reciprocal(ri[:, :], rs[:, :]).then_inc(S("a_ri"), 1)
                if i == HEADS + 1:
                    dve.wait_ge(S("a_out"), HEADS)
                    residual("A1", 0)
                    V.tensor_copy(scratch[:, 12:13], epsc[:, :]).then_inc(S("a_res"), 1)
                if i == HEADS + 2:
                    stats(0)
                if i == HEADS + 3:
                    normalise(0, xn[0])
            ac_lo(HEADS2 - 2)
            x_lo(3, (2, 3), xTh, xTl)
            ac_lo(HEADS2 - 1)
            dve.wait_ge(S("pe_step"), k + 1)
            residual("A1", 1)
            V.tensor_copy(scratch[:, 8:9], epsc[:, :]).then_inc(S("dve_step"), 1)

        def take_logits(l, h):
            e = E1 if l == 1 else E3
            nl = e + 1 if l == 1 else e
            V.tensor_copy(rl[:, :, 0:nl], ps[:, 7, 0:TH * 32].rearrange("p (t n) -> p t n", t=TH)[:, :, 0:nl]).then_inc(S("b7_free"), 1)
            dve.wait_ge(S("b7_free"), bank7.index(("logits", l, h)) + 1)
            V.memset(rp[:, :, e:24], -1.0)
            link(V.tensor_reduce(rc[:, 0, :], rl[:, :, 0:e], AX, ALU.max))
            V.tensor_tensor(rw[:, :, 0:e], rl[:, :, 0:e], bc(rc[:, 0, :].unsqueeze(2), [P, TH, e]), ALU.subtract).then_inc(S("f_shift"), 1)

        def router(l, h):
            e, top = (E1, TOP1) if l == 1 else (E3, TOP3)
            n = e + 1
            dve.wait_ge(S("f_ex"), (0 if l == 1 else 2) + h + 1)
            link(V.tensor_reduce(rc[:, 1, :], rp[:, :, 0:e], AX, ALU.add))
            link(V.reciprocal(rc[:, 1, :], rc[:, 1, :]))
            link(V.tensor_tensor(rp[:, :, 0:e], rp[:, :, 0:e], bc(rc[:, 1, :].unsqueeze(2), [P, TH, e]), ALU.mult))
            for t in range(TH):
                last = V.max(rt[:, t, :], rp[:, t, 0:e])
            link(last)
            link(V.memset(rt[:, :, top:8], -1.0))
            for t in range(TH):
                last = V.match_replace(rr[:, t, :], rt[:, t, :], rp[:, t, :], 0.0)
            link(last)
            link(V.tensor_tensor(rw[:, :, 0:e], rp[:, :, 0:e], rr[:, :, 0:e], ALU.subtract))
            if l == 1:
                link(V.tensor_reduce(rc[:, 2, :], rw[:, :, 0:e], AX, ALU.add))
                link(V.reciprocal(rc[:, 2, :], rc[:, 2, :]))
                link(V.tensor_tensor(rw[:, :, 0:e], rw[:, :, 0:e], bc(rc[:, 2, :].unsqueeze(2), [P, TH, e]), ALU.mult))
                link(V.tensor_scalar(rc[:, 3, :], rc[:, 3, :], 1.0, None, ALU.add))
                link(V.reciprocal(rw[:, :, e], rc[:, 3, :]))
            else:
                link(V.memset(rw[:, :, e:n], 1.0))
            link(V.memset(cmb[:, :, :], 0.0))
            link(V.tensor_copy(cmb[:, :, 0:n], rw[:, :, 0:n]))
            link(V.tensor_tensor(rr[:, :, 0:n], rw[:, :, 0:n], cmb[:, :, 0:n], ALU.subtract))
            link(V.tensor_copy(cmb[:, :, 32:32 + n], rr[:, :, 0:n]))
            V.tensor_tensor(cmb[:, :, 64:64 + n], rr[:, :, 0:n], cmb[:, :, 32:32 + n], ALU.subtract).then_inc(S("f_cmb"), 1)

        def bank7_put(w):
            dve.wait_ge(S("b7_put"), bank7.index(w) + 1)

        def side(place_):
            for w in beside.get(place_, ()):
                kind = w[0]
                if kind == "residual":
                    _, l, h = w
                    dve.wait_ge(S("f_down"), FIRST[2 * (l - 1) + h + 1])
                    residual(f"F{l}", h)
                    V.tensor_copy(scratch[:, 12:13], epsc[:, :]).then_inc(S("x_added"), 1)
                elif kind == "stats":
                    stats(w[1][1])
                elif kind == "normalise":
                    normalise(w[1][1], xn[1])
                elif kind == "xT":
                    _, l, h, c = w
                    n = bank7.index(w)
                    dve.wait_ge(S("f_xT_hi"), sum(1 for v in bank7[:n + 1] if v[0] == "xT"))
                    V.tensor_tensor(xTp[h][1][:, c, :], ps[:, 7, :], xTp[h][0][:, c, :].bitcast(f32),
                                    ALU.subtract).then_inc(S("b7_free"), 1)
                elif kind == "apply":
                    _, l, h, b = w
                    bank7_put(w)
                    xv = x[:, h * TH + 2 * b:h * TH + 2 * b + 2, :].rearrange("p t d -> p (t d)")
                    c = gate_col[f"A{l}"]
                    V.scalar_tensor_tensor(xv, ps[:, 7, :], tg[:, c:c + 1], xv, ALU.mult, ALU.add).then_inc(S("b7_free"), 1)
                    dve.wait_ge(S("b7_free"), bank7.index(w) + 1)
                elif kind == "logits":
                    bank7_put(w)
                    take_logits(w[1], w[2])
                elif kind == "route":
                    router(w[1], w[2])
                elif kind == "cmbT":
                    bank7_put(w)
                    V.tensor_copy(cmbT[w[2]][:, :], psb[0:96, 7, 0:HALF]).then_inc(S("b7_free"), 1)
                elif kind == "map" and w[2] % 7 >= 2:
                    _, l, s_ = w
                    b, s_ = s_ // 7, s_ % 7
                    n = 8 * (l - 2) + 4 * b + s_ - 1
                    bank7_put(w)
                    if s_ < 6:
                        V.tensor_reduce(am[:, 0:1], ps[:, 7, 0:DM], AX, ALU.max).then_inc(S("am_max"), 1)
                    if s_ > 2:
                        t = s_ - 3
                        last = V.tensor_copy(attT[l][:, :, b, t * P:(t + 1) * P], ps[:, 7, DM:2 * DM].rearrange("p (c m) -> p c m", c=KC))
                        if s_ == 6:
                            last.then_inc(S("b7_free"), 1)
                            continue
                        link(last)
                    dve.wait_ge(S("am_max"), n)
                    V.tensor_scalar(am[:, 1:2], am[:, 0:1], -1.0, None, ALU.mult).then_inc(S("am_nb"), 1)
                elif kind == "map_norm":
                    _, l, s_ = w
                    n = 8 * (l - 2) + 4 * (s_ // 7) + s_ % 7 - 1
                    dve.wait_ge(S("am_exp"), n)
                    link(V.reciprocal(am[:, 3:4], am[:, 2:3]))
                    V.tensor_scalar(aP[:, :], aP[:, :], am[:, 3:4], None, ALU.mult).then_inc(S("am_pn"), 1)
                    dve.wait_ge(S("am_pn"), n)
                    V.tensor_copy(scratch[:, 13:14], epsc[:, :]).then_inc(S("b7_free"), 1)
                elif kind == "mix":
                    j = w[1]
                    bank7_put(w)
                    link(V.tensor_copy(wmix[:, 0:2, :], ps[:, 7, :].rearrange("p (a d) -> p a d", a=2)))
                    V.tensor_tensor(f2w[:, j, GU:WJ], wmix[:, 0, :], wmix[:, 1, :], ALU.add)
                    V.tensor_tensor(f2w[:, j + 1, GU:WJ], wmix[:, 0, :], wmix[:, 1, :], ALU.subtract).then_inc(S("b7_free"), 1)
                    dve.wait_ge(S("b7_free"), bank7.index(w) + 1)
                elif kind == "butterfly":
                    st = w[1]
                    for b in range(0, NJ[2], 2 * st):
                        lo_, hi_ = f2w[:, b:b + st, GU:WJ], f2w[:, b + st:b + 2 * st, GU:WJ]
                        link(V.tensor_tensor(wmix[:, 0:st, :], lo_, hi_, ALU.subtract))
                        link(V.tensor_tensor(lo_, lo_, hi_, ALU.add))
                        last = V.tensor_copy(hi_, wmix[:, 0:st, :])
                        if b + 2 * st < NJ[2]:
                            link(last)
                    last.then_inc(S("w2_mixed"), 1)
                    dve.wait_ge(S("w2_mixed"), st // 2)

        def ffns(k):
            def weighted(g):
                dve.wait_ge(S("f_m"), g + 1)
                dve.wait_ge(S("f_cw"), ROUTED[g] + 1)
                V.tensor_tensor(sg[g % 2][:, :], sg[g % 2][:, :], ps[:, 6, :], ALU.mult).then_inc(S("f_h"), 1)

            side(-1)
            for g in range(FN + 1):
                routed = g and FT[g - 1][0] != 2
                if routed and FT[g - 1][3]:
                    weighted(g - 1)
                if g < FN:
                    dve.wait_ge(S("f_sg"), g + 1)
                    V.tensor_tensor(sg[g % 2][:, :], sg[g % 2][:, :], ps[:, 3 + 2 * (g % 2), :], ALU.mult).then_inc(S("f_m"), 1)
                side(2 * g)
                if routed and not FT[g - 1][3]:
                    weighted(g - 1)
                if g:
                    dve.wait_ge(S("f_hh"), g)
                    if g >= 3:
                        dve.wait_ge(S("f_down"), g - 2)
                    V.tensor_tensor(hl[(g - 1) % 2][:, :], sg[(g - 1) % 2][:, :], hh[(g - 1) % 2][:, :].bitcast(f32), ALU.subtract).then_inc(S("f_hl"), 1)
                side(2 * g + 1)
                for q, h in ((5, 0),):
                    if 2 * g + 1 == 2 * FIRST[q] + 3:
                        V.tensor_copy(scratch[:, 10 + h:11 + h], epsc[:, :]).then_inc(S("x_final"), 1)
            dve.wait_ge(S("f_down"), FN)
            residual("F3", 1)
            V.tensor_copy(scratch[:, 11:12], epsc[:, :]).then_inc(S("x_final"), 1)

        for k, s in enumerate(ORDER):
            begin(dve, k)
            if s == "A1":
                attn1(k)
            elif s == "M":
                ssm(k)
            elif s == "F":
                ffns(k)
            else:
                ffn0(k)

    @block.gpsimd
    def _(pool):
        G = nc.gpsimd
        n_rstd = [0]

        def rstd_of():
            n_rstd[0] += 1
            pool.wait_ge(S("ln_var"), n_rstd[0])
            G.tensor_tensor(rstd[:, :], ve[:, :], mhalf[:, :], ALU.pow).then_inc(S("ln_rstd"), 1)

        def parts(i):
            pool.wait_ge(S("a_wh"), i + 1)
            G.tensor_tensor(awl[i % 2][:, 0:KC * P].rearrange("p (c n) -> p c n", c=KC), wq[:, :, (i % HEADS) * P:(i % HEADS + 1) * P],
                            awh[i % 2][:, 0:KC * P].bitcast(f32).rearrange("p (c n) -> p c n", c=KC), ALU.subtract)
            G.tensor_tensor(awl[i % 2][:, KC * P:AQ], wk[:, (i % HEADS) * P:(i % HEADS + 1) * P], awh[i % 2][:, KC * P:AQ].bitcast(f32),
                            ALU.subtract).then_inc(S("a_w"), 1)

        def context_lo():
            pool.wait_ge(S("a_ch"), 1)
            G.tensor_tensor(cl[:, :], ctxT[:, :], ch[:, :].bitcast(f32), ALU.subtract).then_inc(S("a_ctx"), 1)

        def value_parts(i):
            pool.wait_ge(S("a_voh"), i + 1)
            G.tensor_tensor(vol[i % 2][:, :], wvo[:, i % HEADS, :], voh[i % 2][:, :].bitcast(f32), ALU.subtract).then_inc(S("a_vol"), 1)

        def norms(i):
            pool.wait_ge(S("a_rks"), i + 1)
            if i:
                pool.wait_ge(S("a_ktok"), i)
            G.tensor_scalar(rk[:, :], rks[:, :], 1.0 / P, EPS, ALU.mult, ALU.add).then_inc(S("a_rk_var"), 1)
            pool.wait_ge(S("a_rk_var"), i + 1)
            G.tensor_tensor(rk[:, :], rk[:, :], mhalf[:, :], ALU.pow).then_inc(S("a_rk"), 1)

        def norm_q(i):
            pool.wait_ge(S("a_rqs"), i + 1)
            if i > 1:
                pool.wait_ge(S("a_exp"), i - 1)
            G.tensor_scalar(rq[i % 2][:, :], rqs[:, :], 1.0 / P, EPS, ALU.mult, ALU.add).then_inc(S("a_rq_var"), 1)
            pool.wait_ge(S("a_rq_var"), i + 1)
            G.tensor_tensor(rq[i % 2][:, :], rq[i % 2][:, :], mhalf[:, :], ALU.pow).then_inc(S("a_rq"), 1)

        def gu_lo(g):
            l, h, q, j = FT[g]
            pool.wait_ge(S("f_wgh"), g + 1)
            G.tensor_tensor(wgl[g % 2][:, :], raw_w(l, j)[:, 0:GU], wgh[g % 2][:, :].bitcast(f32), ALU.subtract).then_inc(S("f_wg"), 1)

        def d_lo(g):
            l, h, q, j = FT[g]
            pool.wait_ge(S("f_wdh"), g + 1)
            G.tensor_tensor(wdl[g % 3][:, :], raw_w(l, j)[:, GU:WJ], wdh[g % 3][:, :].bitcast(f32), ALU.subtract).then_inc(S("f_wd"), 1)

        def router_lo(l):
            pool.wait_ge(S("r_wh"), 1 if l == 1 else 2)
            G.tensor_tensor(wrl[:, :, :], fr[l][:, :, :], wrh[:, :, :].bitcast(f32), ALU.subtract).then_inc(S("r_w"), 1)

        def side(place_):
            for w in beside.get(place_, ()):
                if w[0] == "stats":
                    rstd_of()
                elif w[0] == "router_w":
                    router_lo(3)

        pool.wait_ge(S("mhalf_set"), 1)
        rstd_of()
        rstd_of()
        for k, s in enumerate(ORDER):
            if s == "F0":
                rstd_of()
                context_lo()
                parts(0)
                parts(1)
                rstd_of()
                continue
            if s == "A1":
                begin(pool, k)
                rstd_of()
                norms(0)
                norm_q(0)
                for i in range(HEADS2 + 1):
                    if i + 1 < HEADS2:
                        norms(i + 1)
                    if i + 2 < HEADS2:
                        parts(i + 2)
                    if i:
                        value_parts(i - 1)
                    if i + 1 < HEADS2:
                        norm_q(i + 1)
                    if i < HEADS2:
                        pool.wait_ge(S("a_ri"), i + 1)
                        G.tensor_tensor(Pm[i % 2][:, :, :], Pm[i % 2][:, :, :], bc(ri[:, :].unsqueeze(2), [P, TH, DM]), ALU.mult).then_inc(S("a_pn"), 1)
                    if i == HEADS + 2:
                        rstd_of()
                pool.wait_ge(S("a_pn"), HEADS2)
                G.tensor_copy(scratch[:, 16:17], mhalf[:, 0:1]).then_inc(S("pool_step"), 1)
                continue
            if s == "F":
                begin(pool, k)
                router_lo(1)
                gu_lo(0)
                gu_lo(1)
                d_lo(0)
                for g in range(FN):
                    side(2 * g)
                    if g + 2 < FN:
                        gu_lo(g + 2)
                    if g + 1 < FN:
                        d_lo(g + 1)
                    side(2 * g + 1)
                continue
            if s == "M":
                begin(pool, k)
                for g in range(2 * NS):
                    pool.wait_ge(S("m_Bcopy"), g + 1)
                    pool.wait_ge(S("m_du"), g // NS + 1)
                    if g >= 2:
                        pool.wait_ge(S("m_h"), g - 1)
                    G.tensor_tensor(dBu[g % 2][:, :, :], du[g // NS][:, :, :], bc(Bs[g % 3][:, :].unsqueeze(1), [P, 2, HALF]),
                                    ALU.mult).then_inc(S("m_dBu"), 1)
                    if g == NS + 7:
                        rstd_of()
                pool.wait_ge(S("m_dBu"), 2 * NS)
                G.tensor_copy(scratch[:, 16:17], mhalf[:, 0:1]).then_inc(S("pool_step"), 1)

    stack.close()


def kernel(**inputs):
    import numpy as np
    import ml_dtypes
    import concourse.bacc as bacc
    from concourse import mybir
    from concourse.bass_utils import run_bass_kernel_spmd

    f = {k: np.asarray(v) for k, v in inputs.items()}
    P = 128

    def rows(w):
        return w.reshape(-1, P, w.shape[1]).transpose(1, 0, 2)

    def pad_rows(w):
        n = -(-w.shape[0] // P) * P
        return np.concatenate([w, np.zeros((n - w.shape[0], w.shape[1]), w.dtype)])

    x = f["x"].reshape(1024, 256)
    ctx = f["ctx_1024"].reshape(1024, 128)
    small = np.zeros((P, 64), np.float32)
    small[:, 0:4] = f["g_xattn"][None, :]
    small[:, 4:8] = f["g_ffn"][None, :]
    small[:, 8:16] = rows(f["L0_xattn_conv_w"]).reshape(P, 8)
    small[:, 16:18] = f["L0_xattn_conv_b"].reshape(2, P).T
    small[:, 18:20] = f["L0_xattn_dt_proj_b"].reshape(2, P).T
    small[:, 20:52] = rows(f["L0_xattn_A_log"]).reshape(P, 32)
    small[:, 52:54] = f["L0_xattn_D"].reshape(2, P).T
    for c, name in enumerate(["L1_xattn_gq", "L1_xattn_gk", "L2_xattn_bq", "L2_xattn_bk", "L3_xattn_bq", "L3_xattn_bk"]):
        small[:, 54 + c] = f[name]

    def selector(owner, width, parts, rows_=96):
        s = np.zeros((rows_, width), np.float32)
        for p in parts:
            s[p + owner, np.arange(width)] = 1.0
        return s.astype(ml_dtypes.bfloat16)

    def experts(e, fdim, shared_width):
        n = e * fdim + shared_width
        owner = np.minimum(np.arange(n) // fdim, e)
        full = -(-n // P) * P
        s = np.zeros((96, full), ml_dtypes.bfloat16)
        s[:, :n] = selector(owner, n, (0, 32, 64))
        return s.reshape(96, -1, P)

    bc_owner = np.repeat(np.arange(32), P)
    had = np.array([[1.0]], np.float32)
    while had.shape[0] < P:
        had = np.block([[had, had], [had, -had]])

    xp = f["L0_xattn_x_proj_w"]
    bcw = np.concatenate([xp[8:40]] * 3).T

    def tiles(gate, up, down):
        n = -(-gate.shape[0] // P)
        g, u_, d = (pad_rows(w) for w in (gate, up, down))
        gu = [w.reshape(n, P, 2, P).transpose(3, 0, 2, 1).reshape(P, n, 256) for w in (g, u_)]
        return np.concatenate(gu + [d.reshape(n, P, 256).transpose(1, 0, 2)], 2)

    def experts_and_shared(gu, shared_gu, down, shared_down):
        w, ws = gu.shape[1] // 2, shared_gu.shape[0] // 2
        gate, up = (np.concatenate([gu[:, p * w:(p + 1) * w].reshape(-1, 256), shared_gu[p * ws:(p + 1) * ws]]) for p in (0, 1))
        return tiles(gate, up, np.concatenate([down.transpose(0, 2, 1).reshape(-1, 256), shared_down.T]))

    def router(w):
        return rows(np.concatenate([w, np.zeros((32 - w.shape[0], 256), w.dtype)]).T)

    wvT = f["L1_xattn_Wv"].reshape(128, 16, 128).transpose(2, 1, 0)
    wo = rows(f["L1_xattn_Wo"])
    f1w = experts_and_shared(f["L1_ffn_expert_gate_up"], f["L1_ffn_shared_gate_up"], f["L1_ffn_expert_down"], f["L1_ffn_shared_down"])

    arrays = {
        "x": rows(x), "ctk": rows(ctx), "ctxT": ctx.T, "small": small,
        "ident": np.eye(P, dtype=np.float32), "identb": np.eye(P, dtype=np.float32).astype(ml_dtypes.bfloat16),
        "had": had * np.float32(1024.0 ** -0.5),
        "sel_bc": selector(bc_owner, 32 * P, (0, 32, 64)).reshape(96, 32, P),
        "sel1": experts(16, 176, 704), "sel3": experts(8, 176, 352),
        "w0raw": np.stack([rows(f["L0_ffn_w_gate"].T).reshape(P, -1), rows(f["L0_ffn_w_up"].T).reshape(P, -1),
                           rows(f["L0_ffn_w_down"].T).reshape(P, -1)], 1),
        "m_in": f["L0_xattn_in_proj_w"].T, "m_bc": rows(bcw), "m_dt": rows(xp[0:8].T), "m_dtw": f["L0_xattn_dt_proj_w"].T,
        "wq": rows(f["L1_xattn_Wq"]), "wk": f["L1_xattn_Wk"],
        "wvT0": wvT[:, :8], "wvT1": wvT[:, 8:], "wo0": wo[:, :8], "wo1": wo[:, 8:],
        "f1a": f1w[:, :22], "f1b": f1w[:, 22:],
        "f1r": router(np.concatenate([f["L1_ffn_gate_w"], f["L1_ffn_shared_gate_vec"]])),
        "am2q": f["L2_xattn_Wq"].T, "am2k": f["L2_xattn_Wk"].T, "am3q": f["L3_xattn_Wq"].T, "am3k": f["L3_xattn_Wk"].T,
        "f2w": tiles(f["L2_ffn_W1"], f["L2_ffn_W3"], f["L2_ffn_W2"].T),
        "f3w": experts_and_shared(f["L3_ffn_gate_up_weights"], f["L3_ffn_shared_gate_up"], f["L3_ffn_down_weights"], f["L3_ffn_shared_down"]),
        "f3r": router(f["L3_ffn_gate_weight"]),
    }
    nc = bacc.Bacc("TRN2", target_bir_lowering=False, num_devices=1)
    dram, given = {}, {}
    for name, a in arrays.items():
        a = np.ascontiguousarray(a)
        given["in_" + name] = a
        t = nc.dram_tensor("in_" + name, a.shape, mybir.dt.from_np(a.dtype), kind="ExternalInput").ap()
        dram[name] = t
    out = nc.dram_tensor("out_x", (P, 8, 256), mybir.dt.float32, kind="ExternalOutput").ap()
    flamingo_kernel(nc, dram, out)
    r = run_bass_kernel_spmd(nc, [given], core_ids=[0])
    return np.asarray(r.results[0]["out_x"]).transpose(1, 0, 2).reshape(4, 256, 256)
```
